# Optimizing a Trainium2 kernel written in Bass

```python
import numpy as np
import jax
import jax.numpy as jnp

def _softmax(x, axis=-1):
    return jax.nn.softmax(x, axis=axis)

def _gelu(x):
    return jax.nn.gelu(x, approximate=True)

def _silu(x):
    return jax.nn.silu(x)

def _sigmoid(x):
    return jax.nn.sigmoid(x)

def _layernorm(x, axis=-1, eps=1e-05):
    m = jnp.mean(x, axis=axis, keepdims=True)
    v = jnp.var(x, axis=axis, keepdims=True)
    return (x - m) / jnp.sqrt(v + eps)

def _scatter_add(tgt, idx, src, axis=0):
    return tgt.at[idx].add(src)

def _segment_sum(src, seg, n):
    return jax.ops.segment_sum(src, seg, n)
kernel_name = 'mk_flamingo_gated_d4_seqx_r8_fcc0cc'

def setup_inputs(seed: int=0):
    np.random.seed(seed)
    _w = jnp.asarray

    def _rec_inputs():
        import jax
        import jax.numpy as jnp
        _rk = jax.random.key(seed)
        x = -0.000125 + 0.9999 * jax.random.normal(jax.random.fold_in(_rk, 1), (4, 256, 256), jnp.float32)
        _lenS = 256 - jax.random.randint(jax.random.fold_in(_rk, 7), (4,), 0, max(1, 256 // 4) + 1, jnp.int32)
        _lenS2 = 256 - jax.random.randint(jax.random.fold_in(_rk, 8), (4,), 0, max(1, 256 // 4) + 1, jnp.int32)
        itok_BxS_13_99985 = jax.random.randint(jax.random.fold_in(_rk, 11), (4, 256), 13, 99986, jnp.int32)
        _ctx_2048P = jax.random.normal(jax.random.fold_in(_rk, 12), (4, 16, 256), jnp.float32)
        _ctx_2048c = jax.random.dirichlet(jax.random.fold_in(_rk, 512), 0.3 * jnp.ones((16,), jnp.float32), (4, 256))
        _ctx_2048t = jnp.einsum('bsk,bkd->bsd', _ctx_2048c, _ctx_2048P)
        _ctx_2048t = _ctx_2048t * jax.lax.rsqrt(jnp.mean(jnp.square(_ctx_2048t)) + 1e-12) * 0.953939
        ctx_2048 = 6.82029e-06 + 0.0200006 * (_ctx_2048t + 0.3 * jax.random.normal(jax.random.fold_in(_rk, 612), (4, 256, 256), jnp.float32))
        _validS = jnp.arange(256)[None, :] < _lenS[:, None]
        _validS2 = jnp.arange(256)[None, :] < _lenS2[:, None]
        _causal = jnp.tril(jnp.ones((256, 256), dtype=bool))
        mask_BxSx4224_bf0 = jnp.logical_not(jnp.ones((4, 256, 528), dtype=bool))
        _g = jax.random.normal(jax.random.fold_in(_rk, 9001), (2, 4), jnp.float32)
        _g = jnp.sign(_g) * jnp.maximum(jnp.abs(_g), 1.0) + (_g == 0) * 1.0
        g_xattn = _g[0]
        g_ffn = _g[1]
        return (x, itok_BxS_13_99985, ctx_2048, mask_BxSx4224_bf0, g_xattn, g_ffn)
    x, itok_BxS_13_99985, ctx_2048, mask_BxSx4224_bf0, g_xattn, g_ffn = _rec_inputs()

    def _L0_xattn_setup():
        import jax, jax.numpy as jnp
        import numpy as np
        B, S, D = (4, 512, 256)
        E = 4
        F = 1024 // E
        VOCAB = 12500
        key = jax.random.key(seed)
        k1, k2, k3, k4, k5 = jax.random.split(key, 5)
        hidden_states = jax.random.normal(k1, (B, S, D), dtype=jnp.float32)
        token_ids = jax.random.randint(k2, (B, S), 0, VOCAB, dtype=jnp.int64)
        Wg = jax.random.normal(k3, (E, F, D), dtype=jnp.float32) * 0.02
        Wu = jax.random.normal(k4, (E, F, D), dtype=jnp.float32) * 0.02
        Wd = jax.random.normal(k5, (E, D, F), dtype=jnp.float32) * 0.02
        return {'hidden_states': hidden_states, 'token_ids': token_ids, 'Wg': Wg, 'Wu': Wu, 'Wd': Wd}
    _L0_xattn_all = _L0_xattn_setup()
    _L0_xattn_in = {k: v for k, v in _L0_xattn_all.items() if k in ()}
    del _L0_xattn_all

    def _L0_ffn_setup():
        import jax, jax.numpy as jnp
        import numpy as np
        B, T, D = (1, 256, 256)
        E, K, F = (64, 4, 64)
        S, SF = (2, 64 * 4)
        CAP = 32

        def _moe_forward(x, router_w, router_bias, gate_w, up_w, down_w, sh_gate_w, sh_up_w, sh_down_w):
            b, t, d = x.shape
            flat = x.reshape(b * t, d)
            N = flat.shape[0]
            logits = flat @ router_w.T
            scores = jax.nn.softmax(logits, axis=-1)
            _, topk_idx = jax.lax.top_k(logits + router_bias, K)
            topk_w = jnp.take_along_axis(scores, topk_idx, axis=-1)
            topk_w = topk_w / topk_w.sum(axis=-1, keepdims=True)
            P = N * K
            e_flat = topk_idx.reshape(-1)
            t_flat = jnp.repeat(jnp.arange(N), K)
            w_flat = topk_w.reshape(-1)
            order = jnp.argsort(e_flat)
            e_s, t_s, w_s = (e_flat[order], t_flat[order], w_flat[order])
            counts = jnp.bincount(e_s, length=E)
            starts = jnp.concatenate([jnp.zeros((1,), counts.dtype), jnp.cumsum(counts)[:-1]])
            pos = jnp.arange(P) - starts[e_s]
            slot = jnp.where(pos < CAP, pos, CAP)
            tok_table = jnp.zeros((E, CAP + 1), jnp.int32).at[e_s, slot].set(t_s)[:, :CAP]
            w_table = jnp.zeros((E, CAP + 1), w_s.dtype).at[e_s, slot].set(w_s)[:, :CAP]
            xg = flat[tok_table]
            g = jnp.einsum('ecd,efd->ecf', xg, gate_w)
            u = jnp.einsum('ecd,efd->ecf', xg, up_w)
            y = jnp.einsum('ecf,edf->ecd', jax.nn.silu(g) * u, down_w)
            out = jnp.zeros_like(flat).at[tok_table.reshape(-1)].add((y * w_table[..., None]).reshape(-1, d))
            sg = jnp.einsum('nd,sfd->nsf', flat, sh_gate_w)
            su = jnp.einsum('nd,sfd->nsf', flat, sh_up_w)
            out = out + jnp.einsum('nsf,sdf->nd', jax.nn.silu(sg) * su, sh_down_w)
            return out.reshape(b, t, d)
        key = jax.random.key(seed)
        ks = jax.random.split(key, 9)
        s = 0.02
        return {'x': jax.random.normal(ks[0], (B, T, D), jnp.float32), 'router_w': jax.random.normal(ks[1], (E, D), jnp.float32) * s, 'router_bias': jnp.zeros((E,), jnp.float32), 'gate_w': jax.random.normal(ks[2], (E, F, D), jnp.float32) * s, 'up_w': jax.random.normal(ks[3], (E, F, D), jnp.float32) * s, 'down_w': jax.random.normal(ks[4], (E, D, F), jnp.float32) * s, 'sh_gate_w': jax.random.normal(ks[5], (S, SF, D), jnp.float32) * s, 'sh_up_w': jax.random.normal(ks[6], (S, SF, D), jnp.float32) * s, 'sh_down_w': jax.random.normal(ks[7], (S, D, SF), jnp.float32) * s}
    _L0_ffn_all = _L0_ffn_setup()
    _L0_ffn_in = {k: v for k, v in _L0_ffn_all.items() if k in ('router_w', 'router_bias', 'gate_w', 'up_w', 'down_w', 'sh_gate_w', 'sh_up_w', 'sh_down_w')}
    del _L0_ffn_all

    def _L1_xattn_setup():
        import jax, jax.numpy as jnp
        import numpy as np
        B, S, E, NH = (2, 128, 256, 16)
        DH = E // NH
        EPS = 1e-06

        def _mlstm_forward(q, k, v, Wi, bi, Wf, bf, ln_scale):
            b, s, e = q.shape
            nh = Wi.shape[1]
            dh = e // nh
            x = jnp.concatenate([q, k, v], axis=-1)
            ig = (x @ Wi + bi).transpose(0, 2, 1)[..., None]
            fg = (x @ Wf + bf).transpose(0, 2, 1)[..., None]
            split = lambda t: t.reshape(b, s, nh, dh).transpose(0, 2, 1, 3)
            qh, kh, vh = (split(q), split(k), split(v))
            log_f = jax.nn.log_sigmoid(fg)
            log_f_cum = jnp.concatenate([jnp.zeros((b, nh, 1, 1), q.dtype), jnp.cumsum(log_f, axis=2)], axis=2)
            fg_mat = log_f_cum - jnp.transpose(log_f_cum, (0, 1, 3, 2))
            ltr = jnp.tril(jnp.ones((s, s), dtype=bool))
            log_fg = jnp.where(ltr, fg_mat[:, :, 1:, 1:], -jnp.inf)
            log_D = log_fg + jnp.transpose(ig, (0, 1, 3, 2))
            max_log_D = jnp.max(log_D, axis=-1, keepdims=True)
            D = jnp.exp(log_D - max_log_D)
            qk = jnp.einsum('bhsd,bhtd->bhst', qh, kh) / jnp.sqrt(jnp.asarray(dh, q.dtype))
            C = qk * D
            normalizer = jnp.maximum(jnp.abs(C.sum(-1, keepdims=True)), jnp.exp(-max_log_D))
            Cn = C / (normalizer + EPS)
            h = jnp.einsum('bhst,bhtd->bhsd', Cn, vh)
            mu = h.mean(-1, keepdims=True)
            var = ((h - mu) ** 2).mean(-1, keepdims=True)
            hn = (h - mu) * jax.lax.rsqrt(var + EPS)
            hn = hn * ln_scale.reshape(1, nh, 1, dh)
            return hn.transpose(0, 2, 1, 3).reshape(b, s, e)
        key = jax.random.key(seed)
        ks = jax.random.split(key, 6)
        q = jax.random.normal(ks[0], (B, S, E), dtype=jnp.float32)
        k = jax.random.normal(ks[1], (B, S, E), dtype=jnp.float32)
        v = jax.random.normal(ks[2], (B, S, E), dtype=jnp.float32)
        Wi = jax.random.normal(ks[3], (3 * E, NH), dtype=jnp.float32) * 0.02
        bi = jax.random.normal(ks[4], (NH,), dtype=jnp.float32) * 0.1
        Wf = jax.random.normal(ks[5], (3 * E, NH), dtype=jnp.float32) * 0.02
        bf = jnp.linspace(3.0, 6.0, NH, dtype=jnp.float32)
        ln_scale = jnp.ones((E,), dtype=jnp.float32)
        return {'q': q, 'k': k, 'v': v, 'Wi': Wi, 'bi': bi, 'Wf': Wf, 'bf': bf, 'ln_scale': ln_scale}
    _L1_xattn_all = _L1_xattn_setup()
    _L1_xattn_in = {k: v for k, v in _L1_xattn_all.items() if k in ('Wi', 'bi', 'Wf', 'bf', 'ln_scale')}
    del _L1_xattn_all

    def _L1_ffn_setup():
        import jax, jax.numpy as jnp
        import numpy as np
        B, S, D, R, E = (4, 256, 256, 64, 8)
        SCALING = 64.0 / 16.0
        key = jax.random.key(seed)
        k1, k2, k3, k4 = jax.random.split(key, 4)
        x = jax.random.normal(k1, (B, S, D), dtype=jnp.float32)
        A = jax.random.normal(k2, (E, R, D), dtype=jnp.float32) * 0.02
        Bw = jax.random.normal(k3, (E, D, R), dtype=jnp.float32) * 0.02
        Wg = jax.random.normal(k4, (E, D), dtype=jnp.float32) * 0.02
        return {'x': x, 'A': A, 'Bw': Bw, 'Wg': Wg}
    _L1_ffn_all = _L1_ffn_setup()
    _L1_ffn_in = {k: v for k, v in _L1_ffn_all.items() if k in ('A', 'Bw', 'Wg')}
    del _L1_ffn_all

    def _L2_xattn_setup():
        import jax, jax.numpy as jnp
        import numpy as np
        import math
        DIM = 256
        B, Q_LEN, KV_LEN = (8, 128, 512)
        key = jax.random.key(seed)
        ks = jax.random.split(key, 8)
        x = jax.random.normal(ks[0], (B, Q_LEN, DIM), dtype=jnp.float32)
        mask = jnp.zeros((B, Q_LEN, KV_LEN + Q_LEN), dtype=bool)
        k_cache = jax.random.normal(ks[1], (B, KV_LEN, DIM), dtype=jnp.float32)
        v_cache = jax.random.normal(ks[2], (B, KV_LEN, DIM), dtype=jnp.float32)
        scale = 1.0 / math.sqrt(DIM)
        wq = jax.random.normal(ks[3], (DIM, DIM), dtype=jnp.float32) * scale
        wk = jax.random.normal(ks[4], (DIM, DIM), dtype=jnp.float32) * scale
        wv = jax.random.normal(ks[5], (DIM, DIM), dtype=jnp.float32) * scale
        wo = jax.random.normal(ks[6], (DIM, DIM), dtype=jnp.float32) * scale
        return {'x': x, 'mask': mask, 'k_cache': k_cache, 'v_cache': v_cache, 'wq': wq, 'wk': wk, 'wv': wv, 'wo': wo}
    _L2_xattn_all = _L2_xattn_setup()
    _L2_xattn_in = {k: v for k, v in _L2_xattn_all.items() if k in ('wq', 'wk', 'wv', 'wo')}
    del _L2_xattn_all

    def _L2_ffn_setup():
        import jax, jax.numpy as jnp
        import numpy as np
        EPS = 1e-05

        def _quant_weight(w):
            scale = jnp.mean(jnp.abs(w)) + EPS
            wq = jnp.clip(jnp.round(w / scale), -1.0, 1.0)
            return (wq, scale)

        def _quant_act(x):
            s = jnp.max(jnp.abs(x), axis=-1, keepdims=True) / 127.0 + EPS
            xq = jnp.clip(jnp.round(x / s), -128.0, 127.0)
            return (xq, s)

        def _qlinear(x, w):
            wq, ws = _quant_weight(w)
            xq, xs = _quant_act(x)
            y = jnp.einsum('bsi,oi->bso', xq, wq)
            return y * xs * ws
        key = jax.random.key(seed)
        k1, k2, k3, k4 = jax.random.split(key, 4)
        H, I = (256, 1024)
        x = jax.random.normal(k1, (4, 512, H), dtype=jnp.float32)
        w_gate = jax.random.normal(k2, (I, H), dtype=jnp.float32) * (1.0 / np.sqrt(H))
        w_up = jax.random.normal(k3, (I, H), dtype=jnp.float32) * (1.0 / np.sqrt(H))
        w_down = jax.random.normal(k4, (H, I), dtype=jnp.float32) * (1.0 / np.sqrt(I))
        return {'x': x, 'w_gate': w_gate, 'w_up': w_up, 'w_down': w_down}
    _L2_ffn_all = _L2_ffn_setup()
    _L2_ffn_in = {k: v for k, v in _L2_ffn_all.items() if k in ('w_gate', 'w_up', 'w_down')}
    del _L2_ffn_all

    def _L3_xattn_setup():
        import jax, jax.numpy as jnp
        import numpy as np
        key = jax.random.key(seed)
        k = jax.random.split(key, 6)
        B, S, D, NKV = (4, 512, 256, 64)
        inv = D ** (-0.5)
        return {'x': jax.random.normal(k[0], (B, S, D), jnp.float32), 'W_qkv': jax.random.normal(k[1], (3 * D, D), jnp.float32) * inv, 'W_o': jax.random.normal(k[2], (D, D), jnp.float32) * inv, 'beta_q': jnp.array(1.0, jnp.float32), 'beta_k': jnp.array(1.0, jnp.float32), 'gate': jnp.array(0.0, jnp.float32), 'log_tau': jnp.array(0.0, jnp.float32), 'K_mem': jax.random.normal(k[3], (B, NKV, D), jnp.float32), 'V_mem': jax.random.normal(k[4], (B, NKV, D), jnp.float32), 'clip_k': 54}
    _L3_xattn_all = _L3_xattn_setup()
    _L3_xattn_in = {k: v for k, v in _L3_xattn_all.items() if k in ('W_qkv', 'W_o', 'beta_q', 'beta_k', 'gate', 'log_tau')}
    del _L3_xattn_all

    def _L3_ffn_setup():
        import jax, jax.numpy as jnp
        import numpy as np
        EPS = 1e-05
        Q_MAX = 127.0

        def _quant_weight(w):
            gamma = jnp.mean(jnp.abs(w)) + EPS
            wq = jnp.clip(jnp.round(w / gamma), -1.0, 1.0) * gamma
            return w + jax.lax.stop_gradient(wq - w)

        def _quant_act(x):
            scale = Q_MAX / jnp.clip(jnp.max(jnp.abs(x), axis=-1, keepdims=True), EPS)
            xq = jnp.clip(jnp.round(x * scale), -Q_MAX - 1.0, Q_MAX) / scale
            return x + jax.lax.stop_gradient(xq - x)

        def bitlinear(x, w):
            return jnp.einsum('bsi,oi->bso', _quant_act(x), _quant_weight(w))
        key = jax.random.key(seed)
        k1, k2, k3 = jax.random.split(key, 3)
        B, S, d_model, d_ff = (4, 256, 256, 1024)
        x = jax.random.normal(k1, (B, S, d_model), dtype=jnp.float32)
        w1 = jax.random.normal(k2, (d_ff, d_model), dtype=jnp.float32) * 0.02
        w2 = jax.random.normal(k3, (d_model, d_ff), dtype=jnp.float32) * 0.02
        return {'x': x, 'w1': w1, 'w2': w2}
    _L3_ffn_all = _L3_ffn_setup()
    _L3_ffn_in = {k: v for k, v in _L3_ffn_all.items() if k in ('w1', 'w2')}
    del _L3_ffn_all
    return {'x': x, 'itok_BxS_13_99985': itok_BxS_13_99985, 'ctx_2048': ctx_2048, 'mask_BxSx4224_bf0': mask_BxSx4224_bf0, 'g_xattn': g_xattn, 'g_ffn': g_ffn, 'L0_ffn_router_w': _L0_ffn_in['router_w'], 'L0_ffn_router_bias': _L0_ffn_in['router_bias'], 'L0_ffn_gate_w': _L0_ffn_in['gate_w'], 'L0_ffn_up_w': _L0_ffn_in['up_w'], 'L0_ffn_down_w': _L0_ffn_in['down_w'], 'L0_ffn_sh_gate_w': _L0_ffn_in['sh_gate_w'], 'L0_ffn_sh_up_w': _L0_ffn_in['sh_up_w'], 'L0_ffn_sh_down_w': _L0_ffn_in['sh_down_w'], 'L1_xattn_Wi': _L1_xattn_in['Wi'], 'L1_xattn_bi': _L1_xattn_in['bi'], 'L1_xattn_Wf': _L1_xattn_in['Wf'], 'L1_xattn_bf': _L1_xattn_in['bf'], 'L1_xattn_ln_scale': _L1_xattn_in['ln_scale'], 'L1_ffn_A': _L1_ffn_in['A'], 'L1_ffn_Bw': _L1_ffn_in['Bw'], 'L1_ffn_Wg': _L1_ffn_in['Wg'], 'L2_xattn_wq': _L2_xattn_in['wq'], 'L2_xattn_wk': _L2_xattn_in['wk'], 'L2_xattn_wv': _L2_xattn_in['wv'], 'L2_xattn_wo': _L2_xattn_in['wo'], 'L2_ffn_w_gate': _L2_ffn_in['w_gate'], 'L2_ffn_w_up': _L2_ffn_in['w_up'], 'L2_ffn_w_down': _L2_ffn_in['w_down'], 'L3_xattn_W_qkv': _L3_xattn_in['W_qkv'], 'L3_xattn_W_o': _L3_xattn_in['W_o'], 'L3_xattn_beta_q': _L3_xattn_in['beta_q'], 'L3_xattn_beta_k': _L3_xattn_in['beta_k'], 'L3_xattn_gate': _L3_xattn_in['gate'], 'L3_xattn_log_tau': _L3_xattn_in['log_tau'], 'L3_ffn_w1': _L3_ffn_in['w1'], 'L3_ffn_w2': _L3_ffn_in['w2']}

def reference(x, itok_BxS_13_99985, ctx_2048, mask_BxSx4224_bf0, g_xattn, g_ffn, L0_ffn_router_w, L0_ffn_router_bias, L0_ffn_gate_w, L0_ffn_up_w, L0_ffn_down_w, L0_ffn_sh_gate_w, L0_ffn_sh_up_w, L0_ffn_sh_down_w, L1_xattn_Wi, L1_xattn_bi, L1_xattn_Wf, L1_xattn_bf, L1_xattn_ln_scale, L1_ffn_A, L1_ffn_Bw, L1_ffn_Wg, L2_xattn_wq, L2_xattn_wk, L2_xattn_wv, L2_xattn_wo, L2_ffn_w_gate, L2_ffn_w_up, L2_ffn_w_down, L3_xattn_W_qkv, L3_xattn_W_o, L3_xattn_beta_q, L3_xattn_beta_k, L3_xattn_gate, L3_xattn_log_tau, L3_ffn_w1, L3_ffn_w2):
    import jax
    import jax.numpy as jnp

    def _L0_xattn_ref(hidden_states, token_ids, Wg, Wu, Wd):
        import jax, jax.numpy as jnp
        import numpy as np
        B, S, D = (4, 512, 256)
        E = 4
        F = 1024 // E
        VOCAB = 12500
        tokens_per_expert = VOCAB // E
        tid = jnp.clip(token_ids, 0, VOCAB - 1)
        expert_ids = jnp.minimum(tid // tokens_per_expert, E - 1)
        out = jnp.zeros_like(hidden_states)
        for e in range(E):
            g = jax.nn.silu(jnp.einsum('bsd,fd->bsf', hidden_states, Wg[e]))
            u = jnp.einsum('bsd,fd->bsf', hidden_states, Wu[e])
            y = jnp.einsum('bsf,df->bsd', g * u, Wd[e])
            out = jnp.where((expert_ids == e)[..., None], y, out)
        return out

    def _L0_ffn_ref(x, router_w, router_bias, gate_w, up_w, down_w, sh_gate_w, sh_up_w, sh_down_w):
        import jax, jax.numpy as jnp
        import numpy as np
        B, T, D = (1, 256, 256)
        E, K, F = (64, 4, 64)
        S, SF = (2, 64 * 4)
        CAP = 32

        def _moe_forward(x, router_w, router_bias, gate_w, up_w, down_w, sh_gate_w, sh_up_w, sh_down_w):
            b, t, d = x.shape
            flat = x.reshape(b * t, d)
            N = flat.shape[0]
            logits = flat @ router_w.T
            scores = jax.nn.softmax(logits, axis=-1)
            _, topk_idx = jax.lax.top_k(logits + router_bias, K)
            topk_w = jnp.take_along_axis(scores, topk_idx, axis=-1)
            topk_w = topk_w / topk_w.sum(axis=-1, keepdims=True)
            P = N * K
            e_flat = topk_idx.reshape(-1)
            t_flat = jnp.repeat(jnp.arange(N), K)
            w_flat = topk_w.reshape(-1)
            order = jnp.argsort(e_flat)
            e_s, t_s, w_s = (e_flat[order], t_flat[order], w_flat[order])
            counts = jnp.bincount(e_s, length=E)
            starts = jnp.concatenate([jnp.zeros((1,), counts.dtype), jnp.cumsum(counts)[:-1]])
            pos = jnp.arange(P) - starts[e_s]
            slot = jnp.where(pos < CAP, pos, CAP)
            tok_table = jnp.zeros((E, CAP + 1), jnp.int32).at[e_s, slot].set(t_s)[:, :CAP]
            w_table = jnp.zeros((E, CAP + 1), w_s.dtype).at[e_s, slot].set(w_s)[:, :CAP]
            xg = flat[tok_table]
            g = jnp.einsum('ecd,efd->ecf', xg, gate_w)
            u = jnp.einsum('ecd,efd->ecf', xg, up_w)
            y = jnp.einsum('ecf,edf->ecd', jax.nn.silu(g) * u, down_w)
            out = jnp.zeros_like(flat).at[tok_table.reshape(-1)].add((y * w_table[..., None]).reshape(-1, d))
            sg = jnp.einsum('nd,sfd->nsf', flat, sh_gate_w)
            su = jnp.einsum('nd,sfd->nsf', flat, sh_up_w)
            out = out + jnp.einsum('nsf,sdf->nd', jax.nn.silu(sg) * su, sh_down_w)
            return out.reshape(b, t, d)
        return _moe_forward(x, router_w, router_bias, gate_w, up_w, down_w, sh_gate_w, sh_up_w, sh_down_w)

    def _L1_xattn_ref(q, k, v, Wi, bi, Wf, bf, ln_scale):
        import jax, jax.numpy as jnp
        import numpy as np
        B, S, E, NH = (2, 128, 256, 16)
        DH = E // NH
        EPS = 1e-06

        def _mlstm_forward(q, k, v, Wi, bi, Wf, bf, ln_scale):
            b, s, e = q.shape
            nh = Wi.shape[1]
            dh = e // nh
            x = jnp.concatenate([q, k, v], axis=-1)
            ig = (x @ Wi + bi).transpose(0, 2, 1)[..., None]
            fg = (x @ Wf + bf).transpose(0, 2, 1)[..., None]
            split = lambda t: t.reshape(b, s, nh, dh).transpose(0, 2, 1, 3)
            qh, kh, vh = (split(q), split(k), split(v))
            log_f = jax.nn.log_sigmoid(fg)
            log_f_cum = jnp.concatenate([jnp.zeros((b, nh, 1, 1), q.dtype), jnp.cumsum(log_f, axis=2)], axis=2)
            fg_mat = log_f_cum - jnp.transpose(log_f_cum, (0, 1, 3, 2))
            ltr = jnp.tril(jnp.ones((s, s), dtype=bool))
            log_fg = jnp.where(ltr, fg_mat[:, :, 1:, 1:], -jnp.inf)
            log_D = log_fg + jnp.transpose(ig, (0, 1, 3, 2))
            max_log_D = jnp.max(log_D, axis=-1, keepdims=True)
            D = jnp.exp(log_D - max_log_D)
            qk = jnp.einsum('bhsd,bhtd->bhst', qh, kh) / jnp.sqrt(jnp.asarray(dh, q.dtype))
            C = qk * D
            normalizer = jnp.maximum(jnp.abs(C.sum(-1, keepdims=True)), jnp.exp(-max_log_D))
            Cn = C / (normalizer + EPS)
            h = jnp.einsum('bhst,bhtd->bhsd', Cn, vh)
            mu = h.mean(-1, keepdims=True)
            var = ((h - mu) ** 2).mean(-1, keepdims=True)
            hn = (h - mu) * jax.lax.rsqrt(var + EPS)
            hn = hn * ln_scale.reshape(1, nh, 1, dh)
            return hn.transpose(0, 2, 1, 3).reshape(b, s, e)
        return _mlstm_forward(q, k, v, Wi, bi, Wf, bf, ln_scale)

    def _L1_ffn_ref(x, A, Bw, Wg):
        import jax, jax.numpy as jnp
        import numpy as np
        B, S, D, R, E = (4, 256, 256, 64, 8)
        SCALING = 64.0 / 16.0
        bsz, seq_len, dim = x.shape
        xf = x.reshape(-1, dim)
        logits = jnp.einsum('nd,ed->ne', xf, Wg)
        prob = jax.nn.softmax(logits, axis=-1)
        gate = jnp.argmax(prob, axis=-1)
        prob_sel = jnp.take_along_axis(prob, gate[:, None], axis=1)
        mask = jax.nn.one_hot(gate, E, dtype=xf.dtype)
        h = jnp.einsum('nd,erd->ner', xf, A)
        h = h * mask[:, :, None]
        y = jnp.einsum('ner,eor->no', h, Bw)
        y = y * SCALING * prob_sel
        return y.reshape(bsz, seq_len, -1)

    def _L2_xattn_ref(x, mask, k_cache, v_cache, wq, wk, wv, wo):
        import jax, jax.numpy as jnp
        import numpy as np
        import math
        DIM = 256
        B, Q_LEN, KV_LEN = (8, 128, 512)
        q = jnp.einsum('bsd,ed->bse', x, wq)
        k_new = jnp.einsum('bsd,ed->bse', x, wk)
        v_new = jnp.einsum('bsd,ed->bse', x, wv)
        k = jnp.concatenate([k_cache, k_new], axis=1)
        v = jnp.concatenate([v_cache, v_new], axis=1)
        scale = 1.0 / math.sqrt(q.shape[-1])
        scores = jnp.einsum('bqd,bkd->bqk', q, k) * scale
        attn = jax.nn.softmax(scores, axis=-1)
        out = jnp.einsum('bqk,bkd->bqd', attn, v)
        return jnp.einsum('bqd,ed->bqe', out, wo)

    def _L2_ffn_ref(x, w_gate, w_up, w_down):
        import jax, jax.numpy as jnp
        import numpy as np
        EPS = 1e-05

        def _quant_weight(w):
            scale = jnp.mean(jnp.abs(w)) + EPS
            wq = jnp.clip(jnp.round(w / scale), -1.0, 1.0)
            return (wq, scale)

        def _quant_act(x):
            s = jnp.max(jnp.abs(x), axis=-1, keepdims=True) / 127.0 + EPS
            xq = jnp.clip(jnp.round(x / s), -128.0, 127.0)
            return (xq, s)

        def _qlinear(x, w):
            wq, ws = _quant_weight(w)
            xq, xs = _quant_act(x)
            y = jnp.einsum('bsi,oi->bso', xq, wq)
            return y * xs * ws
        gate = jax.nn.silu(_qlinear(x, w_gate))
        up = _qlinear(x, w_up)
        return _qlinear(gate * up, w_down)

    def _L3_xattn_ref(x, W_qkv, W_o, beta_q, beta_k, gate, log_tau, K_mem, V_mem, clip_k):
        import jax, jax.numpy as jnp
        import numpy as np
        D = x.shape[-1]
        scale = D ** (-0.5)
        qkv = x @ W_qkv.T
        Q = qkv[..., :D]
        alpha = jax.nn.sigmoid(gate)
        tau = jnp.exp(log_tau)
        coef = (alpha * beta_q + (1.0 - alpha) * beta_k) * scale * tau
        scores = coef * jnp.einsum('bsd,bnd->bsn', Q, K_mem)
        scores = scores - jnp.max(scores, axis=-1, keepdims=True)
        thr = jax.lax.top_k(scores, clip_k)[0][..., -1:]
        scores = jnp.where(scores < thr, -jnp.inf, scores)
        att = jax.nn.softmax(scores, axis=-1)
        out = jnp.einsum('bsn,bnd->bsd', att, V_mem)
        return out @ W_o.T

    def _L3_ffn_ref(x, w1, w2):
        import jax, jax.numpy as jnp
        import numpy as np
        EPS = 1e-05
        Q_MAX = 127.0

        def _quant_weight(w):
            gamma = jnp.mean(jnp.abs(w)) + EPS
            wq = jnp.clip(jnp.round(w / gamma), -1.0, 1.0) * gamma
            return w + jax.lax.stop_gradient(wq - w)

        def _quant_act(x):
            scale = Q_MAX / jnp.clip(jnp.max(jnp.abs(x), axis=-1, keepdims=True), EPS)
            xq = jnp.clip(jnp.round(x * scale), -Q_MAX - 1.0, Q_MAX) / scale
            return x + jax.lax.stop_gradient(xq - x)

        def bitlinear(x, w):
            return jnp.einsum('bsi,oi->bso', _quant_act(x), _quant_weight(w))
        h = bitlinear(x, w1)
        h = jnp.square(jax.nn.relu(h))
        return bitlinear(h, w2)
    x = x + jnp.tanh(g_xattn[0]) * _L0_xattn_ref(_layernorm(x, axis=-1), itok_BxS_13_99985, ctx_2048, ctx_2048, ctx_2048)
    x = x + jnp.tanh(g_ffn[0]) * _L0_ffn_ref(_layernorm(x, axis=-1), L0_ffn_router_w, L0_ffn_router_bias, L0_ffn_gate_w, L0_ffn_up_w, L0_ffn_down_w, L0_ffn_sh_gate_w, L0_ffn_sh_up_w, L0_ffn_sh_down_w)
    x = x + jnp.tanh(g_xattn[1]) * _L1_xattn_ref(_layernorm(x, axis=-1), ctx_2048, ctx_2048, L1_xattn_Wi, L1_xattn_bi, L1_xattn_Wf, L1_xattn_bf, L1_xattn_ln_scale)
    x = x + jnp.tanh(g_ffn[1]) * _L1_ffn_ref(_layernorm(x, axis=-1), L1_ffn_A, L1_ffn_Bw, L1_ffn_Wg)
    x = x + jnp.tanh(g_xattn[2]) * _L2_xattn_ref(_layernorm(x, axis=-1), mask_BxSx4224_bf0, ctx_2048, ctx_2048, L2_xattn_wq, L2_xattn_wk, L2_xattn_wv, L2_xattn_wo)
    x = x + jnp.tanh(g_ffn[2]) * _L2_ffn_ref(_layernorm(x, axis=-1), L2_ffn_w_gate, L2_ffn_w_up, L2_ffn_w_down)
    x = x + jnp.tanh(g_xattn[3]) * _L3_xattn_ref(_layernorm(x, axis=-1), L3_xattn_W_qkv, L3_xattn_W_o, L3_xattn_beta_q, L3_xattn_beta_k, L3_xattn_gate, L3_xattn_log_tau, ctx_2048, ctx_2048, 54)
    x = x + jnp.tanh(g_ffn[3]) * _L3_ffn_ref(_layernorm(x, axis=-1), L3_ffn_w1, L3_ffn_w2)
    return x

_drawn_inputs = setup_inputs


def setup_inputs(seed=0):
    import zlib

    import numpy as np

    out = dict(_drawn_inputs(seed))
    spreads = {'L0_ffn_router_bias': (0.0, 0.8), 'L1_xattn_ln_scale': (1.0, 0.2)}
    factors = {'g_ffn': 8.0,
     'L0_ffn_router_w': 8.0,
     'L0_ffn_gate_w': 8.0,
     'L0_ffn_up_w': 8.0,
     'L0_ffn_down_w': 8.0,
     'L1_xattn_bi': 4.66,
     'L1_xattn_Wf': 5.672,
     'L3_xattn_W_qkv': 200.0,
     'L3_xattn_W_o': 61.047,
     'L0_ffn_sh_gate_w': 6.955,
     'L0_ffn_sh_up_w': 6.876,
     'L0_ffn_sh_down_w': 6.841,
     'L1_ffn_A': 4.094,
     'L1_ffn_Bw': 4.062,
     'L1_ffn_Wg': 4.454,
     'L2_xattn_wq': 3.234,
     'L2_xattn_wk': 3.269,
     'L2_xattn_wv': 2.775,
     'L2_xattn_wo': 2.769,
     'L3_ffn_w1': 5.937,
     'L3_ffn_w2': 4.813,
     'L2_ffn_w_gate': 3.834,
     'L2_ffn_w_up': 3.696,
     'L2_ffn_w_down': 3.708}
    for name, (base, spread) in spreads.items():
        noise = np.random.default_rng([zlib.crc32(name.encode()), seed]).standard_normal(out[name].shape)
        drawn = base * np.exp(spread * noise) if base else spread * noise
        out[name] = jnp.asarray(drawn.astype(out[name].dtype))
    for name, factor in factors.items():
        out[name] = (out[name] * factor).astype(out[name].dtype)
    return out
```

```python
from contextlib import ExitStack

import concourse.bass as bass
from concourse import mybir

ALU = mybir.AluOpType
ACT = mybir.ActivationFunctionType
AX = mybir.AxisListType
F32 = mybir.dt.float32
BF16 = mybir.dt.bfloat16
I32 = mybir.dt.int32
U32 = mybir.dt.uint32

P = 128
B, S, D = 4, 256, 256
N = B * S
KD = D // P
TB = S // P
NT = N // P
E0, VOCAB = 4, 12500
PER = VOCAB // E0
E, K, F, CAP = 64, 4, 64, 32
SLOTS = E * CAP
ST = SLOTS // P
EP = P // CAP
SF = 512
NF = SF // P
NH, DH = 16, 16
E1, R1 = 8, 64
NI = 1024
KI = NI // P
CLIP = 54
MAGIC = 12582912.0
FAR = 1048576.0
NEG = -1e30
LOWEST = -3.0e38


def flamingo(nc, a, out):
    ctx = ExitStack()
    with ctx:
        def sb(name, shape, dt=F32):
            return ctx.enter_context(nc.sbuf_tensor(name, shape, dt))

        def sem(name):
            return ctx.enter_context(nc.semaphore(name))

        bank = [ctx.enter_context(nc.psum_tensor(f"bank{i}", [P, 512], F32)) for i in range(8)]

        xg_dram = nc.dram_tensor("xg_rows", [SLOTS, D], F32, kind="Internal").ap()
        y_dram = nc.dram_tensor("y_rows", [SLOTS, D], F32, kind="Internal").ap()

        X = sb("X", [P, NT, D])
        HN = sb("HN", [P, NT, D])
        HT = sb("HT", [P, KD, N])
        CN = sb("CN", [P, NT, D])
        CT = sb("CT", [P, KD, N])
        identf = sb("identf", [P, P])
        identb = sb("identb", [P, P], BF16)
        onesf = sb("onesf", [P, P])
        onesb = sb("onesb", [P, P], BF16)
        before = sb("before", [P, P], BF16)
        future = sb("future", [P, 3 * P], BF16)
        group = sb("group", [P, 8])
        parity = sb("parity", [P, 2])
        neghalf = sb("neghalf", [P, 32])
        gates8 = sb("gates8", [P, 8])
        tg = sb("tg", [P, 8])
        bnst = sb("bnst", [P, TB, 6])
        mv = sb("mv", [P, TB, 2])
        ve = sb("ve", [P, TB])
        rstd = sb("rstd", [P, TB])

        GROUPS = {"x": ["x"], "g": ["g"], "tokb": ["tokb"], "ctxT": ["ctxT"], "ctx": ["ctx"],
                  "router": ["router", "rbias"], "shared": ["sg", "su", "sd"],
                  "small": ["wi", "wf", "lnsc", "mix", "lg"] + [f"{g}{b}" for g in ("bi", "bf") for b in range(B)],
                  "lowrank": ["la", "lb"], "w2": ["wq", "wk", "wv", "wo"], "w3": ["w3q", "w3o"],
                  "q2g": ["q2g"], "q2u": ["q2u"], "q2d": ["q2d"], "q3a": ["q3a"], "q3b": ["q3b"]}
        group_sem = {g: sem("ld_" + g) for g in GROUPS}
        loads = {n: group_sem[g] for g, ns in GROUPS.items() for n in ns}

        def landed(eng, name):
            g = next(g for g, ns in GROUPS.items() if name in ns)
            eng.wait_ge(group_sem[g], 16 * len(GROUPS[g]))

        ar = sb("ar", [P, 4096])
        tokb = ar[:, 0:N].bitcast(I32)
        ge = ar[:, N:2 * N].bitcast(BF16).rearrange("p (i n) -> p i n", i=2)
        maskb = ar[:, 2 * N:4 * N].bitcast(BF16).rearrange("p (e n) -> p e n", e=E0)
        HM = sb("HM", [P, 2, E0 * KD * S])
        big = sb("big", [P, 12288])
        WK = sb("WK", [P, 2, 2048])
        WK2 = sb("WK2", [P, 2, 1024])
        SH = sb("SH", [P, 3072])
        SG = SH[:, 0:1024].rearrange("p (k f) -> p k f", k=KD)
        SU = SH[:, 1024:2048].rearrange("p (k f) -> p k f", k=KD)
        SD = SH[:, 2048:3072].rearrange("p (f d) -> p f d", d=D)
        RW = sb("RW", [P, KD, E])
        HS = HM[:].rearrange("p q (f n) -> p (q f) n", f=2)

        rbias = sb("rbias", [P, E])
        iota64 = sb("iota64", [P, E])
        eoff = sb("eoff", [P, E])
        zer = sb("zer", [P, D])
        lg = sb("lg", [P, TB, E])
        lgb = sb("lgb", [P, TB, E])
        top = sb("top", [P, TB, 8])
        topi = sb("topi", [P, TB, 8], U32)
        pick = sb("pick", [P, TB, K])
        nmax = sb("nmax", [P, TB])
        ex = sb("ex", [P, NT, E])
        ph = sb("ph", [P, 5120])
        oh = ph[:, 0:1024].bitcast(BF16).rearrange("p (t k e) -> p t k e", t=NT, k=K)
        ohx = ph[:, 1024:1536].rearrange("p (i e) -> p i e", e=E)
        chosen = sb("chosen", [P, NT, E], BF16)
        earlier = sb("earlier", [P, NT + 1, E], BF16)
        wk4 = sb("wk4", [P, TB, K])
        wsum = sb("wsum", [P, TB])
        W4 = sb("W4", [P, NT, K])
        val = sb("val", [P, TB, E])
        far = sb("far", [P, TB, E])
        slotf = sb("slotf", [P, TB, K])
        slot = sb("slot", [P, NT, K], U32)
        SSL = ph[:, 1536:2560].rearrange("p (q n) -> p q n", q=2)
        xgt = ph[:, 2560:3584].rearrange("p (q d) -> p q d", q=4)
        xgT = ph[:, 3584:4096].rearrange("p (q k n) -> p q k n", q=2, k=KD)
        sil = sb("sil", [P, 2, P])
        he = sb("he", [P, 2, 2, 2 * CAP])
        ye = ph[:, 4096:5120].rearrange("p (q d) -> p q d", q=4)
        G4 = WK[:].rearrange("p q (h k d) -> p (q h) k d", k=K, d=D)[:, 0:2]

        WIF = sb("WIF", [P, 2, 3 * KD, 32])
        bif = sb("bif", [P, 2])
        lns = sb("lns", [P, NH * DH])
        selc = sb("selc", [P, NH], BF16)
        sel = sb("sel", [P, NH, P], BF16)
        rows = WK2[:].rearrange("p q (r n) -> p (q r) n", n=S)
        fgt, nf, e1, lf, Fc, ga, cm, nx = (rows[:, r, :] for r in range(8))
        part = sb("part", [P, 3, S], BF16)
        CMP = sb("CMP", [P, B, S], BF16)
        ATN = sb("ATN", [P, 2 * TB, P])
        V1 = HM[:].rearrange("p q f -> p (q f)")[:, 0:NT * NH * 17].rearrange("p (t h c) -> p t h c", t=NT, c=17)
        dcs = HM[:].rearrange("p q f -> p (q f)")[:, NT * NH * 17:NT * NH * 17 + 4 * 384]\
            .rearrange("p (q n) -> p q n", n=384)
        KZ = WK[:, :, 0:KD * 2 * S].rearrange("p q (k r n) -> p q k r n", k=KD, r=2)
        HR = ar[:, 0:TB * NH * 17].rearrange("p (i c) -> p i c", c=17)
        hh = ar[:, 544:544 + 512].rearrange("p (i c) -> p i c", c=DH)
        sq = ar[:, 1056:1056 + 512].rearrange("p (i c) -> p i c", c=DH)
        ab = sb("ab", [P, TB * NH])
        mu = sb("mu", [P, TB * NH])
        vr = sb("vr", [P, TB * NH])
        rs = sb("rs", [P, TB * NH])

        LA = SH[:, 0:1024].rearrange("p (k f) -> p k f", k=KD)
        LB = SH[:, 1024:2048].rearrange("p (f d) -> p f d", d=D)
        LG = sb("LG", [P, KD, E1])
        lg1 = sb("lg1", [P, TB, E1])
        ex1 = sb("ex1", [P, TB, E1])
        top1 = sb("top1", [P, TB, 8])
        topi1 = sb("topi1", [P, TB, 8], U32)
        pick1 = sb("pick1", [P, TB])
        nmax1 = sb("nmax1", [P, TB])
        sum1 = sb("sum1", [P, TB])
        MK = sb("MK", [P, TB, E1])
        wkf = WK[:].rearrange("p q f -> p (q f)")
        HM1 = wkf[:, 0:1024].rearrange("p (j f) -> p j f", j=TB)
        HMT = wkf[:, 2048:3072].rearrange("p (f n) -> p f n", n=S)

        W2 = ar[:, 2048:4096].rearrange("p (w k d) -> p w k d", w=4, k=KD)
        QT = wkf[:, 0:512].rearrange("p (m n) -> p m n", m=KD)
        KT = wkf[:, 512:1024].rearrange("p (m n) -> p m n", m=KD)
        VN = wkf[:, 1024:1536].rearrange("p (j d) -> p j d", j=TB)
        PR = wkf[:, 1536:2560].rearrange("p (j n) -> p j n", j=TB)
        PT = wkf[:, 2560:3584].rearrange("p (c n) -> p c n", n=S)
        OT = wkf[:, 3584:4096].rearrange("p (m n) -> p m n", m=KD)
        nmax2 = sb("nmax2", [P, TB])
        sum2 = sb("sum2", [P, TB])

        NQ = 5
        RAW = [big[:, 2048 * i:2048 * (i + 1)] for i in range(NQ)]
        QW = ph[:].bitcast(BF16).rearrange("p (i c) -> p i c", i=NQ)
        asum = sb("asum", [P, NQ])
        wsc = sb("wsc", [P, NQ])
        wrec = sb("wrec", [P, NQ])
        amax = sb("amax", [P, TB])
        sx = sb("sx", [P, NT])
        rq = sb("rq", [P, TB])
        fg = sb("fg", [P, NT, 2])
        hmf = HM[:].rearrange("p q f -> p (q f)")
        XF = hmf[:, 0:512].rearrange("p (j d) -> p j d", j=TB)
        XQ = hmf[:, 512:1536].bitcast(BF16).rearrange("p (b j d) -> p b j d", b=B, j=TB)
        XQT = hmf[:, 1536:2048].bitcast(BF16).rearrange("p (q k n) -> p q k n", q=2, k=KD)
        am1 = sb("am1", [P, 1])
        sh1 = sb("sh1", [P, 1])
        rh1 = sb("rh1", [P, 1])
        fy1 = sb("fy1", [P, 1])
        H = [WK[:, q, 0:NI] for q in range(2)]
        HQ = [WK[:, q, NI:NI + 512].bitcast(BF16) for q in range(2)]
        HQT = [WK[:, q, NI + 512:NI + 1024].bitcast(BF16).rearrange("p (f n) -> p f n", f=KI) for q in range(2)]
        GS = [WK2[:, q, 0:NI] for q in range(2)]

        W3 = SH[:, 2048:3072].rearrange("p (w k d) -> p w k d", w=2, k=KD)
        mix = sb("mix", [P, 4])
        alpha = sb("alpha", [P, 1])
        coef = sb("coef", [P, 1])
        cf2 = sb("cf2", [P, 1])
        SC = wkf[:, 512:1024].rearrange("p (j n) -> p j n", j=TB)
        WR = wkf[:, 1024:1536].rearrange("p (j n) -> p j n", j=TB)
        EX3 = wkf[:, 1536:2048].rearrange("p (j n) -> p j n", j=TB)
        P3 = wkf[:, 2048:2560].rearrange("p (j n) -> p j n", j=TB)
        PT3 = wkf[:, 2560:3072].rearrange("p (c n) -> p c n", n=S)
        top3 = sb("top3", [P, TB, 8])

        names = ("s_vec s_pool s_const s_tanh s_masks s_lnvar s_lnrstd s_norm s_turned s_ht "
                 "s_hm s_z s_silu s_gm s_y0 s_x s_out "
                 "s_lg s_nmax s_ex s_m s_count s_slot s_zero s_hsg s_ssl s_hs s_ysh s_xsh s_scat s_xgturned s_xgT "
                 "s_egu s_esil s_he s_ey s_ye s_g0 s_gx "
                 "s_par s_v1 s_gate s_nf s_ln s_m1 s_nx s_part s_cmp s_trd s_atn s_kz s_dq s_dexp s_cs s_pv "
                 "s_hcp s_v16 s_r16 s_wif0 "
                 "s_l1 s_nm1 s_ex1 s_hm1 s_hmt s_hmc s_y1 s_xl1 "
                 "s_qkv s_qk2 s_v2 s_sc2 s_nm2 s_ex2 s_pt2 s_ptc2 s_o2 s_oc2 s_y2 s_x2 "
                 "s_asum s_wtot s_wsc s_qw s_mixe s_coef "
                 "s_qn s_qt s_qc s_gu s_gs s_hq s_hqt s_hqc s_yq s_xq s_qr "
                 "s_q3 s_qc3 s_sc3 s_m3 s_ex3 s_p3 s_pt3 s_ptc3 s_o3 s_oc3 s_y3 s_x3").split()
        s = {n: sem(n) for n in names}

        def counter(name):
            c = [0]
            sm = s[name]

            def link(eng, ins):
                c[0] += 1
                ins.then_inc(sm, 1)
                eng.wait_ge(sm, c[0])
            return link

        s_xg = [sem(f"s_xg{i}") for i in range(4)]
        s_ys = [sem(f"s_ys{i}") for i in range(4)]
        s_gat = [sem(f"s_gat{i}") for i in range(2)]
        s_ew = [sem(f"s_ew{i}") for i in range(2)]
        CH = 4
        NCH = ST // CH
        ew = [big[:, 6144 * q:6144 * (q + 1)] for q in range(2)]
        egw = [w[:, 0:2048].rearrange("p (k c) -> p k c", k=KD) for w in ew]
        euw = [w[:, 2048:4096].rearrange("p (k c) -> p k c", k=KD) for w in ew]
        edw = [w[:, 4096:6144].rearrange("p (i d) -> p i d", d=D) for w in ew]

        DMAS = [("x", X[:], a["x"].rearrange("(t p) d -> p t d", p=P)),
                ("g", gates8[:], a["g"].rearrange("(o n) -> o n", o=1).broadcast_to([P, 8])),
                ("tokb", tokb, a["tok"].rearrange("(o n) -> o n", o=1).broadcast_to([P, N])),
                ("ctxT", CT[:], a["ctxT"].rearrange("(k p) n -> p k n", p=P)),
                ("ctx", CN[:], a["ctx"].rearrange("(t p) d -> p t d", p=P)),
                ("router", RW[:], a["router"].rearrange("(k p) e -> p k e", p=P)),
                ("rbias", rbias[:], a["router_bias"].rearrange("(o n) -> o n", o=1).broadcast_to([P, E])),
                ("sg", SG, a["sg"].rearrange("(k p) f -> p k f", p=P)),
                ("su", SU, a["su"].rearrange("(k p) f -> p k f", p=P)),
                ("sd", SD, a["sd"].rearrange("(k p) d -> p k d", p=P)),
                ]
        for g, (w, bi) in enumerate((("wi", "bi"), ("wf", "bf"))):
            DMAS.append((w, WIF[:, g, :, 0:NH], a[w].rearrange("(k p) h -> p k h", p=P)))
            for b in range(B):
                DMAS.append((f"{bi}{b}", bif[32 * b:32 * b + NH, g:g + 1], a[bi].rearrange("(h o) -> h o", o=1)))
        DMAS.append(("lnsc", lns[:], a["lnsc"].rearrange("(o n) -> o n", o=1).broadcast_to([P, D])))
        DMAS.append(("lg", LG[:], a["lg"].rearrange("(k p) e -> p k e", p=P)))
        DMAS.append(("mix", mix[:], a["mix"].rearrange("(o n) -> o n", o=1).broadcast_to([P, 4])))

        block = ctx.enter_context(nc.Block())

        @block.sync
        def _(sp):
            for n, dst, src in DMAS:
                if n == "wi":
                    sp.wait_ge(s["s_wif0"], 1)
                sp.dma_start(dst, src).then_inc(loads[n], 16)
            sp.wait_ge(s["s_const"], 1)
            sp.dma_start(xg_dram.rearrange("(t p) d -> p t d", p=P),
                         zer[:].unsqueeze(1).broadcast_to([P, ST, D])).then_inc(s["s_zero"], 16)

            def expert_weights(c):
                q = c % 2
                if c >= 2:
                    sp.wait_ge(s["s_ey"], CH * (c - 1))
                w = CH * EP * F
                sp.dma_start(egw[q], a["eg"][:, w * c:w * (c + 1)].rearrange("(k p) c -> p k c", p=P))\
                    .then_inc(s_ew[q], 16)
                sp.dma_start(euw[q], a["eu"][:, w * c:w * (c + 1)].rearrange("(k p) c -> p k c", p=P))\
                    .then_inc(s_ew[q], 16)
                sp.dma_start(edw[q], a["ed"][w * c:w * (c + 1), :].rearrange("(i p) d -> p i d", p=P))\
                    .then_inc(s_ew[q], 16)

            expert_weights(0)
            expert_weights(1)
            sp.wait_ge(s["s_scat"], 16 * NT * K)
            for t in range(ST):
                if t >= 4:
                    sp.wait_ge(s["s_xgturned"], t - 3)
                sp.dma_start(xgt[:, t % 4, :], xg_dram[P * t:P * (t + 1), :]).then_inc(s_xg[t % 4], 16)
                if t % CH == CH - 1 and t // CH + 2 < NCH:
                    expert_weights(t // CH + 2)
            sp.wait_ge(s["s_ysh"], B)
            sp.dma_start(LA, a["la"].rearrange("(k p) f -> p k f", p=P)).then_inc(loads["la"], 16)
            sp.dma_start(LB, a["lb"].rearrange("(f p) d -> p f d", p=P)).then_inc(loads["lb"], 16)
            for n, w in enumerate(("wq", "wk", "wv", "wo")):
                sp.dma_start(W2[:, n], a[w].rearrange("(k p) e -> p k e", p=P)).then_inc(loads[w], 16)
            sp.dma_start(W3[:, 0], a["w3q"].rearrange("(k p) e -> p k e", p=P)).then_inc(loads["w3q"], 16)
            sp.dma_start(W3[:, 1], a["w3o"].rearrange("(k p) e -> p k e", p=P)).then_inc(loads["w3o"], 16)
            sp.wait_ge(s["s_ey"], ST)
            for i, n in enumerate(("q2g", "q2u", "q2d", "q3a", "q3b")):
                sp.dma_start(RAW[i].rearrange("p (k c) -> p k c", k=a[n].shape[0] // P),
                             a[n].rearrange("(k p) c -> p k c", p=P)).then_inc(loads[n], 16)
            sp.wait_ge(s["s_x"], 1)
            sp.dma_start(out.rearrange("(t p) d -> p t d", p=P), X[:]).then_inc(s["s_out"], 16)
            sp.wait_ge(s["s_out"], 16)

        def layernorm_rstd(pool, u):
            pool.wait_ge(s["s_lnvar"], u + 1)
            pool.tensor_tensor(rstd[:], ve[:], neghalf[:, 0:TB], ALU.pow).then_inc(s["s_lnrstd"], 1)

        @block.gpsimd
        def _(pool):
            link0 = counter("s_pool")

            def link(ins):
                link0(pool, ins)
            pool.memset(WIF[:], 0.0)
            pool.memset(bif[:], 0.0).then_inc(s["s_wif0"], 1)
            pool.memset(identf[:], 0.0)
            pool.memset(onesf[:], 1.0)
            pool.memset(onesb[:], 1.0)
            pool.memset(future[:], 0.0)
            pool.memset(group[:], 1.0)
            pool.memset(zer[:], 0.0)
            pool.memset(he[:], 0.0)
            pool.memset(earlier[:, 0, :], 0.0)
            pool.iota(iota64[:], [[1, E]], base=0, channel_multiplier=0, allow_small_or_imprecise_dtypes=True)
            pool.iota(eoff[:], [[CAP, E]], base=0, channel_multiplier=0, allow_small_or_imprecise_dtypes=True)
            link(pool.memset(neghalf[:], -0.5))
            pool.affine_select(out=before[:], in_=onesb[:], compare_op=ALU.is_gt, fill=0.0, base=0,
                               pattern=[[1, P]], channel_multiplier=-1)
            for c in (0, 2):
                pool.affine_select(out=future[:, P * c:P * (c + 1)], in_=future[:, P * c:P * (c + 1)],
                                   compare_op=ALU.is_ge, fill=NEG, base=0, pattern=[[1, P]], channel_multiplier=-1)
            pool.affine_select(out=identf[:], in_=identf[:], compare_op=ALU.not_equal, fill=1.0, base=0,
                               pattern=[[-1, P]], channel_multiplier=1)
            link(pool.affine_select(out=group[:], in_=group[:], compare_op=ALU.is_ge, fill=0.0, base=0,
                                    pattern=[[-16, 8]], channel_multiplier=1))
            link(pool.affine_select(out=group[:], in_=group[:], compare_op=ALU.is_ge, fill=0.0, base=15,
                                    pattern=[[16, 8]], channel_multiplier=-1))
            pool.tensor_copy(identb[:], identf[:]).then_inc(s["s_const"], 1)
            landed(pool, "tokb")
            g1, g2 = ge[:, 0, :], ge[:, 1, :]
            link(pool.tensor_scalar(g1, tokb, float(PER), None, ALU.is_ge))
            link(pool.tensor_scalar(maskb[:, 0, :], g1, -1.0, 1.0, ALU.mult, ALU.add))
            link(pool.tensor_scalar(g2, tokb, float(2 * PER), None, ALU.is_ge))
            link(pool.tensor_tensor(maskb[:, 1, :], g1, g2, ALU.subtract))
            link(pool.tensor_scalar(maskb[:, 3, :], tokb, float(3 * PER), None, ALU.is_ge))
            pool.tensor_tensor(maskb[:, 2, :], g2, maskb[:, 3, :], ALU.subtract).then_inc(s["s_masks"], 1)
            for b in range(B):
                layernorm_rstd(pool, b)
            for b in range(B):
                layernorm_rstd(pool, B + b)
            pool.wait_ge(s["s_zero"], 16)
            for t in range(NT):
                if t % TB == 0:
                    pool.wait_ge(s["s_slot"], t // TB + 1)
                for k in range(K):
                    pool.indirect_dma_start(out=xg_dram, out_offset=bass.IndirectOffsetOnAxis(slot[:, t, k:k + 1], 0),
                                            in_=HN[:, t, :], in_offset=None, bounds_check=SLOTS - 1,
                                            oob_is_err=False).then_inc(s["s_scat"], 16)
            for t in range(ST):
                pool.wait_ge(s["s_ye"], t + 1)
                pool.dma_start(y_dram[P * t:P * (t + 1), :], ye[:, t % 4, :]).then_inc(s_ys[t % 4], 16)
            for q in range(4):
                pool.wait_ge(s_ys[q], 16 * ST // 4)
            for t in range(NT):
                q = t % 2
                if t >= 2:
                    pool.wait_ge(s["s_gx"], t - 1)
                pool.memset(G4[:, q], 0.0).then_inc(s["s_g0"], 1)
                pool.wait_ge(s["s_g0"], t + 1)
                for k in range(K):
                    pool.indirect_dma_start(out=G4[:, q, k, :], out_offset=None, in_=y_dram,
                                            in_offset=bass.IndirectOffsetOnAxis(slot[:, t, k:k + 1], 0),
                                            bounds_check=SLOTS - 1, oob_is_err=False).then_inc(s_gat[q], 16)
            pool.wait_ge(s["s_ysh"], B)
            landed(pool, "ctx")
            pool.memset(V1[:, :, :, DH:17], 1.0)
            for t in range(NT):
                last = pool.tensor_copy(V1[:, t, :, 0:DH], CN[:, t, :].rearrange("p (h c) -> p h c", c=DH))
            last.then_inc(s["s_v1"], 1)
            for b in range(B):
                layernorm_rstd(pool, 2 * B + b)
            pool.wait_ge(s["s_par"], 1)
            pool.wait_ge(s["s_gx"], NT)
            for b in range(B):
                if b >= 2:
                    pool.wait_ge(s["s_pv"], NH * (b - 1))
                for k in range(KD):
                    for r in range(2):
                        last = pool.tensor_scalar(KZ[:, b % 2, k, r, :], CT[:, k, S * b:S * (b + 1)],
                                                  parity[:, r:r + 1], None, ALU.mult)
                last.then_inc(s["s_kz"], 1)
                if b >= 1:
                    pool.wait_ge(s["s_v16"], b)
                    pool.tensor_tensor(rs[:], vr[:], neghalf[:], ALU.pow).then_inc(s["s_r16"], 1)
                    pool.wait_ge(s["s_wsc"], 1)
                    for i in range(2 * b - 2, min(2 * b, NQ)):
                        link(pool.tensor_scalar(RAW[i], RAW[i], wrec[:, i:i + 1], 1.0, ALU.mult, ALU.min))
                        link(pool.tensor_scalar(RAW[i], RAW[i], -1.0, MAGIC, ALU.max, ALU.add))
                        pool.tensor_scalar(QW[:, i, :], RAW[i], -MAGIC, None, ALU.add).then_inc(s["s_qw"], 1)
            pool.wait_ge(s["s_v16"], B)
            pool.tensor_tensor(rs[:], vr[:], neghalf[:], ALU.pow).then_inc(s["s_r16"], 1)
            for b in range(B):
                layernorm_rstd(pool, 3 * B + b)
            for l in range(4, 8):
                for b in range(B):
                    layernorm_rstd(pool, l * B + b)

        @block.vector
        def _(dve):
            link0 = counter("s_vec")

            def link(ins):
                link0(dve, ins)

            def layernorm(l, b):
                u = B * l + b
                for j in range(TB):
                    last = dve.bn_stats(bnst[:, j, :], X[:, TB * b + j, :])
                link(last)
                for j in range(TB):
                    last = dve.bn_aggr(mv[:, j, :], bnst[:, j, :])
                link(last)
                dve.tensor_scalar(ve[:], mv[:, :, 1], 1e-5, None, ALU.add).then_inc(s["s_lnvar"], 1)
                dve.wait_ge(s["s_lnrstd"], u + 1)
                for j in range(TB):
                    last = dve.tensor_scalar(HN[:, TB * b + j, :], X[:, TB * b + j, :], mv[:, j, 0:1],
                                             rstd[:, j:j + 1], ALU.subtract, ALU.mult)
                last.then_inc(s["s_norm"], 1)

            landed(dve, "x")
            dve.wait_ge(s["s_const"], 1)
            dve.tensor_reduce(parity[:], group[:].rearrange("p (g two) -> p two g", two=2), AX.X, ALU.add)\
                .then_inc(s["s_par"], 1)
            link(dve.tensor_tensor(selc[:], identb[:, 0:NH], identb[:, 32:32 + NH], ALU.add))
            link(dve.tensor_tensor(selc[:], selc[:], identb[:, 64:64 + NH], ALU.add))
            dve.tensor_copy(sel[:], selc[:].unsqueeze(2).broadcast_to([P, NH, P]))
            for b in range(B):
                layernorm(0, b)
            for b in range(B):
                q = b % 2
                hm = HM[:, q, :].rearrange("p (e k n) -> p e k n", e=E0, k=KD)
                gmk = WK[:, q, :].rearrange("p (e k n) -> p e k n", e=E0, k=KD)
                dve.wait_ge(s["s_masks"], 1)
                dve.wait_ge(s["s_ht"], b + 1)
                if b >= 2:
                    dve.wait_ge(s["s_z"], b - 1)
                for e in range(E0):
                    for k in range(KD):
                        last = dve.tensor_tensor(hm[:, e, k, :], HT[:, k, S * b:S * (b + 1)],
                                                 maskb[:, e, S * b:S * (b + 1)], ALU.mult)
                last.then_inc(s["s_hm"], 1)
                gz = WK2[:, q, 0:512].rearrange("p (k n) -> p k n", k=KD)
                dve.wait_ge(s["s_silu"], b + 1)
                link(dve.tensor_tensor(gz, gz, bank[2 + q][:].rearrange("p (k n) -> p k n", k=KD), ALU.mult))
                if b >= 2:
                    dve.wait_ge(s["s_y0"], b - 1)
                for e in range(E0):
                    for k in range(KD):
                        last = dve.tensor_tensor(gmk[:, e, k, :], gz[:, k, :],
                                                 maskb[:, e, S * b:S * (b + 1)], ALU.mult)
                last.then_inc(s["s_gm"], 1)
                dve.wait_ge(s["s_y0"], b + 1)
                dve.wait_ge(s["s_tanh"], 1)
                xb = X[:, TB * b:TB * (b + 1), :]
                link(dve.scalar_tensor_tensor(out=xb, in0=bank[4 + q][:].rearrange("p (j d) -> p j d", j=TB),
                                              scalar=tg[:, 0:1], in1=xb, op0=ALU.mult, op1=ALU.add))
            for b in range(B):
                layernorm(1, b)
            landed(dve, "rbias")
            for b in range(B):
                t0, t1 = TB * b, TB * (b + 1)
                dve.wait_ge(s["s_lg"], b + 1)
                link(dve.tensor_copy(lg[:], bank[2][:, 0:TB * E].rearrange("p (j e) -> p j e", j=TB)))
                dve.tensor_tensor(lgb[:], lg[:], rbias[:].unsqueeze(1).broadcast_to([P, TB, E]), ALU.add)
                link(dve.tensor_reduce(nmax[:], lg[:], AX.X, ALU.max, negate=True))
                for j in range(TB):
                    last = dve.max(top[:, j, :], lgb[:, j, :])
                link(last)
                for j in range(TB):
                    last = dve.max_index(topi[:, j, :], top[:, j, :], lgb[:, j, :])
                last.then_inc(s["s_nmax"], 1)
                dve.wait_ge(s["s_nmax"], b + 1)
                link(dve.tensor_copy(pick[:], topi[:, :, 0:K]))
                for j in range(TB):
                    last = dve.tensor_tensor(oh[:, t0 + j], iota64[:].unsqueeze(1).broadcast_to([P, K, E]),
                                             pick[:, j, :].unsqueeze(2).broadcast_to([P, K, E]), ALU.is_equal)
                link(last)
                with nc.allow_low_precision(reason="sums of at most 4 zeros and ones"):
                    link(dve.tensor_reduce(chosen[:, t0:t1, :], oh[:, t0:t1].rearrange("p j k e -> p j e k"),
                                           AX.X, ALU.add))
                link(dve.tensor_tensor(earlier[:, t0 + 1, :], earlier[:, t0, :], chosen[:, t0, :], ALU.add))
                dve.tensor_tensor(earlier[:, t0 + 2, :], earlier[:, t0 + 1, :], chosen[:, t0 + 1, :], ALU.add)\
                    .then_inc(s["s_m"], 1)
                dve.wait_ge(s["s_m"], b + 1)
                dve.wait_ge(s["s_ex"], b + 1)
                for j in range(TB):
                    last = dve.tensor_tensor(ohx[:, K * j:K * (j + 1), :], oh[:, t0 + j],
                                             ex[:, t0 + j, :].unsqueeze(1).broadcast_to([P, K, E]), ALU.mult)
                link(last)
                link(dve.tensor_reduce(wk4[:].rearrange("p j k -> p (j k)"), ohx, AX.X, ALU.add))
                link(dve.tensor_reduce(wsum[:], wk4[:], AX.X, ALU.add))
                link(dve.reciprocal(wsum[:], wsum[:]))
                for j in range(TB):
                    last = dve.tensor_scalar(W4[:, t0 + j, :], wk4[:, j, :], wsum[:, j:j + 1], tg[:, 4:5],
                                             ALU.mult, ALU.mult)
                link(last)
            for b in range(B):
                t0, t1 = TB * b, TB * (b + 1)
                dve.wait_ge(s["s_count"], b + 1)
                cnt = bank[3 + 4 * (b % 2)][:, 0:TB * E].rearrange("p (j e) -> p j e", j=TB)
                dve.tensor_scalar(far[:], cnt, float(CAP), FAR, ALU.is_ge, ALU.mult)
                link(dve.tensor_tensor(val[:], cnt, eoff[:].unsqueeze(1).broadcast_to([P, TB, E]), ALU.add))
                link(dve.tensor_tensor(val[:], val[:], far[:], ALU.add))
                for j in range(TB):
                    last = dve.tensor_tensor(ohx[:, K * j:K * (j + 1), :], oh[:, t0 + j],
                                             val[:, j, :].unsqueeze(1).broadcast_to([P, K, E]), ALU.mult)
                link(last)
                link(dve.tensor_reduce(slotf[:].rearrange("p j k -> p (j k)"), ohx, AX.X, ALU.add))
                dve.tensor_copy(slot[:, t0:t1, :], slotf[:]).then_inc(s["s_slot"], 1)
            for c in range(2):
                for f in range(NF):
                    i = NF * c + f
                    dve.wait_ge(s["s_ssl"], i + 1)
                    dve.tensor_tensor(HS[:, f, 512 * c:512 * (c + 1)], SSL[:, i % 2, :], bank[4 + i % 2][:],
                                      ALU.mult).then_inc(s["s_hs"], 1)
            for b in range(B):
                dve.wait_ge(s["s_ysh"], b + 1)
                xb = X[:, TB * b:TB * (b + 1), :]
                dve.scalar_tensor_tensor(out=xb, in0=bank[6 + b % 2][:].rearrange("p (j d) -> p j d", j=TB),
                                         scalar=tg[:, 4:5], in1=xb, op0=ALU.mult, op1=ALU.add)\
                    .then_inc(s["s_xsh"], 1)
            dve.wait_ge(s["s_xsh"], B)
            for t in range(ST):
                q = t % 2
                dve.wait_ge(s["s_esil"], t + 1)
                if t >= 2:
                    dve.wait_ge(s["s_ey"], t - 1)
                for h in range(2):
                    r = slice(F * h, F * (h + 1))
                    cols = slice(CAP * h, CAP * (h + 1))
                    sl = sil[:, q, :].rearrange("p (i c) -> p i c", i=2)
                    up = bank[2 + q][:, P:2 * P].rearrange("p (i c) -> p i c", i=2)
                    last = dve.tensor_tensor(he[r, q, :, cols], sl[r, :, cols], up[r, :, cols], ALU.mult)
                last.then_inc(s["s_he"], 1)
            for t in range(NT):
                dve.wait_ge(s_gat[t % 2], 16 * K * (t // 2 + 1))
                for k in range(K):
                    last = dve.scalar_tensor_tensor(out=X[:, t, :], in0=G4[:, t % 2, k, :], scalar=W4[:, t, k:k + 1],
                                                    in1=X[:, t, :], op0=ALU.mult, op1=ALU.add)
                    if k < K - 1:
                        link(last)
                last.then_inc(s["s_gx"], 1)
                dve.wait_ge(s["s_gx"], t + 1)
            for b in range(B):
                layernorm(2, b)
            landed(dve, "lnsc")
            for g in ("bi", "bf"):
                for b in range(B):
                    landed(dve, f"{g}{b}")
            link(dve.tensor_scalar(lns[:], lns[:], tg[:, 1:2], None, ALU.mult))
            dve.wait_ge(s["s_gate"], 1)
            link(dve.tensor_scalar(fgt, bank[3][:, 0:S], bif[:, 1:2], None, ALU.add))
            dve.scalar_tensor_tensor(out=nf, in0=fgt, scalar=-1.0, in1=fgt, op0=ALU.mult, op1=ALU.min)\
                .then_inc(s["s_nf"], 1)
            dve.wait_ge(s["s_ln"], 2)
            link(dve.scalar_tensor_tensor(out=lf, in0=fgt, scalar=0.0, in1=e1, op0=ALU.min, op1=ALU.subtract))
            link(dve.tensor_tensor_scan(Fc, lf, zer[:], 0.0, ALU.add, ALU.add))
            link(dve.scalar_tensor_tensor(out=ga, in0=bank[2][:, 0:S], scalar=bif[:, 0:1], in1=Fc,
                                          op0=ALU.add, op1=ALU.subtract))
            link(dve.tensor_tensor_scan(cm, ga, ga, LOWEST, ALU.max, ALU.max))
            dve.tensor_tensor(Fc, Fc, cm, ALU.add).then_inc(s["s_m1"], 1)
            link(dve.tensor_scalar(part[:, 0, :], cm, -1.0, None, ALU.mult))
            link(dve.scalar_tensor_tensor(out=lf, in0=cm, scalar=-1.0, in1=part[:, 0, :], op0=ALU.mult,
                                          op1=ALU.subtract))
            link(dve.tensor_copy(part[:, 1, :], lf))
            link(dve.tensor_tensor(lf, lf, part[:, 1, :], ALU.subtract))
            dve.tensor_copy(part[:, 2, :], lf).then_inc(s["s_part"], 1)

            def heads_norm(b):
                dve.wait_ge(s["s_hcp"], b + 1)
                sums = HR[:, :, DH]
                link(dve.scalar_tensor_tensor(out=ab[:], in0=sums, scalar=-1.0, in1=sums, op0=ALU.mult, op1=ALU.max))
                link(dve.tensor_tensor(ab[:].rearrange("p (j h) -> p j h", j=TB),
                                       ab[:].rearrange("p (j h) -> p j h", j=TB),
                                       ATN[:, TB:2 * TB, 32 * b:32 * b + NH], ALU.max))
                link(dve.tensor_scalar(ab[:], ab[:], 1e-6, None, ALU.add))
                link(dve.reciprocal(ab[:], ab[:]))
                link(dve.tensor_tensor(hh, HR[:, :, 0:DH], ab[:].unsqueeze(2).broadcast_to([P, TB * NH, DH]), ALU.mult))
                link(dve.tensor_reduce(mu[:], hh, AX.X, ALU.add))
                link(dve.tensor_scalar(mu[:], mu[:], 1.0 / DH, None, ALU.mult))
                link(dve.tensor_tensor(hh, hh, mu[:].unsqueeze(2).broadcast_to([P, TB * NH, DH]), ALU.subtract))
                link(dve.tensor_tensor(sq, hh, hh, ALU.mult))
                link(dve.tensor_reduce(vr[:], sq, AX.X, ALU.add))
                link(dve.tensor_scalar(vr[:], vr[:], 1.0 / DH, 1e-6, ALU.mult, ALU.add))
                dve.engine_nop().then_inc(s["s_v16"], 1)
                dve.wait_ge(s["s_r16"], b + 1)
                link(dve.tensor_tensor(hh, hh, rs[:].unsqueeze(2).broadcast_to([P, TB * NH, DH]), ALU.mult))
                h2 = ar[:, 544:544 + 512].rearrange("p (j d) -> p j d", j=TB)
                link(dve.tensor_tensor(h2, h2, lns[:].unsqueeze(1).broadcast_to([P, TB, D]), ALU.mult))
                link(dve.tensor_tensor(X[:, TB * b:TB * (b + 1), :], X[:, TB * b:TB * (b + 1), :], h2, ALU.add))

            for i in range(B * NH):
                dve.wait_ge(s["s_dexp"], i + 1)
                if i >= 2:
                    dve.wait_ge(s["s_pv"], i - 1)
                dve.scalar_tensor_tensor(out=dcs[:, 2 + i % 2, :], in0=bank[4 + i % 2][:, 0:384], scalar=DH ** -0.5,
                                         in1=dcs[:, i % 2, :], op0=ALU.mult, op1=ALU.mult).then_inc(s["s_cs"], 1)
                if i >= NH and i % NH == 2:
                    heads_norm(i // NH - 1)
                if i == 12:
                    dve.wait_ge(s["s_wtot"], 1)
                    link(dve.tensor_scalar(wsc[:], bank[0][:, 0:NQ], 1.0 / (NI * D), 1e-5, ALU.mult, ALU.add))
                    dve.reciprocal(wrec[:], wsc[:]).then_inc(s["s_wsc"], 1)
            heads_norm(B - 1)
            for b in range(B):
                layernorm(3, b)
            for b in range(B):
                dve.wait_ge(s["s_l1"], b + 1)
                link(dve.tensor_copy(lg1[:], bank[6][:, 0:TB * E1].rearrange("p (j e) -> p j e", j=TB)))
                link(dve.tensor_reduce(nmax1[:], lg1[:], AX.X, ALU.max, negate=True))
                for j in range(TB):
                    last = dve.max(top1[:, j, :], lg1[:, j, :])
                last.then_inc(s["s_nm1"], 1)
                dve.wait_ge(s["s_nm1"], b + 1)
                for j in range(TB):
                    last = dve.max_index(topi1[:, j, :], top1[:, j, :], lg1[:, j, :])
                link(last)
                link(dve.tensor_copy(pick1[:], topi1[:, :, 0]))
                link(dve.tensor_tensor(MK[:], iota64[:, 0:E1].unsqueeze(1).broadcast_to([P, TB, E1]),
                                       pick1[:].unsqueeze(2).broadcast_to([P, TB, E1]), ALU.is_equal))
                dve.wait_ge(s["s_ex1"], b + 1)
                link(dve.reciprocal(sum1[:], sum1[:]))
                link(dve.tensor_scalar(sum1[:], sum1[:], 64.0 / 16.0, tg[:, 5:6], ALU.mult, ALU.mult))
                link(dve.tensor_tensor(MK[:], MK[:], sum1[:].unsqueeze(2).broadcast_to([P, TB, E1]), ALU.mult))
                if b >= 1:
                    dve.wait_ge(s["s_hmt"], b)
                for j in range(TB):
                    last = dve.tensor_tensor(HM1[:, j, :].rearrange("p (e r) -> p e r", e=E1),
                                             bank[4 + j][:].rearrange("p (e r) -> p e r", e=E1),
                                             MK[:, j, :].unsqueeze(2).broadcast_to([P, E1, R1]), ALU.mult)
                last.then_inc(s["s_hm1"], 1)
                dve.wait_ge(s["s_y1"], b + 1)
                xb = X[:, TB * b:TB * (b + 1), :]
                dve.tensor_tensor(xb, xb, bank[7][:].rearrange("p (j d) -> p j d", j=TB), ALU.add)\
                    .then_inc(s["s_xl1"], 1)
            dve.wait_ge(s["s_xl1"], B)
            for b in range(B):
                layernorm(4, b)
            for b in range(B):
                dve.wait_ge(s["s_qkv"], b + 1)
                dve.tensor_copy(VN, bank[4][:].rearrange("p (j d) -> p j d", j=TB)).then_inc(s["s_v2"], 1)
                dve.wait_ge(s["s_sc2"], b + 1)
                for j in range(TB):
                    last = dve.tensor_reduce(nmax2[:, j:j + 1], bank[5 + j][:], AX.X, ALU.max, negate=True)
                link(last)
                dve.tensor_scalar(nmax2[:], nmax2[:], D ** -0.5, None, ALU.mult).then_inc(s["s_nm2"], 1)
                dve.wait_ge(s["s_ex2"], b + 1)
                link(dve.reciprocal(sum2[:], sum2[:]))
                link(dve.tensor_scalar(sum2[:], sum2[:], tg[:, 2:3], None, ALU.mult))
                dve.wait_ge(s["s_y2"], b + 1)
                for j in range(TB):
                    t = TB * b + j
                    last = dve.scalar_tensor_tensor(out=X[:, t, :], in0=bank[7][:, D * j:D * (j + 1)],
                                                    scalar=sum2[:, j:j + 1], in1=X[:, t, :], op0=ALU.mult, op1=ALU.add)
                last.then_inc(s["s_x2"], 1)
                dve.wait_ge(s["s_x2"], b + 1)

            def quantise_tokens(l, b, f):
                u = B * f + b
                t0, t1 = TB * b, TB * (b + 1)
                link(dve.tensor_reduce(amax[:], HN[:, t0:t1, :], AX.X, ALU.max, apply_absolute_value=True))
                if f == 0:
                    link(dve.tensor_scalar(sx[:, t0:t1], amax[:], 1.0 / 127.0, 1e-5, ALU.mult, ALU.add))
                else:
                    link(dve.tensor_scalar(sx[:, t0:t1], amax[:], 1e-5, 1.0 / 127.0, ALU.max, ALU.mult))
                link(dve.reciprocal(rq[:], sx[:, t0:t1]))
                for w in range(2 - f):
                    dve.tensor_scalar(fg[:, t0:t1, w], sx[:, t0:t1], wsc[:, 3 * f + w:3 * f + w + 1], None, ALU.mult)
                for j in range(TB):
                    last = dve.tensor_scalar(XF[:, j, :], HN[:, t0 + j, :], rq[:, j:j + 1], MAGIC, ALU.mult, ALU.add)
                link(last)
                dve.tensor_scalar(XQ[:, b], XF, -MAGIC, None, ALU.add).then_inc(s["s_qn"], 1)

            def quantise_hidden(v, f):
                q = v % 2
                link(dve.tensor_reduce(am1[:], H[q], AX.X, ALU.max, apply_absolute_value=True))
                if f == 0:
                    link(dve.tensor_scalar(sh1[:], am1[:], 1.0 / 127.0, 1e-5, ALU.mult, ALU.add))
                else:
                    link(dve.tensor_scalar(sh1[:], am1[:], 1e-5, 1.0 / 127.0, ALU.max, ALU.mult))
                link(dve.reciprocal(rh1[:], sh1[:]))
                link(dve.tensor_scalar(H[q], H[q], rh1[:], MAGIC, ALU.mult, ALU.add))
                if v >= 2:
                    dve.wait_ge(s["s_hqt"], v - 1)
                dve.tensor_scalar(HQ[q], H[q], -MAGIC, None, ALU.add).then_inc(s["s_hq"], 1)
                link(dve.tensor_scalar(fy1[:], sh1[:], wsc[:, 2 + 2 * f:3 + 2 * f], tg[:, 6 + f:7 + f], ALU.mult, ALU.mult))

            def add_product(v, t):
                dve.wait_ge(s["s_yq"], v + 1)
                dve.scalar_tensor_tensor(out=X[:, t, :], in0=bank[7][:, 0:D], scalar=fy1[:], in1=X[:, t, :],
                                         op0=ALU.mult, op1=ALU.add).then_inc(s["s_xq"], 1)
                dve.wait_ge(s["s_xq"], v + 1)

            for b in range(B):
                layernorm(5, b)
                dve.wait_ge(s["s_norm"], 5 * B + b + 1)
                quantise_tokens(5, b, 0)
            for t in range(NT):
                q = t % 2
                dve.wait_ge(s["s_gs"], t + 1)
                for n in range(2):
                    last = dve.scalar_tensor_tensor(out=H[q][:, 512 * n:512 * (n + 1)], in0=bank[4 + n][:],
                                                    scalar=fg[:, t, 1:2], in1=GS[q][:, 512 * n:512 * (n + 1)],
                                                    op0=ALU.mult, op1=ALU.mult)
                last.then_inc(s["s_qr"], 1)
                dve.wait_ge(s["s_qr"], t + 1)
                quantise_hidden(t, 0)
                add_product(t, t)
            dve.wait_ge(s["s_mixe"], 1)
            link(dve.tensor_scalar(coef[:], alpha[:], mix[:, 0:1], None, ALU.mult))
            link(dve.tensor_scalar(cf2[:], alpha[:], -1.0, 1.0, ALU.mult, ALU.add))
            link(dve.scalar_tensor_tensor(out=coef[:], in0=cf2[:], scalar=mix[:, 1:2], in1=coef[:],
                                          op0=ALU.mult, op1=ALU.add))
            link(dve.tensor_scalar(coef[:], coef[:], D ** -0.5, mix[:, 3:4], ALU.mult, ALU.mult))
            for b in range(B):
                layernorm(6, b)
            for b in range(B):
                dve.wait_ge(s["s_sc3"], b + 1)
                link(dve.tensor_scalar(SC, bank[3][:].rearrange("p (j n) -> p j n", j=TB), coef[:], None, ALU.mult))
                link(dve.tensor_reduce(nmax2[:], SC, AX.X, ALU.max, negate=True))
                for j in range(TB):
                    last = dve.tensor_scalar(SC[:, j, :], SC[:, j, :], nmax2[:, j:j + 1], None, ALU.add)
                last.then_inc(s["s_m3"], 1)
                dve.wait_ge(s["s_m3"], b + 1)
                for r in range((CLIP + 7) // 8):
                    src = SC if r == 0 else WR
                    for j in range(TB):
                        last = dve.max(top3[:, j, :], src[:, j, :])
                    link(last)
                    if 8 * (r + 1) < CLIP:
                        for j in range(TB):
                            last = dve.match_replace(WR[:, j, :], top3[:, j, :], src[:, j, :], LOWEST)
                        link(last)
                dve.wait_ge(s["s_ex3"], b + 1)
                if b >= 1:
                    dve.wait_ge(s["s_pt3"], b)
                at = (CLIP - 1) % 8
                for j in range(TB):
                    last = dve.scalar_tensor_tensor(out=P3[:, j, :], in0=SC[:, j, :], scalar=top3[:, j, at:at + 1],
                                                    in1=EX3[:, j, :], op0=ALU.is_ge, op1=ALU.mult)
                last.then_inc(s["s_p3"], 1)
                dve.wait_ge(s["s_p3"], b + 1)
                link(dve.tensor_reduce(sum2[:], P3, AX.X, ALU.add))
                link(dve.reciprocal(sum2[:], sum2[:]))
                link(dve.tensor_scalar(sum2[:], sum2[:], tg[:, 3:4], None, ALU.mult))
                dve.wait_ge(s["s_y3"], b + 1)
                for j in range(TB):
                    t = TB * b + j
                    last = dve.scalar_tensor_tensor(out=X[:, t, :], in0=bank[6][:, D * j:D * (j + 1)],
                                                    scalar=sum2[:, j:j + 1], in1=X[:, t, :], op0=ALU.mult, op1=ALU.add)
                last.then_inc(s["s_x3"], 1)
                dve.wait_ge(s["s_x3"], b + 1)
            for b in range(B):
                layernorm(7, b)
                dve.wait_ge(s["s_norm"], 7 * B + b + 1)
                quantise_tokens(7, b, 1)
            for t in range(NT):
                q = t % 2
                dve.wait_ge(s["s_gs"], NT + t + 1)
                link(dve.tensor_tensor(H[q], GS[q], GS[q], ALU.mult))
                quantise_hidden(NT + t, 1)
                add_product(NT + t, t)
            dve.engine_nop().then_inc(s["s_x"], 1)

        @block.scalar
        def _(act):
            def turned_copy(u, b):
                act.wait_ge(s["s_turned"], u + 1)
                act.activation(HT[:, :, S * b:S * (b + 1)], bank[u % 2][:].rearrange("p (k n) -> p k n", k=KD),
                               ACT.Copy).then_inc(s["s_ht"], 1)

            landed(act, "g")
            act.activation(tg[:], gates8[:], ACT.Tanh).then_inc(s["s_tanh"], 1)
            for b in range(B):
                turned_copy(b, b)
            for b in range(B):
                q = b % 2
                act.wait_ge(s["s_z"], b + 1)
                if b >= 2:
                    act.wait_ge(s["s_gm"], b - 1)
                act.activation(WK2[:, q, 0:512], bank[2 + q][:], ACT.Silu).then_inc(s["s_silu"], 1)
            for b in range(B):
                turned_copy(B + b, b)
            for b in range(B):
                act.wait_ge(s["s_nmax"], b + 1)
                for j in range(TB):
                    last = act.activation(ex[:, TB * b + j, :], lg[:, j, :], ACT.Exp, bias=nmax[:, j:j + 1])
                last.then_inc(s["s_ex"], 1)
            for i in range(2 * NF):
                act.wait_ge(s["s_hsg"], i + 1)
                if i >= 2:
                    act.wait_ge(s["s_hs"], i - 1)
                act.activation(SSL[:, i % 2, :], bank[2 + i % 2][:], ACT.Silu).then_inc(s["s_ssl"], 1)
            for t in range(ST):
                q = t % 2
                act.wait_ge(s["s_xgturned"], t + 1)
                if t >= 2:
                    act.wait_ge(s["s_egu"], t - 1)
                act.activation(xgT[:, q], bank[q][:, 0:D].rearrange("p (k n) -> p k n", k=KD), ACT.Copy)\
                    .then_inc(s["s_xgT"], 1)
                act.wait_ge(s["s_egu"], t + 1)
                if t >= 2:
                    act.wait_ge(s["s_he"], t - 1)
                act.activation(sil[:, q, :], bank[2 + q][:, 0:P], ACT.Silu).then_inc(s["s_esil"], 1)
                act.wait_ge(s["s_ey"], t + 1)
                if t >= 4:
                    act.wait_ge(s_ys[t % 4], 16 * (t // 4))
                act.activation(ye[:, t % 4, :], bank[4 + q][:, 0:D], ACT.Copy).then_inc(s["s_ye"], 1)
            for b in range(B):
                turned_copy(2 * B + b, b)
            act.wait_ge(s["s_nf"], 1)
            act.activation(e1, nf, ACT.Exp).then_inc(s["s_ln"], 1)
            act.wait_ge(s["s_ln"], 1)
            act.activation(e1, e1, ACT.Ln, bias=1.0).then_inc(s["s_ln"], 1)
            act.wait_ge(s["s_m1"], 1)
            act.activation(nx, Fc, ACT.Exp, scale=-1.0).then_inc(s["s_nx"], 1)
            act.wait_ge(s["s_part"], 1)
            for p in range(3):
                for b in range(B):
                    last = act.activation(CMP[32 * p:32 * (p + 1), b, :], part[32 * b:32 * (b + 1), p, :], ACT.Copy)
            last.then_inc(s["s_cmp"], 1)
            act.wait_ge(s["s_trd"], 1)
            act.activation(ATN[:], bank[6][:].rearrange("p (i n) -> p i n", n=P), ACT.Copy).then_inc(s["s_atn"], 1)
            act.wait_ge(s["s_atn"], 1)

            def heads_copy(b):
                act.wait_ge(s["s_pv"], NH * (b + 1))
                if b >= 1:
                    act.wait_ge(s["s_v16"], b)
                act.activation(HR[:, 0:NH, :], bank[6][:, 0:NH * 17].rearrange("p (h c) -> p h c", c=17), ACT.Copy)
                act.activation(HR[:, NH:2 * NH, :], bank[7][:, 0:NH * 17].rearrange("p (h c) -> p h c", c=17),
                               ACT.Copy).then_inc(s["s_hcp"], 1)

            for i in range(B * NH):
                b, h = i // NH, i % NH
                act.wait_ge(s["s_dq"], i + 1)
                if i >= 2:
                    act.wait_ge(s["s_cs"], i - 1)
                act.activation(dcs[:, i % 2, 0:S], bank[2 + i % 2][:, 0:S], ACT.Exp,
                               bias=ATN[:, 0, 32 * b + h:32 * b + h + 1])
                act.activation(dcs[:, i % 2, S:384], bank[2 + i % 2][:, S:384], ACT.Exp,
                               bias=ATN[:, 1, 32 * b + h:32 * b + h + 1]).then_inc(s["s_dexp"], 1)
                if i >= NH and h == 0:
                    heads_copy(b - 1)
                if i < NQ:
                    landed(act, ("q2g", "q2u", "q2d", "q3a", "q3b")[i])
                    act.activation(QW[:, i, :], RAW[i], ACT.Abs, accum_out=asum[:, i:i + 1]).then_inc(s["s_asum"], 1)
            heads_copy(B - 1)
            for b in range(B):
                turned_copy(3 * B + b, b)
            for b in range(B):
                act.wait_ge(s["s_nm1"], b + 1)
                for j in range(TB):
                    last = act.activation(ex1[:, j, :], lg1[:, j, :], ACT.Exp, bias=nmax1[:, j:j + 1],
                                          accum_out=sum1[:, j:j + 1])
                last.then_inc(s["s_ex1"], 1)
                act.wait_ge(s["s_hmt"], b + 1)
                for h in range(2):
                    last = act.activation(HMT[:, 2 * h:2 * h + 2, :], bank[2 + h][:].rearrange("p (f n) -> p f n", f=2),
                                          ACT.Copy)
                last.then_inc(s["s_hmc"], 1)
            for b in range(B):
                turned_copy(4 * B + b, b)
            for b in range(B):
                act.wait_ge(s["s_qkv"], b + 1)
                act.activation(QT, bank[2][:].rearrange("p (m n) -> p m n", m=KD), ACT.Copy)
                act.activation(KT, bank[3][:].rearrange("p (m n) -> p m n", m=KD), ACT.Copy).then_inc(s["s_qk2"], 1)
                act.wait_ge(s["s_nm2"], b + 1)
                if b >= 1:
                    act.wait_ge(s["s_pt2"], b)
                for j in range(TB):
                    last = act.activation(PR[:, j, :], bank[5 + j][:], ACT.Exp, bias=nmax2[:, j:j + 1],
                                          scale=D ** -0.5, accum_out=sum2[:, j:j + 1])
                last.then_inc(s["s_ex2"], 1)
                act.wait_ge(s["s_pt2"], b + 1)
                for h in range(2):
                    last = act.activation(PT[:, 2 * h:2 * h + 2, :], bank[2 + h][:].rearrange("p (c n) -> p c n", c=2),
                                          ACT.Copy)
                last.then_inc(s["s_ptc2"], 1)
                act.wait_ge(s["s_o2"], b + 1)
                act.activation(OT, bank[4][:].rearrange("p (m n) -> p m n", m=KD), ACT.Copy).then_inc(s["s_oc2"], 1)

            def quantised_copy(u):
                act.wait_ge(s["s_qt"], u + 1)
                if u >= 2:
                    act.wait_ge(s["s_gu"], TB * (u - 1))
                act.activation(XQT[:, u % 2], bank[u % 2][:, 0:S].bitcast(BF16).rearrange("p (k n) -> p k n", k=KD),
                               ACT.Copy).then_inc(s["s_qc"], 1)

            def hidden_copy(v):
                act.wait_ge(s["s_hqt"], v + 1)
                if v >= 2:
                    act.wait_ge(s["s_yq"], v - 1)
                act.activation(HQT[v % 2], bank[6][:].bitcast(BF16).rearrange("p (f n) -> p f n", f=KI), ACT.Copy)\
                    .then_inc(s["s_hqc"], 1)

            for t in range(NT):
                if t % TB == 0:
                    quantised_copy(t // TB)
                act.wait_ge(s["s_gu"], t + 1)
                if t >= 2:
                    act.wait_ge(s["s_qr"], t - 1)
                for n in range(2):
                    last = act.activation(GS[t % 2][:, 512 * n:512 * (n + 1)], bank[2 + n][:], ACT.Silu,
                                          scale=fg[:, t, 0:1])
                last.then_inc(s["s_gs"], 1)
                hidden_copy(t)
            landed(act, "mix")
            act.activation(alpha[:], mix[:, 2:3], ACT.Sigmoid)
            act.activation(mix[:, 3:4], mix[:, 3:4], ACT.Exp).then_inc(s["s_mixe"], 1)
            for b in range(B):
                turned_copy(5 * B + b, b)
            for b in range(B):
                act.wait_ge(s["s_q3"], b + 1)
                act.activation(QT, bank[2][:].rearrange("p (m n) -> p m n", m=KD), ACT.Copy).then_inc(s["s_qc3"], 1)
                act.wait_ge(s["s_m3"], b + 1)
                act.activation(EX3, SC, ACT.Exp).then_inc(s["s_ex3"], 1)
                act.wait_ge(s["s_pt3"], b + 1)
                act.activation(PT3, bank[4][:].rearrange("p (c n) -> p c n", c=2), ACT.Copy).then_inc(s["s_ptc3"], 1)
                act.wait_ge(s["s_o3"], b + 1)
                act.activation(OT, bank[5][:].rearrange("p (m n) -> p m n", m=KD), ACT.Copy).then_inc(s["s_oc3"], 1)
            for t in range(NT):
                v = NT + t
                if t % TB == 0:
                    quantised_copy(B + t // TB)
                act.wait_ge(s["s_gu"], v + 1)
                act.wait_ge(s["s_hq"], v - 1)
                for n in range(2):
                    last = act.activation(GS[t % 2][:, 512 * n:512 * (n + 1)], bank[2 + 2 * (t % 2) + n][:], ACT.Relu,
                                          scale=fg[:, t, 0:1])
                last.then_inc(s["s_gs"], 1)
                hidden_copy(v)

        @block.tensor
        def _(pe):
            def turn(u, b, ln=None):
                pe.wait_ge(s["s_norm"], (u if ln is None else ln) + 1)
                if u >= 2:
                    pe.wait_ge(s["s_ht"], u - 1)
                for k in range(KD):
                    for j in range(TB):
                        last = pe.transpose(bank[u % 2][:, S * k + P * j:S * k + P * (j + 1)],
                                            HN[:, TB * b + j, P * k:P * (k + 1)], identf[:])
                last.then_inc(s["s_turned"], 1)

            pe.wait_ge(s["s_const"], 1)
            for b in range(B):
                turn(b, b)
            landed(pe, "ctxT")
            for b in range(B):
                q = b % 2
                hm = HM[:, q, :].rearrange("p (e k n) -> p e k n", e=E0, k=KD)
                gmk = WK[:, q, :].rearrange("p (e k n) -> p e k n", e=E0, k=KD)
                pe.wait_ge(s["s_hm"], b + 1)
                if b >= 2:
                    pe.wait_ge(s["s_gm"], b - 1)
                for m in range(KD):
                    for e in range(E0):
                        for k in range(KD):
                            last = pe.matmul(bank[2 + q][:, S * m:S * (m + 1)],
                                             CT[:, k, S * e + P * m:S * e + P * (m + 1)], hm[:, e, k, :],
                                             start=(e + k == 0), stop=(e == E0 - 1 and k == KD - 1))
                last.then_inc(s["s_z"], 1)
                pe.wait_ge(s["s_gm"], b + 1)
                for j in range(TB):
                    for e in range(E0):
                        for k in range(KD):
                            last = pe.matmul(bank[4 + q][:, D * j:D * (j + 1)],
                                             gmk[:, e, k, P * j:P * (j + 1)], CT[:, k, S * e:S * (e + 1)],
                                             start=(e + k == 0), stop=(e == E0 - 1 and k == KD - 1))
                last.then_inc(s["s_y0"], 1)
            for b in range(B):
                turn(B + b, b)
            landed(pe, "router")
            for b in range(B):
                pe.wait_ge(s["s_ht"], B + b + 1)
                if b >= 1:
                    pe.wait_ge(s["s_nmax"], b)
                for j in range(TB):
                    for k in range(KD):
                        last = pe.matmul(bank[2][:, E * j:E * (j + 1)], HT[:, k, S * b + P * j:S * b + P * (j + 1)],
                                         RW[:, k, :], start=(k == 0), stop=(k == KD - 1))
                last.then_inc(s["s_lg"], 1)
            for b in range(B):
                pe.wait_ge(s["s_m"], b + 1)
                if b >= 2:
                    pe.wait_ge(s["s_slot"], b - 1)
                for j in range(TB):
                    c = bank[3 + 4 * (b % 2)][:, E * j:E * (j + 1)]
                    pe.matmul(c, before[:], chosen[:, TB * b + j, :], start=True, stop=False)
                    last = pe.matmul(c, onesb[:], earlier[:, TB * b + j, :], start=False, stop=True)
                last.then_inc(s["s_count"], 1)
            pe.wait_ge(s["s_slot"], B)
            landed(pe, "sg")
            landed(pe, "su")
            for c in range(2):
                for f in range(NF):
                    i = NF * c + f
                    if i >= 2:
                        pe.wait_ge(s["s_hs"], i - 1)
                    for w, bk in ((SG, 2), (SU, 4)):
                        for k in range(KD):
                            last = pe.matmul(bank[bk + i % 2][:], w[:, k, P * f:P * (f + 1)],
                                             HT[:, k, 512 * c:512 * (c + 1)], start=(k == 0), stop=(k == KD - 1))
                    last.then_inc(s["s_hsg"], 1)
            landed(pe, "sd")
            for b in range(B):
                pe.wait_ge(s["s_hs"], NF * (b // 2 + 1))
                if b >= 2:
                    pe.wait_ge(s["s_xsh"], b - 1)
                for j in range(TB):
                    for f in range(NF):
                        last = pe.matmul(bank[6 + b % 2][:, D * j:D * (j + 1)],
                                         HS[:, f, S * b + P * j:S * b + P * (j + 1)], SD[:, f, :],
                                         start=(f == 0), stop=(f == NF - 1))
                last.then_inc(s["s_ysh"], 1)
            pe.wait_ge(s["s_const"], 1)
            for t in range(ST):
                q, c, o = t % 2, t // CH, t % CH
                pe.wait_ge(s_xg[t % 4], 16 * (t // 4 + 1))
                if t >= 2:
                    pe.wait_ge(s["s_xgT"], t - 1)
                for k in range(KD):
                    last = pe.transpose(bank[q][:, P * k:P * (k + 1)], xgt[:, t % 4, P * k:P * (k + 1)], identf[:])
                last.then_inc(s["s_xgturned"], 1)
                pe.wait_ge(s["s_xgT"], t + 1)
                if t >= 2:
                    pe.wait_ge(s["s_he"], t - 1)
                if o == 0:
                    pe.wait_ge(s_ew[c % 2], 48 * (c // 2 + 1))
                for w, at in ((egw[c % 2], 0), (euw[c % 2], P)):
                    for i in range(2):
                        for k in range(KD):
                            last = pe.matmul(bank[2 + q][:, at + 64 * i:at + 64 * (i + 1)],
                                             w[:, k, 256 * o + P * i:256 * o + P * (i + 1)],
                                             xgT[:, q, k, 64 * i:64 * (i + 1)], start=(k == 0), stop=(k == KD - 1))
                last.then_inc(s["s_egu"], 1)
                pe.wait_ge(s["s_he"], t + 1)
                if t >= 2:
                    pe.wait_ge(s["s_ye"], t - 1)
                for i in range(2):
                    last = pe.matmul(bank[4 + q][64 * i:64 * (i + 1), 0:D], he[:, q, i, :],
                                     edw[c % 2][:, 2 * o + i, :], start=True, stop=True)
                last.then_inc(s["s_ey"], 1)
            pe.wait_ge(s["s_xgT"], ST)
            for b in range(B):
                turn(2 * B + b, b)
            landed(pe, "wi")
            landed(pe, "wf")
            pe.wait_ge(s["s_ht"], 3 * B)
            for g in range(2):
                for b in range(B):
                    for kt in range(3 * KD):
                        src = HT if kt < KD else CT
                        last = pe.matmul(bank[2 + g][32 * b:32 * (b + 1), 0:S], WIF[:, g, kt, :],
                                         src[:, kt % KD, S * b:S * (b + 1)],
                                         start=(kt == 0), stop=(kt == 3 * KD - 1))
            last.then_inc(s["s_gate"], 1)
            pe.wait_ge(s["s_nx"], 1)
            for j in range(TB):
                pe.transpose(bank[6][:, P * j:P * (j + 1)], ga[:, P * j:P * (j + 1)], identf[:])
                last = pe.transpose(bank[6][:, P * (TB + j):P * (TB + j + 1)], nx[:, P * j:P * (j + 1)], identf[:])
            last.then_inc(s["s_trd"], 1)
            pe.wait_ge(s["s_cmp"], 1)
            pe.wait_ge(s["s_v1"], 1)

            def scores(i):
                b, h = i // NH, i % NH
                kt, r, o = h // 8, h % 2, 32 * (h % 8 // 2)
                if h == 0:
                    pe.wait_ge(s["s_kz"], b + 1)
                if i >= 2:
                    pe.wait_ge(s["s_dexp"], i - 1)
                    pe.wait_ge(s["s_cs"], i - 1)
                dbk, sbk = bank[2 + i % 2], bank[4 + i % 2]
                pe.matmul(dbk[:, 0:384], identb[:], future[:], start=True, stop=False)
                pe.matmul(dbk[:, 0:S], sel[0:96, h, :], CMP[0:96, b, :], start=False, stop=True)
                pe.matmul(dbk[:, S:384], sel[0:96, h, :], CMP[0:96, b, P:S], start=False, stop=True,
                          skip_group_check=True)
                kz = KZ[o:o + 32, b % 2, kt, r, :]
                pe.matmul(sbk[:, 0:S], kz[:, 0:P], HT[o:o + 32, kt, S * b:S * (b + 1)], start=True, stop=True)
                pe.matmul(sbk[:, S:384], kz[:, P:S], HT[o:o + 32, kt, S * b + P:S * (b + 1)], start=True, stop=True)\
                    .then_inc(s["s_dq"], 1)

            def values(i):
                b, h = i // NH, i % NH
                pe.wait_ge(s["s_cs"], i + 1)
                if h == 0:
                    pe.wait_ge(s["s_atn"], 1)
                    if b >= 1:
                        pe.wait_ge(s["s_hcp"], b)
                cs = dcs[:, 2 + i % 2, :]
                pe.matmul(bank[6][:, 17 * h:17 * (h + 1)], cs[:, 0:P], V1[:, TB * b, h, :], start=True, stop=True)
                pe.matmul(bank[7][:, 17 * h:17 * (h + 1)], cs[:, P:S], V1[:, TB * b, h, :], start=True, stop=False)
                pe.matmul(bank[7][:, 17 * h:17 * (h + 1)], cs[:, S:384], V1[:, TB * b + 1, h, :], start=False,
                          stop=True).then_inc(s["s_pv"], 1)

            for i in range(B * NH):
                scores(i)
                if i >= 1:
                    values(i - 1)
                if i == 10:
                    pe.wait_ge(s["s_asum"], NQ)
                    pe.matmul(bank[0][:, 0:NQ], onesf[:], asum[:], start=True, stop=True).then_inc(s["s_wtot"], 1)
            values(B * NH - 1)
            pe.wait_ge(s["s_wsc"], 1)
            for b in range(B):
                turn(3 * B + b, b)
            for n in ("lg", "la", "lb"):
                landed(pe, n)
            pe.wait_ge(s["s_hcp"], B)
            pe.wait_ge(s["s_cs"], B * NH)
            for b in range(B):
                pe.wait_ge(s["s_ht"], 3 * B + b + 1)
                if b >= 1:
                    pe.wait_ge(s["s_hm1"], b)
                for j in range(TB):
                    for k in range(KD):
                        pe.matmul(bank[6][:, E1 * j:E1 * (j + 1)], HT[:, k, S * b + P * j:S * b + P * (j + 1)],
                                  LG[:, k, :], start=(k == 0), stop=(k == KD - 1))
                    for k in range(KD):
                        last = pe.matmul(bank[4 + j][:], HT[:, k, S * b + P * j:S * b + P * (j + 1)],
                                         LA[:, k, :], start=(k == 0), stop=(k == KD - 1))
                last.then_inc(s["s_l1"], 1)
                pe.wait_ge(s["s_hm1"], b + 1)
                if b >= 1:
                    pe.wait_ge(s["s_hmc"], b)
                for j in range(TB):
                    for f in range(4):
                        last = pe.transpose(bank[2 + f // 2][:, S * (f % 2) + P * j:S * (f % 2) + P * (j + 1)],
                                            HM1[:, j, P * f:P * (f + 1)], identf[:])
                last.then_inc(s["s_hmt"], 1)
                pe.wait_ge(s["s_hmc"], b + 1)
                if b >= 1:
                    pe.wait_ge(s["s_xl1"], b)
                for j in range(TB):
                    for f in range(4):
                        last = pe.matmul(bank[7][:, D * j:D * (j + 1)], HMT[:, f, P * j:P * (j + 1)], LB[:, f, :],
                                         start=(f == 0), stop=(f == 3))
                last.then_inc(s["s_y1"], 1)
            for b in range(B):
                turn(4 * B + b, b)
            for n in ("wq", "wk", "wv", "wo"):
                landed(pe, n)
            for b in range(B):
                pe.wait_ge(s["s_ht"], 4 * B + b + 1)
                if b >= 1:
                    pe.wait_ge(s["s_oc2"], b)
                for w in range(2):
                    for m in range(KD):
                        for k in range(KD):
                            pe.matmul(bank[2 + w][:, S * m:S * (m + 1)], W2[:, w, k, P * m:P * (m + 1)],
                                      HT[:, k, S * b:S * (b + 1)], start=(k == 0), stop=(k == KD - 1))
                for j in range(TB):
                    for k in range(KD):
                        last = pe.matmul(bank[4][:, D * j:D * (j + 1)], HT[:, k, S * b + P * j:S * b + P * (j + 1)],
                                         W2[:, 2, k, :], start=(k == 0), stop=(k == KD - 1))
                last.then_inc(s["s_qkv"], 1)
                pe.wait_ge(s["s_qk2"], b + 1)
                for j in range(TB):
                    for half in range(2):
                        for k in range(KD):
                            keys = CT[:, k, S * b:S * (b + 1)] if half == 0 else KT[:, k, :]
                            last = pe.matmul(bank[5 + j][:, S * half:S * (half + 1)], QT[:, k, P * j:P * (j + 1)], keys,
                                             start=(k == 0), stop=(k == KD - 1))
                last.then_inc(s["s_sc2"], 1)
                pe.wait_ge(s["s_ex2"], b + 1)
                for j in range(TB):
                    for c in range(4):
                        last = pe.transpose(bank[2 + c // 2][:, S * (c % 2) + P * j:S * (c % 2) + P * (j + 1)],
                                            PR[:, j, P * c:P * (c + 1)], identf[:])
                last.then_inc(s["s_pt2"], 1)
                pe.wait_ge(s["s_ptc2"], b + 1)
                pe.wait_ge(s["s_v2"], b + 1)
                for m in range(KD):
                    for c in range(4):
                        v = CN[:, TB * b + c, P * m:P * (m + 1)] if c < TB else VN[:, c - TB, P * m:P * (m + 1)]
                        last = pe.matmul(bank[4][:, S * m:S * (m + 1)], v, PT[:, c, :], start=(c == 0), stop=(c == 3))
                last.then_inc(s["s_o2"], 1)
                pe.wait_ge(s["s_oc2"], b + 1)
                if b >= 1:
                    pe.wait_ge(s["s_x2"], b)
                for j in range(TB):
                    for m in range(KD):
                        last = pe.matmul(bank[7][:, D * j:D * (j + 1)], OT[:, m, P * j:P * (j + 1)], W2[:, 3, m, :],
                                         start=(m == 0), stop=(m == KD - 1))
                last.then_inc(s["s_y2"], 1)

            def quantised_turn(u, ln):
                pe.wait_ge(s["s_qn"], u + 1)
                if u >= 2:
                    pe.wait_ge(s["s_qc"], u - 1)
                for k in range(KD):
                    for j in range(TB):
                        o = S * k + P * j
                        last = pe.transpose(bank[u % 2][:, 0:S].bitcast(BF16)[:, o:o + P],
                                            XQ[:, u % B, j, P * k:P * (k + 1)], identb[:])
                last.then_inc(s["s_qt"], 1)

            def product_in(v, w, first):
                j, u = v % TB, v // TB
                for n in range(2):
                    for k in range(KD):
                        last = pe.matmul(bank[first + n][:], XQT[:, u % 2, k, P * j:P * (j + 1)],
                                         QW[:, w, NI * k + 512 * n:NI * k + 512 * (n + 1)],
                                         start=(k == 0), stop=(k == KD - 1))
                return last

            def product_out(v, w):
                pe.wait_ge(s["s_hq"], v + 1)
                if v >= 1:
                    pe.wait_ge(s["s_hqc"], v)
                for f in range(KI):
                    last = pe.transpose(bank[6][:].bitcast(BF16)[:, P * f:P * (f + 1)],
                                        HQ[v % 2][:, P * f:P * (f + 1)], identb[:])
                last.then_inc(s["s_hqt"], 1)
                pe.wait_ge(s["s_hqc"], v + 1)
                if v >= 1:
                    pe.wait_ge(s["s_xq"], v)
                for f in range(KI):
                    last = pe.matmul(bank[7][:, 0:D], HQT[v % 2][:, f, :], QW[:, w, D * f:D * (f + 1)],
                                     start=(f == 0), stop=(f == KI - 1))
                last.then_inc(s["s_yq"], 1)

            pe.wait_ge(s["s_qw"], NQ)
            pe.wait_ge(s["s_x2"], B)
            pe.wait_ge(s["s_oc2"], B)
            for t in range(NT):
                if t % TB == 0:
                    quantised_turn(t // TB, 5)
                    pe.wait_ge(s["s_qc"], t // TB + 1)
                if t >= 1:
                    pe.wait_ge(s["s_qr"], t)
                product_in(t, 0, 2)
                product_in(t, 1, 4).then_inc(s["s_gu"], 1)
                product_out(t, 2)
            for b in range(B):
                turn(5 * B + b, b, ln=6 * B + b)
            landed(pe, "w3q")
            landed(pe, "w3o")
            for b in range(B):
                pe.wait_ge(s["s_ht"], 5 * B + b + 1)
                for m in range(KD):
                    for k in range(KD):
                        last = pe.matmul(bank[2][:, S * m:S * (m + 1)], W3[:, 0, k, P * m:P * (m + 1)],
                                         HT[:, k, S * b:S * (b + 1)], start=(k == 0), stop=(k == KD - 1))
                last.then_inc(s["s_q3"], 1)
                pe.wait_ge(s["s_qc3"], b + 1)
                for j in range(TB):
                    for k in range(KD):
                        last = pe.matmul(bank[3][:, S * j:S * (j + 1)], QT[:, k, P * j:P * (j + 1)],
                                         CT[:, k, S * b:S * (b + 1)], start=(k == 0), stop=(k == KD - 1))
                last.then_inc(s["s_sc3"], 1)
                pe.wait_ge(s["s_p3"], b + 1)
                for j in range(TB):
                    for c in range(TB):
                        last = pe.transpose(bank[4][:, S * c + P * j:S * c + P * (j + 1)],
                                            P3[:, j, P * c:P * (c + 1)], identf[:])
                last.then_inc(s["s_pt3"], 1)
                pe.wait_ge(s["s_ptc3"], b + 1)
                for m in range(KD):
                    for c in range(TB):
                        last = pe.matmul(bank[5][:, S * m:S * (m + 1)], CN[:, TB * b + c, P * m:P * (m + 1)],
                                         PT3[:, c, :], start=(c == 0), stop=(c == TB - 1))
                last.then_inc(s["s_o3"], 1)
                pe.wait_ge(s["s_oc3"], b + 1)
                if b >= 1:
                    pe.wait_ge(s["s_x3"], b)
                for j in range(TB):
                    for m in range(KD):
                        last = pe.matmul(bank[6][:, D * j:D * (j + 1)], OT[:, m, P * j:P * (j + 1)], W3[:, 1, m, :],
                                         start=(m == 0), stop=(m == KD - 1))
                last.then_inc(s["s_y3"], 1)
            pe.wait_ge(s["s_x3"], B)
            for t in range(NT):
                v = NT + t
                if t % TB == 0:
                    quantised_turn(B + t // TB, 7)
                    pe.wait_ge(s["s_qc"], B + t // TB + 1)
                if t >= 2:
                    pe.wait_ge(s["s_gs"], v - 1)
                product_in(v, 3, 2 + 2 * (t % 2)).then_inc(s["s_gu"], 1)
                product_out(v, 4)


def kernel(**inputs):
    import numpy as _np
    import concourse.bacc as _bacc
    from concourse import mybir as _mybir
    from concourse.bass_utils import run_bass_kernel_spmd as _run

    i = {n: _np.asarray(v) for n, v in inputs.items()}
    c = _np.ascontiguousarray

    def turned(w):
        return c(_np.moveaxis(w, -1, 0).reshape(w.shape[-1], -1))

    arrays = {
        "x": i["x"].reshape(N, D), "g": _np.concatenate([i["g_xattn"], i["g_ffn"]]),
        "tok": i["itok_BxS_13_99985"].reshape(N), "ctx": i["ctx_2048"].reshape(N, D), "ctxT": turned(i["ctx_2048"]),
        "router": turned(i["L0_ffn_router_w"]), "router_bias": i["L0_ffn_router_bias"],
        "eg": turned(i["L0_ffn_gate_w"]), "eu": turned(i["L0_ffn_up_w"]),
        "ed": c(i["L0_ffn_down_w"].transpose(0, 2, 1)).reshape(E * F, D),
        "sg": turned(i["L0_ffn_sh_gate_w"]), "su": turned(i["L0_ffn_sh_up_w"]),
        "sd": c(i["L0_ffn_sh_down_w"].transpose(0, 2, 1)).reshape(SF, D),
        "wi": i["L1_xattn_Wi"], "bi": i["L1_xattn_bi"], "wf": i["L1_xattn_Wf"], "bf": i["L1_xattn_bf"],
        "lnsc": i["L1_xattn_ln_scale"],
        "la": turned(i["L1_ffn_A"]), "lb": c(i["L1_ffn_Bw"].transpose(0, 2, 1)).reshape(E1 * R1, D),
        "lg": turned(i["L1_ffn_Wg"]),
        "wq": turned(i["L2_xattn_wq"]), "wk": turned(i["L2_xattn_wk"]), "wv": turned(i["L2_xattn_wv"]),
        "wo": turned(i["L2_xattn_wo"]),
        "q2g": turned(i["L2_ffn_w_gate"]), "q2u": turned(i["L2_ffn_w_up"]), "q2d": turned(i["L2_ffn_w_down"]),
        "w3q": turned(i["L3_xattn_W_qkv"][0:D]), "w3o": turned(i["L3_xattn_W_o"]),
        "mix": _np.stack([i["L3_xattn_beta_q"], i["L3_xattn_beta_k"], i["L3_xattn_gate"], i["L3_xattn_log_tau"]]),
        "q3a": turned(i["L3_ffn_w1"]), "q3b": turned(i["L3_ffn_w2"]),
    }
    nc = _bacc.Bacc("TRN2", target_bir_lowering=False, num_devices=1)
    ins = {n: nc.dram_tensor(f"in_{n}", v.shape, _mybir.dt.from_np(v.dtype), kind="ExternalInput").ap()
           for n, v in arrays.items()}
    out = nc.dram_tensor("out_x", (N, D), F32, kind="ExternalOutput").ap()
    flamingo(nc, ins, out)
    r = _run(nc, [{f"in_{n}": c(v) for n, v in arrays.items()}], core_ids=[0])
    return r.results[0]["out_x"].reshape(B, S, D)
```

```python
from contextlib import ExitStack

import concourse.bass as bass
from concourse import mybir

ALU = mybir.AluOpType
ACT = mybir.ActivationFunctionType
AX = mybir.AxisListType
F32 = mybir.dt.float32
BF16 = mybir.dt.bfloat16
I32 = mybir.dt.int32
U32 = mybir.dt.uint32

P = 128
B, S, D = 4, 256, 256
N = B * S
KD = D // P
TB = S // P
NT = N // P
E0, VOCAB = 4, 12500
PER = VOCAB // E0
E, K, F, CAP = 64, 4, 64, 32
SLOTS = E * CAP
ST = SLOTS // P
EP = P // CAP
SF = 512
NF = SF // P
NH, DH = 16, 16
E1, R1 = 8, 64
NI = 1024
KI = NI // P
CLIP = 54
MAGIC = 12582912.0
FAR = 1048576.0
NEG = -1e30
LOWEST = -3.0e38


def flamingo(nc, a, out):
    ctx = ExitStack()
    with ctx:
        def sb(name, shape, dt=F32):
            return ctx.enter_context(nc.sbuf_tensor(name, shape, dt))

        def sem(name):
            return ctx.enter_context(nc.semaphore(name))

        bank = [ctx.enter_context(nc.psum_tensor(f"bank{i}", [P, 512], F32)) for i in range(8)]

        xg_dram = nc.dram_tensor("xg_rows", [SLOTS, D], F32, kind="Internal").ap()
        y_dram = nc.dram_tensor("y_rows", [SLOTS, D], F32, kind="Internal").ap()

        kp_dram = nc.dram_tensor("key_parts", [3, D, N], BF16, kind="Internal").ap()
        qp_dram = nc.dram_tensor("query_parts", [3, D, N], BF16, kind="Internal").ap()

        def bank_a(b):
            return bank[2 * b]

        def bank_b(b):
            return bank[2 * b + 1]

        def pair(ap, n=TB):
            return ap.rearrange("p (j n) -> p j n", j=n)

        X = sb("X", [P, NT, D])
        HN = sb("HN", [P, NT, D])
        HT = sb("HT", [P, KD, N])
        CN = sb("CN", [P, NT, D])
        CT = sb("CT", [P, KD, N])
        identf = sb("identf", [P, P])
        identb = sb("identb", [P, P], BF16)
        onesf = sb("onesf", [P, P])
        onesb = sb("onesb", [P, P], BF16)
        before = sb("before", [P, P], BF16)
        future = sb("future", [P, 2 * P], BF16)
        neghalf = sb("neghalf", [P, 32])
        magic = sb("magic", [P, 2])
        gates8 = sb("gates8", [P, 8])
        tg = sb("tg", [P, 8])
        bnst = sb("bnst", [P, TB, 6])
        mv = sb("mv", [P, B, TB, 2])
        ve = sb("ve", [P, B, TB])
        rstd = sb("rstd", [P, B, TB])

        ar = sb("ar", [P, 4096])
        HM = sb("HM", [P, 4096])
        big = sb("big", [P, 12288])
        WK = sb("WK", [P, 4096])
        WK2 = sb("WK2", [P, 2048])
        SH = sb("SH", [P, 3072])
        ph = sb("ph", [P, 5120])

        def big_of(b, lo, hi):
            return big[:, 3072 * b + lo:3072 * b + hi]

        tokb = ar[:, 0:N].bitcast(I32)
        ge = ar[:, N:2 * N].bitcast(BF16).rearrange("p (i n) -> p i n", i=2)
        maskb = ar[:, 2 * N:4 * N].bitcast(BF16).rearrange("p (e n) -> p e n", e=E0)
        hm = [HM[:, 2048 * q:2048 * (q + 1)].rearrange("p (e k n) -> p e k n", e=E0, k=KD) for q in range(2)]
        gm = [WK[:, 2048 * q:2048 * (q + 1)].rearrange("p (e k n) -> p e k n", e=E0, k=KD) for q in range(2)]
        gz = [WK2[:, 1024 * q:1024 * q + 512] for q in range(2)]

        SG = pair(SH[:, 0:1024])
        SU = pair(SH[:, 1024:2048])
        SD = pair(SH[:, 2048:3072], NF)
        HS = pair(HM[:], NF)

        RW = sb("RW", [P, KD, E])
        rbias = sb("rbias", [P, E])
        iota64 = sb("iota64", [P, E])
        eoff = sb("eoff", [P, E])
        zer = sb("zer", [P, D])
        lg = sb("lg", [P, TB, E])
        lgb = sb("lgb", [P, TB, E])
        top = sb("top", [P, TB, 8])
        topi = sb("topi", [P, TB, 8], U32)
        pick = sb("pick", [P, TB, K])
        nmax = sb("nmax", [P, TB])
        ex = sb("ex", [P, TB, E])
        oh = ph[:, 0:1024].bitcast(BF16).rearrange("p (t k e) -> p t k e", t=NT, k=K)
        ohx = pair(ph[:, 1024:1536], TB * K)
        chosen = sb("chosen", [P, NT, E], BF16)
        earlier = sb("earlier", [P, NT + 1, E], BF16)
        wk4 = sb("wk4", [P, TB, K])
        wsum = sb("wsum", [P, TB])
        W4 = sb("W4", [P, NT, K])
        val = sb("val", [P, TB, E])
        far = sb("far", [P, TB, E])
        slotf = sb("slotf", [P, TB, K])
        slot = sb("slot", [P, NT, K], U32)
        SSL = pair(ph[:, 1536:2560], 2)
        xgt = pair(ph[:, 2560:3584], 4)
        xgT = ph[:, 3584:4096].rearrange("p (q k n) -> p q k n", q=2, k=KD)
        sil = sb("sil", [P, 2, P])
        he = sb("he", [P, 2, 2, 2 * CAP])
        ye = pair(ph[:, 4096:5120], 4)
        G4 = WK[:, 0:2048].rearrange("p (q k d) -> p q k d", q=2, k=K)
        CH, RING = 2, 4
        NCH = ST // CH
        CW = CH * EP * F
        egw = [pair(big[:, 3072 * q:3072 * q + 1024]) for q in range(RING)]
        euw = [pair(big[:, 3072 * q + 1024:3072 * q + 2048]) for q in range(RING)]
        edw = [pair(big[:, 3072 * q + 2048:3072 * (q + 1)], CH * EP // 2) for q in range(RING)]

        WIF = sb("WIF", [P, 2, 3 * KD, 32])
        bif = sb("bif", [P, 2])
        lns = sb("lns", [P, NH * DH])
        selc = sb("selc", [P, NH], BF16)
        sel = sb("sel", [P, NH, P], BF16)
        rows = pair(WK[:, 2048:4096], 8)
        fgt, nf, e1, lf, Fc, ga, cm, nx = (rows[:, r, :] for r in range(8))
        part = sb("part", [P, 3, S], BF16)
        CMP = sb("CMP", [P, B, S], BF16)
        ATN = sb("ATN", [P, 2 * TB, P])
        V1 = HM[:, 0:NT * NH * 17].rearrange("p (t h c) -> p t h c", t=NT, c=17)
        dcs = pair(HM[:, NT * NH * 17:NT * NH * 17 + 5 * 384], 5)
        PAIRS = [(0, 0), (0, 1), (1, 0), (1, 1), (0, 2), (2, 0), (1, 2), (2, 1)]
        kparts = ar[:, 0:3072].bitcast(BF16).rearrange("p (a k n) -> p a k n", a=3, k=KD)
        krest = pair(WK[:, 0:2048])
        qparts = [ar[:, 2048 + 768 * q:2048 + 768 * (q + 1)].bitcast(BF16).rearrange("p (a k n) -> p a k n", a=3, k=KD)
                  for q in range(2)]
        KST = [m.bitcast(BF16).rearrange("p (h n) -> p h n", h=NH) for m in (WK2[:], big[:, 10240:12288])]
        QST = [m.bitcast(BF16).rearrange("p (h n) -> p h n", h=NH) for m in (SH[:, 0:2048], WK[:, 0:2048])]
        HR = pair(ar[:, 0:TB * NH * 17], TB * NH)
        hhf = ar[:, 544:544 + 512]
        hh = pair(hhf, TB * NH)
        sq = pair(ar[:, 1056:1056 + 512], TB * NH)
        ab = sb("ab", [P, TB * NH])
        mu = sb("mu", [P, TB * NH])
        vr = sb("vr", [P, TB * NH])
        rs = sb("rs", [P, TB * NH])
        FORGET = {1: 1, 2: 12}
        GATHER = (0, 2, 5)
        TURN = (3, 7)
        SPLIT = (6, 17, 19)
        PART = [(0, 32), (32, 64), (64, 128)]

        LA = pair(SH[:, 0:1024])
        LB = pair(SH[:, 1024:2048], 4)
        LG = sb("LG", [P, KD, E1])
        lg1 = sb("lg1", [P, B, TB, E1])
        ex1 = sb("ex1", [P, B, TB, E1])
        top1 = sb("top1", [P, TB, 8])
        topi1 = sb("topi1", [P, TB, 8], U32)
        pick1 = sb("pick1", [P, TB])
        nmax1 = sb("nmax1", [P, B, TB])
        sum1 = sb("sum1", [P, B, TB])
        MK = sb("MK", [P, B, TB, E1])
        HM1 = [pair(WK[:, 1024 * b:1024 * (b + 1)]) for b in range(B)]
        HMT = [pair(big_of(b, 0, 1024), 4) for b in range(B)]

        W2 = ar[:, 2048:4096].rearrange("p (w k d) -> p w k d", w=4, k=KD)
        W3 = SH[:, 2048:3072].rearrange("p (w k d) -> p w k d", w=2, k=KD)
        QT = [pair(big_of(b, 0, 512)) for b in range(B)]
        KT = [pair(big_of(b, 512, 1024)) for b in range(B)]
        VN = [pair(big_of(b, 1024, 1536)) for b in range(B)]
        PR = [pair(big_of(b, 1536, 2560)) for b in range(B)]
        OT = [pair(big_of(b, 2560, 3072)) for b in range(B)]
        PT = [pair(WK[:, 1024 * b:1024 * (b + 1)], 4) for b in range(B)]
        nmax2 = sb("nmax2", [P, B, TB])
        sum2 = sb("sum2", [P, B, TB])
        mix = sb("mix", [P, 4])
        alpha = sb("alpha", [P, 1])
        coef = sb("coef", [P, 1])
        cf2 = sb("cf2", [P, 1])
        SC = KT
        WR = VN
        EX3 = [pair(big_of(b, 1536, 2048)) for b in range(B)]
        P3 = [pair(big_of(b, 2048, 2560)) for b in range(B)]
        top3 = sb("top3", [P, TB, 8])

        NQ = 5
        RAW = [big[:, 2048 * i:2048 * (i + 1)] for i in range(NQ)]
        QW = pair(ph[:].bitcast(BF16), NQ)
        asum = sb("asum", [P, NQ])
        wsc = sb("wsc", [P, NQ])
        wrec = sb("wrec", [P, NQ])
        amax = sb("amax", [P, TB])
        sx = sb("sx", [P, NT])
        rq = sb("rq", [P, TB])
        fg = sb("fg", [P, NT, 2])
        XF = pair(HM[:, 0:512])
        XQ = HM[:, 512:1536].bitcast(BF16).rearrange("p (b j d) -> p b j d", b=B, j=TB)
        XQT = HM[:, 1536:2560].bitcast(BF16).rearrange("p (b k n) -> p b k n", b=B, k=KD)
        am1 = sb("am1", [P, B])
        sh1 = sb("sh1", [P, B])
        rh1 = sb("rh1", [P, B])
        fy1 = sb("fy1", [P, B])
        H = [big_of(b, 0, 1024) for b in range(B)]
        GS = [big_of(b, 1024, 2048) for b in range(B)]
        HQ = [big_of(b, 2048, 2560).bitcast(BF16) for b in range(B)]
        HQT = [pair(big_of(b, 2560, 3072).bitcast(BF16), KI) for b in range(B)]

        names = ("s_vec s_const s_tanh s_lnvar s_lnrstd s_norm s_turned s_ht s_out s_xout "
                 "s_hm s_z s_silu s_gm s_y0 "
                 "s_lg s_nmax s_ex s_m s_count s_slot s_zero s_hsg s_ssl s_hs s_ysh s_xsh s_scat s_xgturned s_xgT "
                 "s_egu s_esil s_he s_ey s_ye s_g0 s_gx "
                 "s_kp s_kst s_qp s_qst s_v1 s_gate s_nf s_e1 s_ln s_m1 s_nx s_part s_cmp s_trd s_atn s_dq s_dexp s_cs s_pv "
                 "s_hcp s_v16 s_r16 s_wif0 "
                 "s_l1 s_nm1 s_ex1 s_ha s_hm1 s_hmt s_hmc s_y1 "
                 "s_qk s_qk2 s_v s_v2 s_sc2 s_nm2 s_ex2 s_pt2 s_ptc2 s_o2 s_oc2 s_y2 "
                 "s_asum s_wtot s_wsc s_wr s_wc s_qw s_mixe "
                 "s_qn s_qt s_qc s_gu s_gs s_hr s_rh s_hm s_hq s_hqt s_hqc s_yq s_xq "
                 "s_q3 s_qc3 s_sc3 s_m3 s_ex3 s_p3 s_pt3 s_ptc3 s_o3 s_oc3 s_y3").split()
        s = {n: sem(n) for n in dict.fromkeys(names)}
        s_hmg = sem("s_hmg")
        s_ptd2 = sem("s_ptd2")
        s_xg = [sem(f"s_xg{i}") for i in range(4)]
        s_ys = [sem(f"s_ys{i}") for i in range(4)]
        s_gat = [sem(f"s_gat{i}") for i in range(2)]
        s_st = [sem(f"s_st{i}") for i in range(2)]
        s_ew = [sem(f"s_ew{i}") for i in range(RING)]

        GROUPS = {"x0": ["x0"], "x1": ["x1"], "x2": ["x2"], "x3": ["x3"], "g": ["g"], "tokb": ["tokb"],
                  "ctxT": ["ctxT"], "ctx": ["ctx"],
                  "router": ["router", "rbias"], "shared": ["sg", "su", "sd"],
                  "small": ["wi", "wf", "lnsc", "mix", "lg"] + [f"{g}{b}" for g in ("bi", "bf") for b in range(B)],
                  "lowrank": ["la", "lb"], "w2": ["wq", "wk", "wv", "wo"], "w3": ["w3q", "w3o"],
                  "q2g": ["q2g"], "q2u": ["q2u"], "q2d": ["q2d"], "q3a": ["q3a"], "q3b": ["q3b"]}
        group_sem = {g: sem("ld_" + g) for g in GROUPS}
        loads = {n: group_sem[g] for g, ns in GROUPS.items() for n in ns}

        def landed(eng, g):
            eng.wait_ge(group_sem[g], 16 * len(GROUPS[g]))

        def rows_of(name, k=P):
            return a[name].rearrange("(k p) c -> p k c", p=k)

        def to_all(name, n):
            return a[name].rearrange("(o n) -> o n", o=1).broadcast_to([P, n])

        xd = a["x"].rearrange("(b j p) d -> b p j d", b=B, j=TB)
        DMAS = [("tokb", tokb, to_all("tok", N)),
                ("x0", X[:, 0:TB, :], xd[0]), ("g", gates8[:], to_all("g", 8)),
                ("x1", X[:, TB:2 * TB, :], xd[1]), ("ctxT", CT[:], rows_of("ctxT")),
                ("x2", X[:, 2 * TB:3 * TB, :], xd[2]), ("x3", X[:, 3 * TB:4 * TB, :], xd[3]),
                ("router", RW[:], rows_of("router")), ("rbias", rbias[:], to_all("router_bias", E)),
                ("sg", SG, rows_of("sg")), ("su", SU, rows_of("su")), ("sd", SD, rows_of("sd")),
                ("ctx", CN[:], rows_of("ctx"))]
        for g, (w, bi) in enumerate((("wi", "bi"), ("wf", "bf"))):
            DMAS.append((w, WIF[:, g, :, 0:NH], rows_of(w)))
            for b in range(B):
                DMAS.append((f"{bi}{b}", bif[32 * b:32 * b + NH, g:g + 1], a[bi].rearrange("(h o) -> h o", o=1)))
        DMAS += [("lnsc", lns[:], to_all("lnsc", D)), ("lg", LG[:], rows_of("lg")), ("mix", mix[:], to_all("mix", 4))]

        block = ctx.enter_context(nc.Block())

        @block.sync
        def _(sp):
            def expert_weights(c):
                q = c % RING
                if c >= RING:
                    sp.wait_ge(s["s_ey"], CH * (c - RING + 1))
                sp.dma_start(egw[q], a["eg"][:, CW * c:CW * (c + 1)].rearrange("(k p) c -> p k c", p=P))\
                    .then_inc(s_ew[q], 16)
                sp.dma_start(euw[q], a["eu"][:, CW * c:CW * (c + 1)].rearrange("(k p) c -> p k c", p=P))\
                    .then_inc(s_ew[q], 16)
                sp.dma_start(edw[q], a["ed"][CW * c:CW * (c + 1), :].rearrange("(i p) d -> p i d", p=P))\
                    .then_inc(s_ew[q], 16)

            def stack(b, dst, parts, which):
                for c, p in enumerate(PAIRS):
                    src = parts[p[which], :, S * b:S * (b + 1)].rearrange("(h d) n -> d h n", d=DH)
                    sp.dma_start(dst[DH * c:DH * (c + 1)], src).then_inc(s_st[b % 2], 16)

            def store_queries(b):
                sp.wait_ge(s["s_qp"], 4 * (b + 1))
                for p in range(3):
                    sp.dma_start(qp_dram[p, :, S * b:S * (b + 1)].rearrange("(k p) n -> p k n", p=P),
                                 qparts[b % 2][:, p]).then_inc(s["s_qst"], 16)
                sp.wait_ge(s["s_qst"], 48 * (b + 1))

            for n, dst, src in DMAS:
                if n == "wi":
                    sp.wait_ge(s["s_wif0"], 1)
                sp.dma_start(dst, src).then_inc(loads[n], 16)
            sp.wait_ge(s["s_const"], 1)
            sp.dma_start(xg_dram.rearrange("(t p) d -> p t d", p=P),
                         zer[:].unsqueeze(1).broadcast_to([P, ST, D])).then_inc(s["s_zero"], 16)
            for c in range(RING):
                expert_weights(c)
            sp.wait_ge(s["s_scat"], 16 * NT * K)
            for t in range(ST + 3):
                if t < ST:
                    if t >= 4:
                        sp.wait_ge(s["s_xgturned"], t - 3)
                    sp.dma_start(xgt[:, t % 4, :], xg_dram[P * t:P * (t + 1), :]).then_inc(s_xg[t % 4], 16)
                    if t == ST // 2:
                        sp.wait_ge(s["s_kp"], 4)
                        for p in range(3):
                            sp.dma_start(kp_dram[p].rearrange("(k p) n -> p k n", p=P), kparts[:, p])\
                                .then_inc(s["s_kst"], 16)
                    if t == ST - 4:
                        sp.wait_ge(s["s_kst"], 48)
                        stack(0, KST[0], kp_dram, 1)
                    if t % CH == CH - 1 and t // CH >= 1 and t // CH + RING - 1 < NCH:
                        expert_weights(t // CH + RING - 1)
                if t >= 3:
                    sp.wait_ge(s["s_ye"], t - 2)
                    sp.dma_start(y_dram[P * (t - 3):P * (t - 2), :], ye[:, (t - 3) % 4, :])\
                        .then_inc(s_ys[(t - 3) % 4], 16)
            sp.wait_ge(s["s_ysh"], B)
            sp.wait_ge(s["s_ey"], ST)
            stack(1, KST[1], kp_dram, 1)
            store_queries(0)
            stack(0, QST[0], qp_dram, 0)
            sp.wait_ge(s["s_gx"], NT)
            store_queries(1)
            stack(1, QST[1], qp_dram, 0)
            for i, n in enumerate(("q2g", "q2u", "q2d", "q3a", "q3b")):
                sp.dma_start(pair(RAW[i], a[n].shape[0] // P), rows_of(n)).then_inc(loads[n], 16)
            for n, dst in (("w3q", W3[:, 0]), ("w3o", W3[:, 1])):
                sp.dma_start(dst, rows_of(n)).then_inc(loads[n], 16)
            for b in range(2, B):
                sp.wait_ge(s["s_dq"], NH * (b - 1))
                stack(b, KST[b % 2], kp_dram, 1)
                store_queries(b)
                stack(b, QST[b % 2], qp_dram, 0)
            for n, dst in (("wq", W2[:, 0]), ("wk", W2[:, 1]), ("wv", W2[:, 2]), ("wo", W2[:, 3])):
                sp.dma_start(dst, rows_of(n)).then_inc(loads[n], 16)
            sp.wait_ge(s["s_dq"], NH * (B - 1))
            for n, dst in (("la", LA), ("lb", LB)):
                sp.dma_start(dst, rows_of(n)).then_inc(loads[n], 16)
            od = out.rearrange("(t p) d -> t p d", p=P)
            for v in range(NT):
                t = TB * (v % B) + v // B
                sp.wait_ge(s["s_xout"], v + 1)
                sp.dma_start(od[t], X[:, t, :]).then_inc(s["s_out"], 16)
            sp.wait_ge(s["s_out"], 16 * NT)

        @block.gpsimd
        def _(pool):
            def ln_rstd(u):
                pool.wait_ge(s["s_lnvar"], u + 1)
                pool.tensor_tensor(rstd[:, u % B, :], ve[:, u % B, :], neghalf[:, 0:TB], ALU.pow)\
                    .then_inc(s["s_lnrstd"], 1)

            def ln_rstds(l):
                for b in range(B):
                    ln_rstd(B * l + b)

            pool.memset(zer[:], 0.0)
            pool.memset(WIF[:], 0.0)
            pool.memset(bif[:], 0.0).then_inc(s["s_wif0"], 1)
            pool.memset(identf[:], 0.0)
            pool.memset(onesf[:], 1.0)
            pool.memset(onesb[:], 1.0)
            pool.memset(future[:], 0.0)
            pool.memset(he[:], 0.0)
            pool.memset(earlier[:, 0, :], 0.0)
            pool.memset(magic[:, 0:1], MAGIC)
            pool.memset(magic[:, 1:2], -MAGIC)
            pool.iota(iota64[:], [[1, E]], base=0, channel_multiplier=0, allow_small_or_imprecise_dtypes=True)
            pool.iota(eoff[:], [[CAP, E]], base=0, channel_multiplier=0, allow_small_or_imprecise_dtypes=True)
            pool.memset(neghalf[:], -0.5).then_inc(s["s_wif0"], 1)
            pool.wait_ge(s["s_wif0"], 2)
            pool.affine_select(out=before[:], in_=onesb[:], compare_op=ALU.is_gt, fill=0.0, base=0,
                               pattern=[[1, P]], channel_multiplier=-1)
            for c in range(2):
                pool.affine_select(out=future[:, P * c:P * (c + 1)], in_=future[:, P * c:P * (c + 1)],
                                   compare_op=ALU.is_ge, fill=NEG, base=0, pattern=[[1, P]], channel_multiplier=-1)
            pool.affine_select(out=identf[:], in_=identf[:], compare_op=ALU.not_equal, fill=1.0, base=0,
                               pattern=[[-1, P]], channel_multiplier=1).then_inc(s["s_wif0"], 1)
            pool.wait_ge(s["s_wif0"], 3)
            pool.tensor_copy(identb[:], identf[:]).then_inc(s["s_const"], 1)
            ln_rstds(0)
            ln_rstds(1)
            pool.wait_ge(s["s_zero"], 16)
            for t in range(NT):
                if t % TB == 0:
                    pool.wait_ge(s["s_slot"], t // TB + 1)
                for k in range(K):
                    pool.indirect_dma_start(out=xg_dram, out_offset=bass.IndirectOffsetOnAxis(slot[:, t, k:k + 1], 0),
                                            in_=HN[:, t, :], in_offset=None, bounds_check=SLOTS - 1,
                                            oob_is_err=False).then_inc(s["s_scat"], 16)
            pool.tensor_copy(kparts[:, 0], CT[:]).then_inc(s["s_kp"], 1)
            pool.wait_ge(s["s_kp"], 1)
            pool.tensor_tensor(krest, CT[:], kparts[:, 0], ALU.subtract).then_inc(s["s_kp"], 1)
            pool.wait_ge(s["s_kp"], 2)
            pool.tensor_copy(kparts[:, 1], krest).then_inc(s["s_kp"], 1)
            pool.wait_ge(s["s_kp"], 3)
            pool.tensor_tensor(kparts[:, 2], krest, kparts[:, 1], ALU.subtract).then_inc(s["s_kp"], 1)
            pool.wait_ge(s["s_kp"], 4)
            pool.memset(G4, 0.0).then_inc(s["s_g0"], 1)
            pool.wait_ge(s["s_ysh"], B)
            landed(pool, "ctx")
            pool.memset(V1[:, :, :, DH:17], 1.0)
            for t in range(NT):
                last = pool.tensor_copy(V1[:, t, :, 0:DH], CN[:, t, :].rearrange("p (h c) -> p h c", c=DH))
            last.then_inc(s["s_v1"], 1)

            for q in range(4):
                pool.wait_ge(s_ys[q], 16 * ST // 4)
            pool.wait_ge(s["s_g0"], 1)
            for t in range(NT):
                q = t % 2
                if t >= 2:
                    pool.wait_ge(s["s_gx"], t - 1)
                for k in range(K):
                    pool.indirect_dma_start(out=G4[:, q, k, :], out_offset=None, in_=y_dram,
                                            in_offset=bass.IndirectOffsetOnAxis(slot[:, t, k:k + 1], 0),
                                            bounds_check=SLOTS - 1, oob_is_err=False).then_inc(s_gat[q], 16)
                if t >= 2 and t % 2 == 0:
                    ln_rstd(2 * B + t // 2 - 1)
            ln_rstd(2 * B + B - 1)

            def weights_clip(i):
                pool.wait_ge(s["s_wr"], i + 1)
                pool.tensor_scalar(RAW[i], RAW[i], MAGIC + 1.0, MAGIC - 1.0, ALU.min, ALU.max)\
                    .then_inc(s["s_wc"], 1)

            for b in range(1, B + 1):
                pool.wait_ge(s["s_v16"], b)
                pool.tensor_tensor(rs[:], vr[:], neghalf[:], ALU.pow).then_inc(s["s_r16"], 1)
                ln_rstd(3 * B + b - 1)
                if b >= 2 and b < B:
                    for i in range(3 * (b - 2), min(3 * (b - 1), NQ)):
                        weights_clip(i)
            for l in range(4, 8):
                ln_rstds(l)

        @block.vector
        def _(dve):
            chain = [0]

            def link(ins):
                chain[0] += 1
                ins.then_inc(s["s_vec"], 1)
                dve.wait_ge(s["s_vec"], chain[0])

            def xb(b):
                return X[:, TB * b:TB * (b + 1), :]

            def ln_stats(l, b):
                for j in range(TB):
                    last = dve.bn_stats(bnst[:, j, :], X[:, TB * b + j, :])
                link(last)
                for j in range(TB):
                    last = dve.bn_aggr(mv[:, b, j, :], bnst[:, j, :])
                link(last)
                dve.tensor_scalar(ve[:, b, :], mv[:, b, :, 1], 1e-5, None, ALU.add).then_inc(s["s_lnvar"], 1)

            def ln_norm(l, b):
                dve.wait_ge(s["s_lnrstd"], B * l + b + 1)
                for j in range(TB):
                    last = dve.tensor_scalar(HN[:, TB * b + j, :], X[:, TB * b + j, :], mv[:, b, j, 0:1],
                                             rstd[:, b, j:j + 1], ALU.subtract, ALU.mult)
                last.then_inc(s["s_norm"], 1)

            landed(dve, "tokb")
            g1, g2 = ge[:, 0, :], ge[:, 1, :]
            dve.tensor_scalar(g1, tokb, float(PER), None, ALU.is_ge)
            dve.tensor_scalar(g2, tokb, float(2 * PER), None, ALU.is_ge)
            link(dve.tensor_scalar(maskb[:, 3, :], tokb, float(3 * PER), None, ALU.is_ge))
            dve.tensor_scalar(maskb[:, 0, :], g1, -1.0, 1.0, ALU.mult, ALU.add)
            dve.tensor_tensor(maskb[:, 1, :], g1, g2, ALU.subtract)
            link(dve.tensor_tensor(maskb[:, 2, :], g2, maskb[:, 3, :], ALU.subtract))
            for b in range(B):
                landed(dve, f"x{b}")
                ln_stats(0, b)
                if b >= 1:
                    ln_norm(0, b - 1)
            ln_norm(0, B - 1)

            def masked(out_, in_, b):
                m = maskb[:, :, S * b:S * (b + 1)].unsqueeze(2).broadcast_to([P, E0, KD, S])
                i = in_.unsqueeze(1).broadcast_to([P, E0, KD, S])
                return dve.tensor_tensor(out_, i, m, ALU.mult)

            def masked_in(b):
                dve.wait_ge(s["s_ht"], b + 1)
                if b >= 2:
                    dve.wait_ge(s["s_z"], b - 1)
                masked(hm[b % 2], HT[:, :, S * b:S * (b + 1)], b).then_inc(s["s_hm"], 1)

            def masked_hidden(b):
                q = b % 2
                dve.wait_ge(s["s_silu"], b + 1)
                link(dve.tensor_tensor(gz[q], gz[q], bank_a(b)[:], ALU.mult))
                if b >= 2:
                    dve.wait_ge(s["s_y0"], b - 1)
                masked(gm[q], pair(gz[q]), b).then_inc(s["s_gm"], 1)

            def add_gated(b, src, g):
                link(dve.scalar_tensor_tensor(out=xb(b), in0=pair(src), scalar=tg[:, g:g + 1], in1=xb(b),
                                              op0=ALU.mult, op1=ALU.add))

            masked_in(0)
            masked_in(1)
            dve.wait_ge(s["s_tanh"], 1)
            for b in range(B + 1):
                if b < B:
                    masked_hidden(b)
                if b + 2 < B:
                    masked_in(b + 2)
                if b >= 1:
                    dve.wait_ge(s["s_y0"], b)
                    add_gated(b - 1, bank_b(b - 1)[:], 0)
                    ln_stats(1, b - 1)
                if b >= 2:
                    ln_norm(1, b - 2)
            ln_norm(1, B - 1)
            dve.wait_ge(s["s_const"], 1)
            link(dve.tensor_tensor(selc[:], identb[:, 0:NH], identb[:, 32:32 + NH], ALU.add))
            link(dve.tensor_tensor(selc[:], selc[:], identb[:, 64:64 + NH], ALU.add))
            dve.tensor_copy(sel[:], selc[:].unsqueeze(2).broadcast_to([P, NH, P]))
            landed(dve, "router")

            def route(b):
                t0, t1 = TB * b, TB * (b + 1)
                dve.wait_ge(s["s_lg"], 1)
                if b >= 1:
                    dve.wait_ge(s["s_ex"], b)
                link(dve.tensor_copy(lg[:], pair(bank[6][:, TB * E * b:TB * E * (b + 1)])))
                dve.tensor_tensor(lgb[:], lg[:], rbias[:].unsqueeze(1).broadcast_to([P, TB, E]), ALU.add)
                link(dve.tensor_reduce(nmax[:], lg[:], AX.X, ALU.max, negate=True))
                for j in range(TB):
                    last = dve.max(top[:, j, :], lgb[:, j, :])
                last.then_inc(s["s_nmax"], 1)
                dve.wait_ge(s["s_nmax"], b + 1)
                for j in range(TB):
                    last = dve.max_index(topi[:, j, :], top[:, j, :], lgb[:, j, :])
                link(last)
                link(dve.tensor_copy(pick[:], topi[:, :, 0:K]))
                for j in range(TB):
                    last = dve.tensor_tensor(oh[:, t0 + j], iota64[:].unsqueeze(1).broadcast_to([P, K, E]),
                                             pick[:, j, :].unsqueeze(2).broadcast_to([P, K, E]), ALU.is_equal)
                link(last)
                with nc.allow_low_precision(reason="sums of at most 4 zeros and ones"):
                    link(dve.tensor_reduce(chosen[:, t0:t1, :], oh[:, t0:t1].rearrange("p j k e -> p j e k"),
                                           AX.X, ALU.add))
                link(dve.tensor_tensor(earlier[:, t0 + 1, :], earlier[:, t0, :], chosen[:, t0, :], ALU.add))
                dve.tensor_tensor(earlier[:, t0 + 2, :], earlier[:, t0 + 1, :], chosen[:, t0 + 1, :], ALU.add)\
                    .then_inc(s["s_m"], 1)
                dve.wait_ge(s["s_ex"], b + 1)
                for j in range(TB):
                    last = dve.tensor_tensor(ohx[:, K * j:K * (j + 1), :], oh[:, t0 + j],
                                             ex[:, j, :].unsqueeze(1).broadcast_to([P, K, E]), ALU.mult)
                link(last)
                link(dve.tensor_reduce(wk4[:].rearrange("p j k -> p (j k)"), ohx, AX.X, ALU.add))
                link(dve.tensor_reduce(wsum[:], wk4[:], AX.X, ALU.add))
                link(dve.reciprocal(wsum[:], wsum[:]))
                for j in range(TB):
                    last = dve.tensor_scalar(W4[:, t0 + j, :], wk4[:, j, :], wsum[:, j:j + 1], tg[:, 4:5],
                                             ALU.mult, ALU.mult)
                link(last)
                dve.wait_ge(s["s_m"], b + 1)

            def places(b):
                t0, t1 = TB * b, TB * (b + 1)
                dve.wait_ge(s["s_count"], b + 1)
                cnt = pair(bank[7][:, 0:TB * E])
                dve.tensor_scalar(far[:], cnt, float(CAP), FAR, ALU.is_ge, ALU.mult)
                link(dve.tensor_tensor(val[:], cnt, eoff[:].unsqueeze(1).broadcast_to([P, TB, E]), ALU.add))
                link(dve.tensor_tensor(val[:], val[:], far[:], ALU.add))
                for j in range(TB):
                    last = dve.tensor_tensor(ohx[:, K * j:K * (j + 1), :], oh[:, t0 + j],
                                             val[:, j, :].unsqueeze(1).broadcast_to([P, K, E]), ALU.mult)
                link(last)
                link(dve.tensor_reduce(slotf[:].rearrange("p j k -> p (j k)"), ohx, AX.X, ALU.add))
                dve.tensor_copy(slot[:, t0:t1, :], slotf[:]).then_inc(s["s_slot"], 1)
                link(dve.scalar_tensor_tensor(out=W4[:, t0:t1, :], in0=slotf[:], scalar=float(SLOTS),
                                              in1=W4[:, t0:t1, :], op0=ALU.is_lt, op1=ALU.mult))

            def shared_hidden(i):
                c, f, q = i // NF, i % NF, i % 3
                dve.wait_ge(s["s_ssl"], i + 1)
                dve.tensor_tensor(HS[:, f, 512 * c:512 * (c + 1)], SSL[:, i % 2, :], bank[3 + q][:],
                                  ALU.mult).then_inc(s["s_hs"], 1)

            route(0)
            shared_hidden(0)
            route(1)
            shared_hidden(1)
            places(0)
            route(2)
            shared_hidden(2)
            places(1)
            route(3)
            shared_hidden(3)
            places(2)
            shared_hidden(4)
            places(3)
            for i in range(5, 2 * NF):
                shared_hidden(i)
            for b in range(B):
                dve.wait_ge(s["s_ysh"], b + 1)
                add_gated(b, bank[6 + b % 2][:], 4)
                dve.tensor_copy(nmax[:, 0:1], tg[:, 0:1]).then_inc(s["s_xsh"], 1)
            for t in range(ST):
                q = t % 2
                dve.wait_ge(s["s_esil"], t + 1)
                if t >= 2:
                    dve.wait_ge(s["s_ey"], t - 1)
                for h in range(2):
                    r = slice(F * h, F * (h + 1))
                    cols = slice(CAP * h, CAP * (h + 1))
                    last = dve.tensor_tensor(he[r, q, :, cols], pair(sil[:, q, :])[r, :, cols],
                                             pair(bank[2 + q][:, P:2 * P])[r, :, cols], ALU.mult)
                last.then_inc(s["s_he"], 1)

            def gathered(t):
                dve.wait_ge(s_gat[t % 2], 16 * K * (t // 2 + 1))
                for k in range(K):
                    last = dve.scalar_tensor_tensor(out=X[:, t, :], in0=G4[:, t % 2, k, :], scalar=W4[:, t, k:k + 1],
                                                    in1=X[:, t, :], op0=ALU.mult, op1=ALU.add)
                    if k < K - 1:
                        link(last)
                last.then_inc(s["s_gx"], 1)
                dve.wait_ge(s["s_gx"], t + 1)

            def forget_rows(r):
                p0, p1 = PART[r]
                dve.wait_ge(s["s_gate"], (1, 2, 4)[r])
                link(dve.tensor_scalar(fgt[p0:p1], bank[1][p0:p1, S:2 * S], bif[p0:p1, 1:2], None, ALU.add))
                dve.scalar_tensor_tensor(out=nf[p0:p1], in0=fgt[p0:p1], scalar=-1.0, in1=fgt[p0:p1],
                                         op0=ALU.mult, op1=ALU.min).then_inc(s["s_nf"], 1)

            def sum_rows(r):
                p0, p1 = PART[r]
                dve.wait_ge(s["s_ln"], r + 1)
                link(dve.scalar_tensor_tensor(out=lf[p0:p1], in0=fgt[p0:p1], scalar=0.0, in1=e1[p0:p1],
                                              op0=ALU.min, op1=ALU.subtract))
                link(dve.tensor_tensor_scan(Fc[p0:p1], lf[p0:p1], zer[p0:p1], 0.0, ALU.add, ALU.add))

            def max_rows(r):
                p0, p1 = PART[r]
                link(dve.scalar_tensor_tensor(out=ga[p0:p1], in0=bank[1][p0:p1, 0:S], scalar=bif[p0:p1, 0:1],
                                              in1=Fc[p0:p1], op0=ALU.add, op1=ALU.subtract))
                link(dve.tensor_tensor_scan(cm[p0:p1], ga[p0:p1], ga[p0:p1], LOWEST, ALU.max, ALU.max))
                dve.tensor_tensor(Fc[p0:p1], Fc[p0:p1], cm[p0:p1], ALU.add).then_inc(s["s_m1"], 1)

            def part_rows(r):
                p0, p1 = PART[r]
                link(dve.tensor_scalar(part[p0:p1, 0, :], cm[p0:p1], -1.0, None, ALU.mult))
                link(dve.scalar_tensor_tensor(out=lf[p0:p1], in0=cm[p0:p1], scalar=-1.0, in1=part[p0:p1, 0, :],
                                              op0=ALU.mult, op1=ALU.subtract))
                link(dve.tensor_copy(part[p0:p1, 1, :], lf[p0:p1]))
                link(dve.tensor_tensor(lf[p0:p1], lf[p0:p1], part[p0:p1, 1, :], ALU.subtract))
                dve.tensor_copy(part[p0:p1, 2, :], lf[p0:p1]).then_inc(s["s_part"], 1)

            def part_queries(b):
                q, h, rest = qparts[b % 2], HT[:, :, S * b:S * (b + 1)], HN[:, TB * b:TB * (b + 1), :]
                dve.wait_ge(s["s_ht"], 2 * B + b + 1)
                if b == 0:
                    dve.wait_ge(s["s_kst"], 48)
                if b >= 2:
                    dve.wait_ge(s["s_qst"], 48 * (b - 1))
                for n, (out_, in0, in1) in enumerate(((q[:, 0], h, None), (rest, h, q[:, 0]), (q[:, 1], rest, None),
                                                      (q[:, 2], rest, q[:, 1]))):
                    if n >= 1:
                        dve.wait_ge(s["s_qp"], 4 * b + n)
                    if in1 is None:
                        dve.tensor_copy(out_, in0).then_inc(s["s_qp"], 1)
                    else:
                        dve.tensor_tensor(out_, in0, in1, ALU.subtract).then_inc(s["s_qp"], 1)

            landed(dve, "small")
            link(dve.tensor_scalar(lns[:], lns[:], tg[:, 1:2], None, ALU.mult))
            gathered(0)
            gathered(1)
            ln_stats(2, 0)
            gathered(2)
            ln_norm(2, 0)
            gathered(3)
            ln_stats(2, 1)
            forget_rows(0)
            part_queries(0)
            ln_norm(2, 1)
            sum_rows(0)
            max_rows(0)
            part_rows(0)
            gathered(4)

            def heads_norm(b, step):
                wide = ab[:].unsqueeze(2).broadcast_to([P, TB * NH, DH])
                if step == 0:
                    dve.wait_ge(s["s_hcp"], b + 1)
                    sums = HR[:, :, DH]
                    link(dve.scalar_tensor_tensor(out=ab[:], in0=sums, scalar=-1.0, in1=sums, op0=ALU.mult,
                                                  op1=ALU.max))
                    link(dve.tensor_tensor(pair(ab[:]), pair(ab[:]), ATN[:, TB:2 * TB, 32 * b:32 * b + NH], ALU.max))
                    link(dve.tensor_scalar(ab[:], ab[:], 1e-6, None, ALU.add))
                    link(dve.reciprocal(ab[:], ab[:]))
                elif step == 1:
                    link(dve.tensor_tensor(hh, HR[:, :, 0:DH], wide, ALU.mult))
                    link(dve.tensor_reduce(mu[:], hh, AX.X, ALU.add))
                    link(dve.tensor_scalar(mu[:], mu[:], 1.0 / DH, None, ALU.mult))
                elif step == 2:
                    link(dve.tensor_tensor(hh, hh, mu[:].unsqueeze(2).broadcast_to([P, TB * NH, DH]), ALU.subtract))
                    link(dve.tensor_tensor(sq, hh, hh, ALU.mult))
                elif step == 3:
                    link(dve.tensor_reduce(vr[:], sq, AX.X, ALU.add))
                    dve.tensor_scalar(vr[:], vr[:], 1.0 / DH, 1e-6, ALU.mult, ALU.add).then_inc(s["s_v16"], 1)
                elif step == 4:
                    dve.wait_ge(s["s_r16"], b + 1)
                    link(dve.tensor_tensor(hh, hh, rs[:].unsqueeze(2).broadcast_to([P, TB * NH, DH]), ALU.mult))
                    link(dve.tensor_tensor(pair(hhf), pair(hhf), lns[:].unsqueeze(1).broadcast_to([P, TB, D]), ALU.mult))
                elif step == 5:
                    link(dve.tensor_tensor(xb(b), xb(b), pair(hhf), ALU.add))
                    ln_stats(3, b)
                elif step == 6:
                    ln_norm(3, b)

            for i in range(B * NH):
                b, h = i // NH, i % NH
                dve.wait_ge(s["s_dexp"], i + 1)
                if i >= 3:
                    dve.wait_ge(s["s_pv"], i - 2)
                dve.scalar_tensor_tensor(out=dcs[:, 2 + i % 3, :], in0=bank[4 + i % 2][:, 0:384], scalar=DH ** -0.5,
                                         in1=dcs[:, i % 2, :], op0=ALU.mult, op1=ALU.mult).then_inc(s["s_cs"], 1)
                for r in (1, 2):
                    if i == FORGET[r]:
                        forget_rows(r)
                    if i == FORGET[r] + 2:
                        sum_rows(r)
                    if i == FORGET[r] + 3:
                        max_rows(r)
                    if i == FORGET[r] + 4:
                        part_rows(r)
                if i in GATHER:
                    gathered(5 + GATHER.index(i))
                    if i != GATHER[1]:
                        ln_stats(2, 2 + GATHER.index(i) // 2)
                if i in TURN:
                    ln_norm(2, 2 + TURN.index(i))
                if i in SPLIT:
                    part_queries(1 + SPLIT.index(i))
                if b == 0:
                    pass
                elif 4 <= h < 8:
                    heads_norm(b - 1, h - 4)
                elif 10 <= h < 12:
                    heads_norm(b - 1, h - 6)
                elif h == 13:
                    heads_norm(b - 1, 6)
                if i == NH + 9:
                    dve.wait_ge(s["s_wtot"], 1)
                    link(dve.tensor_scalar(wsc[:], bank[0][:, 0:NQ], 1.0 / (NI * D), 1e-5, ALU.mult, ALU.add))
                    dve.reciprocal(wrec[:], wsc[:]).then_inc(s["s_wsc"], 1)
            for step in range(7):
                heads_norm(B - 1, step)

            for b in range(B):
                dve.wait_ge(s["s_l1"], b + 1)
                link(dve.tensor_copy(lg1[:, b], pair(bank_a(b)[:, 0:TB * E1])))
                dve.tensor_reduce(nmax1[:, b], lg1[:, b], AX.X, ALU.max, negate=True)
                for j in range(TB):
                    last = dve.max(top1[:, j, :], lg1[:, b, j, :])
                last.then_inc(s["s_nm1"], 1)
                dve.wait_ge(s["s_nm1"], b + 1)
                for j in range(TB):
                    last = dve.max_index(topi1[:, j, :], top1[:, j, :], lg1[:, b, j, :])
                link(last)
                link(dve.tensor_copy(pick1[:], topi1[:, :, 0]))
                link(dve.tensor_tensor(MK[:, b], iota64[:, 0:E1].unsqueeze(1).broadcast_to([P, TB, E1]),
                                       pick1[:].unsqueeze(2).broadcast_to([P, TB, E1]), ALU.is_equal))
            for b in range(B):
                dve.wait_ge(s["s_ex1"], b + 1)
                link(dve.reciprocal(sum1[:, b], sum1[:, b]))
                link(dve.tensor_scalar(sum1[:, b], sum1[:, b], 64.0 / 16.0, tg[:, 5:6], ALU.mult, ALU.mult))
                link(dve.tensor_tensor(MK[:, b], MK[:, b], sum1[:, b].unsqueeze(2).broadcast_to([P, TB, E1]), ALU.mult))
                dve.wait_ge(s["s_ha"], b + 1)
                for j in range(TB):
                    last = dve.tensor_tensor(pair(HM1[b][:, j, :], E1), pair(bank[2 * b + j][:], E1),
                                             MK[:, b, j, :].unsqueeze(2).broadcast_to([P, E1, R1]), ALU.mult)
                last.then_inc(s["s_hm1"], 1)
            for b in range(B):
                dve.wait_ge(s["s_y1"], b + 1)
                link(dve.tensor_tensor(xb(b), xb(b), pair(bank_a(b)[:]), ALU.add))
                ln_stats(4, b)
                if b >= 1:
                    ln_norm(4, b - 1)
            ln_norm(4, B - 1)

            def add_scaled(b, src):
                for j in range(TB):
                    t = TB * b + j
                    last = dve.scalar_tensor_tensor(out=X[:, t, :], in0=src[:, D * j:D * (j + 1)],
                                                    scalar=sum2[:, b, j:j + 1], in1=X[:, t, :], op0=ALU.mult,
                                                    op1=ALU.add)
                link(last)

            for b in range(B):
                dve.wait_ge(s["s_v"], b + 1)
                dve.tensor_copy(VN[b], pair(bank_a(b)[:])).then_inc(s["s_v2"], 1)
            for b in range(B):
                dve.wait_ge(s["s_sc2"], b + 1)
                for j in range(TB):
                    last = dve.tensor_reduce(nmax2[:, b, j:j + 1], bank[2 * b + j][:], AX.X, ALU.max, negate=True)
                link(last)
                dve.tensor_scalar(nmax2[:, b], nmax2[:, b], D ** -0.5, None, ALU.mult).then_inc(s["s_nm2"], 1)
            for b in range(B):
                dve.wait_ge(s["s_pt2"], b + 1)
                dve.tensor_copy(PT[b][:, TB:2 * TB, :], pair(bank_b(b)[:])).then_inc(s_ptd2, 1)
            for b in range(B):
                link(dve.reciprocal(sum2[:, b], sum2[:, b]))
                link(dve.tensor_scalar(sum2[:, b], sum2[:, b], tg[:, 2:3], None, ALU.mult))
                dve.wait_ge(s["s_y2"], b + 1)
                add_scaled(b, bank_b(b))
                ln_stats(5, b)
                if b >= 1:
                    ln_norm(5, b - 1)
            ln_norm(5, B - 1)

            def quantise_tokens(b, f):
                t0, t1 = TB * b, TB * (b + 1)
                link(dve.tensor_reduce(amax[:], HN[:, t0:t1, :], AX.X, ALU.max, apply_absolute_value=True))
                if f == 0:
                    link(dve.tensor_scalar(sx[:, t0:t1], amax[:], 1.0 / 127.0, 1e-5, ALU.mult, ALU.add))
                else:
                    link(dve.tensor_scalar(sx[:, t0:t1], amax[:], 1e-5, 1.0 / 127.0, ALU.max, ALU.mult))
                link(dve.reciprocal(rq[:], sx[:, t0:t1]))
                for w in range(2 - f):
                    dve.tensor_scalar(fg[:, t0:t1, w], sx[:, t0:t1], wsc[:, 3 * f + w:3 * f + w + 1], None, ALU.mult)
                for j in range(TB):
                    last = dve.tensor_scalar(XF[:, j, :], HN[:, t0 + j, :], rq[:, j:j + 1], MAGIC, ALU.mult, ALU.add)
                link(last)
                dve.tensor_scalar(XQ[:, b], XF, -MAGIC, None, ALU.add).then_inc(s["s_qn"], 1)

            def hidden_scale(v, f):
                b = v % B
                w = slice(b, b + 1)
                link(dve.tensor_reduce(am1[:, w], H[b], AX.X, ALU.max, apply_absolute_value=True))
                if f == 0:
                    link(dve.tensor_scalar(sh1[:, w], am1[:, w], 1.0 / 127.0, 1e-5, ALU.mult, ALU.add))
                else:
                    link(dve.tensor_scalar(sh1[:, w], am1[:, w], 1e-5, 1.0 / 127.0, ALU.max, ALU.mult))
                dve.reciprocal(rh1[:, w], sh1[:, w]).then_inc(s["s_rh"], 1)
                link(dve.tensor_scalar(fy1[:, w], sh1[:, w], wsc[:, 2 + 2 * f:3 + 2 * f], tg[:, 6 + f:7 + f],
                                       ALU.mult, ALU.mult))

            def hidden_integers(v):
                b = v % B
                dve.wait_ge(s["s_hr"], v + 1)
                dve.tensor_scalar(HQ[b], H[b], -MAGIC, None, ALU.add).then_inc(s["s_hq"], 1)

            def add_product(v):
                b, t = v % B, TB * (v % B) + v % NT // B
                dve.wait_ge(s["s_yq"], v + 1)
                last = dve.scalar_tensor_tensor(out=X[:, t, :], in0=bank_b(b)[:, 0:D], scalar=fy1[:, b:b + 1],
                                                in1=X[:, t, :], op0=ALU.mult, op1=ALU.add)
                if v >= NT:
                    last.then_inc(s["s_xout"], 1)
                else:
                    last.then_inc(s["s_xq"], 1)
                    dve.wait_ge(s["s_xq"], v + 1)

            for b in range(B):
                dve.wait_ge(s["s_norm"], 5 * B + b + 1)
                quantise_tokens(b, 0)
            for j in range(TB):
                for n in range(2):
                    for b in range(B):
                        g = B * (2 * j + n) + b
                        dve.wait_ge(s["s_gs"], g + 1)
                        last = dve.scalar_tensor_tensor(out=H[b][:, 512 * n:512 * (n + 1)], in0=bank_b(b)[:],
                                                        scalar=fg[:, TB * b + j, 1:2],
                                                        in1=GS[b][:, 512 * n:512 * (n + 1)], op0=ALU.mult, op1=ALU.mult)
                        last.then_inc(s_hmg, 1)
                        if n == 1:
                            dve.wait_ge(s_hmg, g + 1)
                            hidden_scale(B * j + b, 0)
                for b in range(B):
                    hidden_integers(B * j + b)
                for b in range(B):
                    add_product(B * j + b)
                    if j == TB - 1:
                        ln_stats(6, b)
                        if b >= 1:
                            ln_norm(6, b - 1)
            ln_norm(6, B - 1)
            dve.wait_ge(s["s_mixe"], 1)
            link(dve.tensor_scalar(coef[:], alpha[:], mix[:, 0:1], None, ALU.mult))
            link(dve.tensor_scalar(cf2[:], alpha[:], -1.0, 1.0, ALU.mult, ALU.add))
            link(dve.scalar_tensor_tensor(out=coef[:], in0=cf2[:], scalar=mix[:, 1:2], in1=coef[:],
                                          op0=ALU.mult, op1=ALU.add))
            link(dve.tensor_scalar(coef[:], coef[:], D ** -0.5, mix[:, 3:4], ALU.mult, ALU.mult))
            for b in range(B):
                dve.wait_ge(s["s_sc3"], b + 1)
                link(dve.tensor_scalar(SC[b], pair(bank_a(b)[:]), coef[:], None, ALU.mult))
                link(dve.tensor_reduce(nmax2[:, b], SC[b], AX.X, ALU.max, negate=True))
                for j in range(TB):
                    last = dve.tensor_scalar(SC[b][:, j, :], SC[b][:, j, :], nmax2[:, b, j:j + 1], None, ALU.add)
                last.then_inc(s["s_m3"], 1)
                dve.wait_ge(s["s_m3"], b + 1)
                for r in range((CLIP + 7) // 8):
                    src = SC[b] if r == 0 else WR[b]
                    for j in range(TB):
                        last = dve.max(top3[:, j, :], src[:, j, :])
                    link(last)
                    if 8 * (r + 1) < CLIP:
                        for j in range(TB):
                            last = dve.match_replace(WR[b][:, j, :], top3[:, j, :], src[:, j, :], LOWEST)
                        link(last)
                dve.wait_ge(s["s_ex3"], b + 1)
                at = (CLIP - 1) % 8
                for j in range(TB):
                    last = dve.scalar_tensor_tensor(out=P3[b][:, j, :], in0=SC[b][:, j, :],
                                                    scalar=top3[:, j, at:at + 1], in1=EX3[b][:, j, :],
                                                    op0=ALU.is_ge, op1=ALU.mult)
                last.then_inc(s["s_p3"], 1)
                dve.wait_ge(s["s_p3"], b + 1)
                link(dve.tensor_reduce(sum2[:, b], P3[b], AX.X, ALU.add))
                link(dve.reciprocal(sum2[:, b], sum2[:, b]))
                link(dve.tensor_scalar(sum2[:, b], sum2[:, b], tg[:, 3:4], None, ALU.mult))
            for b in range(B):
                dve.wait_ge(s["s_y3"], b + 1)
                add_scaled(b, bank_b(b))
                ln_stats(7, b)
                if b >= 1:
                    ln_norm(7, b - 1)
            ln_norm(7, B - 1)
            for b in range(B):
                dve.wait_ge(s["s_norm"], 7 * B + b + 1)
                quantise_tokens(b, 1)
            for j in range(TB):
                for b in range(B):
                    v = NT + B * j + b
                    dve.wait_ge(s["s_gs"], 2 * NT + B * j + b + 1)
                    link(dve.tensor_tensor(H[b], GS[b], GS[b], ALU.mult))
                    hidden_scale(v, 1)
                for b in range(B):
                    hidden_integers(NT + B * j + b)
                for b in range(B):
                    add_product(NT + B * j + b)

        @block.scalar
        def _(act):
            def turned_copy(u, src):
                b = u % B
                act.wait_ge(s["s_turned"], u + 1)
                act.activation(HT[:, :, S * b:S * (b + 1)], pair(src[:]), ACT.Copy).then_inc(s["s_ht"], 1)

            landed(act, "g")
            act.activation(tg[:], gates8[:], ACT.Tanh).then_inc(s["s_tanh"], 1)
            for b in range(B):
                turned_copy(b, bank_a(b))
            for b in range(B):
                q = b % 2
                act.wait_ge(s["s_z"], b + 1)
                if b >= 2:
                    act.wait_ge(s["s_gm"], b - 1)
                act.activation(gz[q], bank_a(b)[:], ACT.Silu).then_inc(s["s_silu"], 1)
            for b in range(B):
                turned_copy(B + b, bank[b])

            def route_exp(b):
                act.wait_ge(s["s_nmax"], b + 1)
                for j in range(TB):
                    last = act.activation(ex[:, j, :], lg[:, j, :], ACT.Exp, bias=nmax[:, j:j + 1])
                last.then_inc(s["s_ex"], 1)

            def shared_silu(i):
                act.wait_ge(s["s_hsg"], i + 1)
                if i >= 2:
                    act.wait_ge(s["s_hs"], i - 1)
                act.activation(SSL[:, i % 2, :], bank[i % 3][:], ACT.Silu).then_inc(s["s_ssl"], 1)

            for b in range(B):
                route_exp(b)
                shared_silu(b)
            for i in range(B, 2 * NF):
                shared_silu(i)
            for t in range(ST + 2):
                if t < ST:
                    q = t % 2
                    act.wait_ge(s["s_xgturned"], t + 1)
                    if t >= 2:
                        act.wait_ge(s["s_egu"], t - 1)
                    act.activation(xgT[:, q], pair(bank[q][:, 0:D]), ACT.Copy).then_inc(s["s_xgT"], 1)
                if 1 <= t <= ST:
                    q = (t - 1) % 2
                    act.wait_ge(s["s_egu"], t)
                    if t >= 3:
                        act.wait_ge(s["s_he"], t - 2)
                    act.activation(sil[:, q, :], bank[2 + q][:, 0:P], ACT.Silu).then_inc(s["s_esil"], 1)
                if t >= 2:
                    r = t - 2
                    act.wait_ge(s["s_ey"], r + 1)
                    if r >= 4:
                        act.wait_ge(s_ys[r % 4], 16 * (r // 4))
                    act.activation(ye[:, r % 4, :], bank[4 + r % 2][:, 0:D], ACT.Copy).then_inc(s["s_ye"], 1)

            def log_rows(r):
                p0, p1 = PART[r]
                act.wait_ge(s["s_nf"], r + 1)
                act.activation(e1[p0:p1], nf[p0:p1], ACT.Exp).then_inc(s["s_e1"], 1)
                act.wait_ge(s["s_e1"], r + 1)
                act.activation(e1[p0:p1], e1[p0:p1], ACT.Ln, bias=1.0).then_inc(s["s_ln"], 1)

            def spread_rows(r):
                p0, p1 = PART[r]
                act.wait_ge(s["s_m1"], r + 1)
                act.activation(nx[p0:p1], Fc[p0:p1], ACT.Exp, scale=-1.0).then_inc(s["s_nx"], 1)
                act.wait_ge(s["s_part"], r + 1)
                for p in range(3):
                    for b in range(p0 // 32, p1 // 32):
                        last = act.activation(CMP[32 * p:32 * (p + 1), b, :], part[32 * b:32 * (b + 1), p, :],
                                              ACT.Copy)
                last.then_inc(s["s_cmp"], 1)

            def turned_rows(r):
                p0, p1 = PART[r]
                act.wait_ge(s["s_trd"], r + 1)
                act.activation(ATN[:, :, p0:p1], pair(bank[0][:], 4)[:, :, 0:p1 - p0], ACT.Copy)\
                    .then_inc(s["s_atn"], 1)

            turned_copy(2 * B, bank[0])
            log_rows(0)
            turned_copy(2 * B + 1, bank[0])
            spread_rows(0)
            turned_rows(0)
            act.wait_ge(s["s_atn"], 1)

            def heads_copy(b):
                act.wait_ge(s["s_pv"], NH * (b + 1))
                act.activation(HR[:, 0:NH, :], pair(bank[6][:, 0:NH * 17], NH), ACT.Copy)
                act.activation(HR[:, NH:2 * NH, :], pair(bank[7][:, 0:NH * 17], NH), ACT.Copy)\
                    .then_inc(s["s_hcp"], 1)

            for i in range(B * NH):
                b, h = i // NH, i % NH
                act.wait_ge(s["s_dq"], i + 1)
                if h == 0 and b >= 1:
                    act.wait_ge(s["s_atn"], (2, 3, 3)[b - 1])
                if i >= 2:
                    act.wait_ge(s["s_cs"], i - 1)
                act.activation(dcs[:, i % 2, 0:S], bank[2 + i % 2][:, 0:S], ACT.Exp,
                               bias=ATN[:, 0, 32 * b + h:32 * b + h + 1])
                act.activation(dcs[:, i % 2, S:384], bank[2 + i % 2][:, S:384], ACT.Exp,
                               bias=ATN[:, 1, 32 * b + h:32 * b + h + 1]).then_inc(s["s_dexp"], 1)
                if i >= NH and h == 2:
                    heads_copy(b - 1)
                for r in (1, 2):
                    if i == FORGET[r] + 1:
                        log_rows(r)
                    if i == FORGET[r] + 5:
                        spread_rows(r)
                    if i == FORGET[r] + 7:
                        turned_rows(r)
                for n in range(2):
                    if i == TURN[n] + 2:
                        turned_copy(2 * B + 2 + n, bank[0])
                if b >= 1 and h == 15:
                    turned_copy(3 * B + b - 1, bank[1])
                if NH <= i < NH + NQ:
                    w = i - NH
                    landed(act, ("q2g", "q2u", "q2d", "q3a", "q3b")[w])
                    act.activation(QW[:, w, :], RAW[w], ACT.Abs, accum_out=asum[:, w:w + 1]).then_inc(s["s_asum"], 1)
                if i >= NH + 11 and (i - NH - 11) % 3 == 0 and (i - NH - 11) // 3 < NQ:
                    w = (i - NH - 11) // 3
                    act.wait_ge(s["s_wsc"], 1)
                    act.activation(RAW[w], RAW[w], ACT.Identity, bias=magic[:, 0:1], scale=wrec[:, w:w + 1])\
                        .then_inc(s["s_wr"], 1)
            heads_copy(B - 1)
            for w in range(NQ):
                act.wait_ge(s["s_wc"], w + 1)
                act.activation(QW[:, w, :], RAW[w], ACT.Identity, bias=magic[:, 1:2]).then_inc(s["s_qw"], 1)
            turned_copy(3 * B + B - 1, bank[1])
            for b in range(B):
                act.wait_ge(s["s_nm1"], b + 1)
                for j in range(TB):
                    last = act.activation(ex1[:, b, j, :], lg1[:, b, j, :], ACT.Exp, bias=nmax1[:, b, j:j + 1],
                                          accum_out=sum1[:, b, j:j + 1])
                last.then_inc(s["s_ex1"], 1)
            act.wait_ge(s["s_qw"], NQ)
            for b in range(B):
                act.wait_ge(s["s_hmt"], b + 1)
                for h in range(2):
                    last = act.activation(HMT[b][:, 2 * h:2 * h + 2, :], pair(bank[2 * b + h][:]), ACT.Copy)
                last.then_inc(s["s_hmc"], 1)
            for b in range(B):
                turned_copy(4 * B + b, bank_a(b))
            for b in range(B):
                act.wait_ge(s["s_qk"], b + 1)
                act.activation(QT[b], pair(bank_a(b)[:]), ACT.Copy)
                act.activation(KT[b], pair(bank_b(b)[:]), ACT.Copy).then_inc(s["s_qk2"], 1)
            for b in range(B):
                act.wait_ge(s["s_nm2"], b + 1)
                for j in range(TB):
                    last = act.activation(PR[b][:, j, :], bank[2 * b + j][:], ACT.Exp, bias=nmax2[:, b, j:j + 1],
                                          scale=D ** -0.5, accum_out=sum2[:, b, j:j + 1])
                last.then_inc(s["s_ex2"], 1)
            for b in range(B):
                act.wait_ge(s["s_pt2"], b + 1)
                act.activation(PT[b][:, 0:TB, :], pair(bank_a(b)[:]), ACT.Copy).then_inc(s["s_ptc2"], 1)
            for b in range(B):
                act.wait_ge(s["s_o2"], b + 1)
                act.activation(OT[b], pair(bank_a(b)[:]), ACT.Copy).then_inc(s["s_oc2"], 1)

            def quantised_copy(u):
                b = u % B
                act.wait_ge(s["s_qt"], u + 1)
                act.activation(XQT[:, b], pair(bank_a(b)[:, 0:S].bitcast(BF16)), ACT.Copy).then_inc(s["s_qc"], 1)

            def hidden_round(v):
                b = v % B
                act.wait_ge(s["s_rh"], v + 1)
                act.activation(H[b], H[b], ACT.Identity, bias=magic[:, 0:1], scale=rh1[:, b:b + 1])\
                    .then_inc(s["s_hr"], 1)

            def hidden_copy(v):
                b = v % B
                act.wait_ge(s["s_hqt"], v + 1)
                act.activation(HQT[b], pair(bank_a(b)[:].bitcast(BF16), KI), ACT.Copy).then_inc(s["s_hqc"], 1)

            for b in range(B):
                quantised_copy(b)
            for j in range(TB):
                for n in range(2):
                    for b in range(B):
                        g = B * (2 * j + n) + b
                        act.wait_ge(s["s_gu"], g + 1)
                        act.activation(GS[b][:, 512 * n:512 * (n + 1)], bank_a(b)[:], ACT.Silu,
                                       scale=fg[:, TB * b + j, 0:1]).then_inc(s["s_gs"], 1)
                for b in range(B):
                    hidden_round(B * j + b)
                for b in range(B):
                    hidden_copy(B * j + b)
            landed(act, "small")
            act.activation(alpha[:], mix[:, 2:3], ACT.Sigmoid)
            act.activation(mix[:, 3:4], mix[:, 3:4], ACT.Exp).then_inc(s["s_mixe"], 1)
            for b in range(B):
                turned_copy(5 * B + b, bank_a(b))
            for b in range(B):
                act.wait_ge(s["s_q3"], b + 1)
                act.activation(QT[b], pair(bank_b(b)[:]), ACT.Copy).then_inc(s["s_qc3"], 1)
            for b in range(B):
                act.wait_ge(s["s_m3"], b + 1)
                act.activation(EX3[b], SC[b], ACT.Exp).then_inc(s["s_ex3"], 1)
            for b in range(B):
                act.wait_ge(s["s_pt3"], b + 1)
                act.activation(PT[b][:, 0:TB, :], pair(bank_b(b)[:]), ACT.Copy).then_inc(s["s_ptc3"], 1)
            for b in range(B):
                act.wait_ge(s["s_o3"], b + 1)
                act.activation(OT[b], pair(bank_a(b)[:]), ACT.Copy).then_inc(s["s_oc3"], 1)
            for b in range(B):
                quantised_copy(B + b)
            for j in range(TB):
                for b in range(B):
                    act.wait_ge(s["s_gu"], 2 * NT + B * j + b + 1)
                    for n in range(2):
                        last = act.activation(GS[b][:, 512 * n:512 * (n + 1)], bank[2 * b + n][:], ACT.Relu,
                                              scale=fg[:, TB * b + j, 0:1])
                    last.then_inc(s["s_gs"], 1)
                for b in range(B):
                    hidden_round(NT + B * j + b)
                for b in range(B):
                    hidden_copy(NT + B * j + b)

        @block.tensor
        def _(pe):
            def turn(u, dst, ln=None):
                b = u % B
                pe.wait_ge(s["s_norm"], (u if ln is None else ln) + 1)
                for k in range(KD):
                    for j in range(TB):
                        last = pe.transpose(dst[:, S * k + P * j:S * k + P * (j + 1)],
                                            HN[:, TB * b + j, P * k:P * (k + 1)], identf[:])
                last.then_inc(s["s_turned"], 1)

            def tokens(b, j, k):
                return HT[:, k, S * b + P * j:S * b + P * (j + 1)]

            pe.wait_ge(s["s_const"], 1)
            for b in range(B):
                turn(b, bank_a(b))
            landed(pe, "ctxT")

            def product_in0(b):
                pe.wait_ge(s["s_hm"], b + 1)
                for m in range(KD):
                    for e in range(E0):
                        for k in range(KD):
                            last = pe.matmul(bank_a(b)[:, S * m:S * (m + 1)],
                                             CT[:, k, S * e + P * m:S * e + P * (m + 1)], hm[b % 2][:, e, k, :],
                                             start=(e + k == 0), stop=(e == E0 - 1 and k == KD - 1))
                last.then_inc(s["s_z"], 1)

            def product_out0(b):
                pe.wait_ge(s["s_gm"], b + 1)
                for j in range(TB):
                    for e in range(E0):
                        for k in range(KD):
                            last = pe.matmul(bank_b(b)[:, D * j:D * (j + 1)],
                                             gm[b % 2][:, e, k, P * j:P * (j + 1)], CT[:, k, S * e:S * (e + 1)],
                                             start=(e + k == 0), stop=(e == E0 - 1 and k == KD - 1))
                last.then_inc(s["s_y0"], 1)

            product_in0(0)
            for b in range(1, B):
                product_in0(b)
                product_out0(b - 1)
            product_out0(B - 1)

            for b in range(B):
                turn(B + b, bank[b])
            landed(pe, "router")
            for b in range(B):
                pe.wait_ge(s["s_ht"], B + b + 1)
                for j in range(TB):
                    for k in range(KD):
                        last = pe.matmul(bank[6][:, E * (TB * b + j):E * (TB * b + j + 1)], tokens(b, j, k), RW[:, k, :],
                                         start=(k == 0), stop=(k == KD - 1))
            last.then_inc(s["s_lg"], 1)
            landed(pe, "shared")

            def shared_in(i):
                c, f, q = i // NF, i % NF, i % 3
                if i >= 3:
                    pe.wait_ge(s["s_hs"], i - 2)
                for w, bk in ((SG, 0), (SU, 3)):
                    for k in range(KD):
                        last = pe.matmul(bank[bk + q][:], w[:, k, P * f:P * (f + 1)],
                                         HT[:, k, 512 * c:512 * (c + 1)], start=(k == 0), stop=(k == KD - 1))
                last.then_inc(s["s_hsg"], 1)

            def counts(b):
                pe.wait_ge(s["s_m"], b + 1)
                if b >= 1:
                    pe.wait_ge(s["s_slot"], b)
                for j in range(TB):
                    c = bank[7][:, E * j:E * (j + 1)]
                    pe.matmul(c, before[:], chosen[:, TB * b + j, :], start=True, stop=False)
                    last = pe.matmul(c, onesb[:], earlier[:, TB * b + j, :], start=False, stop=True)
                last.then_inc(s["s_count"], 1)

            shared_in(0)
            shared_in(1)
            counts(0)
            shared_in(2)
            counts(1)
            for i in range(3, 2 * NF):
                shared_in(i)
                if i <= 4:
                    counts(i - 1)
            pe.wait_ge(s["s_slot"], B)
            for b in range(B):
                pe.wait_ge(s["s_hs"], NF * (b // 2 + 1))
                if b >= 2:
                    pe.wait_ge(s["s_xsh"], b - 1)
                for j in range(TB):
                    for f in range(NF):
                        last = pe.matmul(bank[6 + b % 2][:, D * j:D * (j + 1)],
                                         HS[:, f, S * b + P * j:S * b + P * (j + 1)], SD[:, f, :],
                                         start=(f == 0), stop=(f == NF - 1))
                last.then_inc(s["s_ysh"], 1)

            def experts_turn(t):
                q = t % 2
                pe.wait_ge(s_xg[t % 4], 16 * (t // 4 + 1))
                if t >= 2:
                    pe.wait_ge(s["s_xgT"], t - 1)
                for k in range(KD):
                    last = pe.transpose(bank[q][:, P * k:P * (k + 1)], xgt[:, t % 4, P * k:P * (k + 1)], identf[:])
                last.then_inc(s["s_xgturned"], 1)

            def experts_in(t):
                q, c, o = t % 2, t // CH, t % CH
                pe.wait_ge(s["s_xgT"], t + 1)
                if t >= 2:
                    pe.wait_ge(s["s_he"], t - 1)
                if o == 0:
                    pe.wait_ge(s_ew[c % RING], 48 * (c // RING + 1))
                for w, at in ((egw[c % RING], 0), (euw[c % RING], P)):
                    for i in range(2):
                        for k in range(KD):
                            last = pe.matmul(bank[2 + q][:, at + 64 * i:at + 64 * (i + 1)],
                                             w[:, k, 256 * o + P * i:256 * o + P * (i + 1)],
                                             xgT[:, q, k, 64 * i:64 * (i + 1)], start=(k == 0), stop=(k == KD - 1))
                last.then_inc(s["s_egu"], 1)

            def experts_out(t):
                q, c, o = t % 2, t // CH, t % CH
                pe.wait_ge(s["s_he"], t + 1)
                if t >= 2:
                    pe.wait_ge(s["s_ye"], t - 1)
                for i in range(2):
                    last = pe.matmul(bank[4 + q][64 * i:64 * (i + 1), 0:D], he[:, q, i, :],
                                     edw[c % RING][:, 2 * o + i, :], start=True, stop=True)
                last.then_inc(s["s_ey"], 1)

            for t in range(ST + 2):
                if t < ST:
                    experts_turn(t)
                if 1 <= t <= ST:
                    experts_in(t - 1)
                if t >= 2:
                    experts_out(t - 2)

            def gates(b):
                pe.wait_ge(s["s_ht"], 2 * B + b + 1)
                for g in range(2):
                    for kt in range(3 * KD):
                        src = HT if kt < KD else CT
                        last = pe.matmul(bank[1][32 * b:32 * (b + 1), S * g:S * (g + 1)], WIF[:, g, kt, :],
                                         src[:, kt % KD, S * b:S * (b + 1)],
                                         start=(kt == 0), stop=(kt == 3 * KD - 1))
                last.then_inc(s["s_gate"], 1)

            def rows_turn(r):
                p0, p1 = PART[r]
                pe.wait_ge(s["s_nx"], r + 1)
                if r >= 1:
                    pe.wait_ge(s["s_atn"], r)
                for i, row in enumerate((ga, nx)):
                    for j in range(TB):
                        o = P * (TB * i + j)
                        last = pe.transpose(bank[0][:, o:o + p1 - p0], row[p0:p1, P * j:P * (j + 1)],
                                            identf[p0:p1, p0:p1])
                last.then_inc(s["s_trd"], 1)

            landed(pe, "small")
            turn(2 * B, bank[0])
            gates(0)
            turn(2 * B + 1, bank[0])
            gates(1)
            rows_turn(0)
            pe.wait_ge(s["s_v1"], 1)

            def scores(i):
                b, h = i // NH, i % NH
                if h == 0:
                    pe.wait_ge(s_st[b % 2], 16 * 2 * len(PAIRS) * (b // 2 + 1))
                    pe.wait_ge(s["s_cmp"], (1, 2, 3, 3)[b])
                if i >= 2:
                    pe.wait_ge(s["s_dexp"], i - 1)
                    pe.wait_ge(s["s_cs"], i - 1)
                dbk, sbk = bank[2 + i % 2], bank[4 + i % 2]
                pe.matmul(dbk[:, 0:S], sel[0:96, h, :], CMP[0:96, b, :], start=True, stop=True)
                pe.matmul(dbk[:, S:384], sel[0:96, h, :], CMP[0:96, b, P:S], start=False, stop=True,
                          skip_group_check=True)
                pe.matmul(pair(dbk[:, 0:384], 3)[:, 0:3:2, :], identb[:], pair(future[:], 2), start=False, stop=True,
                          skip_group_check=True)
                k, q = KST[b % 2][:, h, :], QST[b % 2][:, h, :]
                pe.matmul(sbk[:, 0:S], k[:, 0:P], q, start=True, stop=True)
                pe.matmul(sbk[:, S:384], k[:, P:S], q[:, P:S], start=True, stop=True).then_inc(s["s_dq"], 1)

            def values(i):
                b, h = i // NH, i % NH
                pe.wait_ge(s["s_cs"], i + 1)
                if h == 0 and b >= 1:
                    pe.wait_ge(s["s_hcp"], b)
                cs = dcs[:, 2 + i % 3, :]
                pe.matmul(bank[6][:, 17 * h:17 * (h + 1)], cs[:, 0:P], V1[:, TB * b, h, :], start=True, stop=True)
                pe.matmul(bank[7][:, 17 * h:17 * (h + 1)], cs[:, P:S], V1[:, TB * b, h, :], start=True, stop=False)
                pe.matmul(bank[7][:, 17 * h:17 * (h + 1)], cs[:, S:384], V1[:, TB * b + 1, h, :], start=False,
                          stop=True).then_inc(s["s_pv"], 1)

            for i in range(B * NH):
                b, h = i // NH, i % NH
                scores(i)
                if i >= 2:
                    values(i - 2)
                for n in range(2):
                    if i == TURN[n] + 2:
                        pe.wait_ge(s["s_atn"], n + 1)
                        turn(2 * B + 2 + n, bank[0])
                    if i == TURN[n] + 3:
                        gates(2 + n)
                for r in (1, 2):
                    if i == FORGET[r] + 6:
                        rows_turn(r)
                if i == NH + 8:
                    pe.wait_ge(s["s_atn"], 3)
                    pe.wait_ge(s["s_asum"], NQ)
                    pe.matmul(bank[0][:, 0:NQ], onesf[:], asum[:], start=True, stop=True).then_inc(s["s_wtot"], 1)
                if b >= 1 and h == 15:
                    if b >= 2:
                        pe.wait_ge(s["s_ht"], 3 * B + b - 1)
                    turn(3 * B + b - 1, bank[1])
            values(B * NH - 2)
            values(B * NH - 1)
            pe.wait_ge(s["s_ht"], 3 * B + B - 1)
            turn(3 * B + B - 1, bank[1])

            landed(pe, "lowrank")
            pe.wait_ge(s["s_wsc"], 1)
            pe.wait_ge(s["s_hcp"], B)
            for b in range(B):
                if b == 0:
                    pe.wait_ge(s["s_ht"], 4 * B)
                for j in range(TB):
                    for k in range(KD):
                        last = pe.matmul(bank_a(b)[:, E1 * j:E1 * (j + 1)], tokens(b, j, k), LG[:, k, :],
                                         start=(k == 0), stop=(k == KD - 1))
                last.then_inc(s["s_l1"], 1)
            for b in range(B):
                pe.wait_ge(s["s_nm1"], b + 1)
                for j in range(TB):
                    for k in range(KD):
                        last = pe.matmul(bank[2 * b + j][:], tokens(b, j, k), LA[:, k, :],
                                         start=(k == 0), stop=(k == KD - 1))
                last.then_inc(s["s_ha"], 1)
            for b in range(B):
                pe.wait_ge(s["s_hm1"], b + 1)
                for j in range(TB):
                    for f in range(4):
                        last = pe.transpose(bank[2 * b + f // 2][:, S * (f % 2) + P * j:S * (f % 2) + P * (j + 1)],
                                            HM1[b][:, j, P * f:P * (f + 1)], identf[:])
                last.then_inc(s["s_hmt"], 1)
            for b in range(B):
                pe.wait_ge(s["s_hmc"], b + 1)
                for j in range(TB):
                    for f in range(4):
                        last = pe.matmul(bank_a(b)[:, D * j:D * (j + 1)], HMT[b][:, f, P * j:P * (j + 1)], LB[:, f, :],
                                         start=(f == 0), stop=(f == 3))
                last.then_inc(s["s_y1"], 1)

            landed(pe, "w2")
            for b in range(B):
                turn(4 * B + b, bank_a(b))
            for b in range(B):
                pe.wait_ge(s["s_ht"], 4 * B + b + 1)
                for w in range(2):
                    for m in range(KD):
                        for k in range(KD):
                            last = pe.matmul(bank[2 * b + w][:, S * m:S * (m + 1)], W2[:, w, k, P * m:P * (m + 1)],
                                             HT[:, k, S * b:S * (b + 1)], start=(k == 0), stop=(k == KD - 1))
                last.then_inc(s["s_qk"], 1)
            for b in range(B):
                pe.wait_ge(s["s_qk2"], b + 1)
                for j in range(TB):
                    for k in range(KD):
                        last = pe.matmul(bank_a(b)[:, D * j:D * (j + 1)], tokens(b, j, k), W2[:, 2, k, :],
                                         start=(k == 0), stop=(k == KD - 1))
                last.then_inc(s["s_v"], 1)
            for b in range(B):
                pe.wait_ge(s["s_v2"], b + 1)
                for j in range(TB):
                    for half in range(2):
                        for k in range(KD):
                            keys = CT[:, k, S * b:S * (b + 1)] if half == 0 else KT[b][:, k, :]
                            last = pe.matmul(bank[2 * b + j][:, S * half:S * (half + 1)], QT[b][:, k, P * j:P * (j + 1)],
                                             keys, start=(k == 0), stop=(k == KD - 1))
                last.then_inc(s["s_sc2"], 1)
            for b in range(B):
                pe.wait_ge(s["s_ex2"], b + 1)
                for j in range(TB):
                    for c in range(4):
                        last = pe.transpose(bank[2 * b + c // 2][:, S * (c % 2) + P * j:S * (c % 2) + P * (j + 1)],
                                            PR[b][:, j, P * c:P * (c + 1)], identf[:])
                last.then_inc(s["s_pt2"], 1)
            for b in range(B):
                pe.wait_ge(s["s_ptc2"], b + 1)
                pe.wait_ge(s_ptd2, b + 1)
                for m in range(KD):
                    for c in range(4):
                        v = CN[:, TB * b + c, P * m:P * (m + 1)] if c < TB else VN[b][:, c - TB, P * m:P * (m + 1)]
                        last = pe.matmul(bank_a(b)[:, S * m:S * (m + 1)], v, PT[b][:, c, :],
                                         start=(c == 0), stop=(c == 3))
                last.then_inc(s["s_o2"], 1)
            for b in range(B):
                pe.wait_ge(s["s_oc2"], b + 1)
                for j in range(TB):
                    for m in range(KD):
                        last = pe.matmul(bank_b(b)[:, D * j:D * (j + 1)], OT[b][:, m, P * j:P * (j + 1)], W2[:, 3, m, :],
                                         start=(m == 0), stop=(m == KD - 1))
                last.then_inc(s["s_y2"], 1)

            def quantised_turn(u):
                b = u % B
                pe.wait_ge(s["s_qn"], u + 1)
                for k in range(KD):
                    for j in range(TB):
                        o = S * k + P * j
                        last = pe.transpose(bank_a(b)[:, 0:S].bitcast(BF16)[:, o:o + P],
                                            XQ[:, b, j, P * k:P * (k + 1)], identb[:])
                last.then_inc(s["s_qt"], 1)

            def quantised_product(b, j, w, n, dst):
                for k in range(KD):
                    last = pe.matmul(dst[:], XQT[:, b, k, P * j:P * (j + 1)],
                                     QW[:, w, NI * k + 512 * n:NI * k + 512 * (n + 1)],
                                     start=(k == 0), stop=(k == KD - 1))
                return last

            def hidden_turn(v):
                b = v % B
                pe.wait_ge(s["s_hq"], v + 1)
                for f in range(KI):
                    last = pe.transpose(bank_a(b)[:].bitcast(BF16)[:, P * f:P * (f + 1)],
                                        HQ[b][:, P * f:P * (f + 1)], identb[:])
                last.then_inc(s["s_hqt"], 1)

            def product_out(v, w):
                b = v % B
                pe.wait_ge(s["s_hqc"], v + 1)
                for f in range(KI):
                    last = pe.matmul(bank_b(b)[:, 0:D], HQT[b][:, f, :], QW[:, w, D * f:D * (f + 1)],
                                     start=(f == 0), stop=(f == KI - 1))
                last.then_inc(s["s_yq"], 1)

            for b in range(B):
                quantised_turn(b)
            for j in range(TB):
                for n in range(2):
                    for b in range(B):
                        g = B * (2 * j + n) + b
                        if g < B:
                            pe.wait_ge(s["s_qc"], b + 1)
                        else:
                            pe.wait_ge(s_hmg, g - B + 1)
                        if j >= 1 and n == 0:
                            pe.wait_ge(s["s_xq"], B * (j - 1) + b + 1)
                        quantised_product(b, j, 0, n, bank_a(b))
                        quantised_product(b, j, 1, n, bank_b(b)).then_inc(s["s_gu"], 1)
                for b in range(B):
                    hidden_turn(B * j + b)
                for b in range(B):
                    product_out(B * j + b, 2)
            landed(pe, "w3")
            for b in range(B):
                turn(5 * B + b, bank_a(b), ln=6 * B + b)
            for b in range(B):
                pe.wait_ge(s["s_ht"], 5 * B + b + 1)
                for m in range(KD):
                    for k in range(KD):
                        last = pe.matmul(bank_b(b)[:, S * m:S * (m + 1)], W3[:, 0, k, P * m:P * (m + 1)],
                                         HT[:, k, S * b:S * (b + 1)], start=(k == 0), stop=(k == KD - 1))
                last.then_inc(s["s_q3"], 1)
            for b in range(B):
                pe.wait_ge(s["s_qc3"], b + 1)
                for j in range(TB):
                    for k in range(KD):
                        last = pe.matmul(bank_a(b)[:, S * j:S * (j + 1)], QT[b][:, k, P * j:P * (j + 1)],
                                         CT[:, k, S * b:S * (b + 1)], start=(k == 0), stop=(k == KD - 1))
                last.then_inc(s["s_sc3"], 1)
            for b in range(B):
                pe.wait_ge(s["s_p3"], b + 1)
                for j in range(TB):
                    for c in range(TB):
                        last = pe.transpose(bank_b(b)[:, S * c + P * j:S * c + P * (j + 1)],
                                            P3[b][:, j, P * c:P * (c + 1)], identf[:])
                last.then_inc(s["s_pt3"], 1)
            for b in range(B):
                pe.wait_ge(s["s_ptc3"], b + 1)
                for m in range(KD):
                    for c in range(TB):
                        last = pe.matmul(bank_a(b)[:, S * m:S * (m + 1)], CN[:, TB * b + c, P * m:P * (m + 1)],
                                         PT[b][:, c, :], start=(c == 0), stop=(c == TB - 1))
                last.then_inc(s["s_o3"], 1)
            for b in range(B):
                pe.wait_ge(s["s_oc3"], b + 1)
                for j in range(TB):
                    for m in range(KD):
                        last = pe.matmul(bank_b(b)[:, D * j:D * (j + 1)], OT[b][:, m, P * j:P * (j + 1)], W3[:, 1, m, :],
                                         start=(m == 0), stop=(m == KD - 1))
                last.then_inc(s["s_y3"], 1)
            for b in range(B):
                quantised_turn(B + b)
            for j in range(TB):
                for b in range(B):
                    if j == 0:
                        pe.wait_ge(s["s_qc"], B + b + 1)
                    else:
                        pe.wait_ge(s["s_xout"], b + 1)
                    quantised_product(b, j, 3, 0, bank_a(b))
                    quantised_product(b, j, 3, 1, bank_b(b)).then_inc(s["s_gu"], 1)
                for b in range(B):
                    hidden_turn(NT + B * j + b)
                for b in range(B):
                    product_out(NT + B * j + b, 4)


def kernel(**inputs):
    import numpy as _np
    import concourse.bacc as _bacc
    from concourse import mybir as _mybir
    from concourse.bass_utils import run_bass_kernel_spmd as _run

    i = {n: _np.asarray(v) for n, v in inputs.items()}
    c = _np.ascontiguousarray

    def turned(w):
        return c(_np.moveaxis(w, -1, 0).reshape(w.shape[-1], -1))

    arrays = {
        "x": i["x"].reshape(N, D), "g": _np.concatenate([i["g_xattn"], i["g_ffn"]]),
        "tok": i["itok_BxS_13_99985"].reshape(N), "ctx": i["ctx_2048"].reshape(N, D), "ctxT": turned(i["ctx_2048"]),
        "router": turned(i["L0_ffn_router_w"]), "router_bias": i["L0_ffn_router_bias"],
        "eg": turned(i["L0_ffn_gate_w"]), "eu": turned(i["L0_ffn_up_w"]),
        "ed": c(i["L0_ffn_down_w"].transpose(0, 2, 1)).reshape(E * F, D),
        "sg": turned(i["L0_ffn_sh_gate_w"]), "su": turned(i["L0_ffn_sh_up_w"]),
        "sd": c(i["L0_ffn_sh_down_w"].transpose(0, 2, 1)).reshape(SF, D),
        "wi": i["L1_xattn_Wi"], "bi": i["L1_xattn_bi"], "wf": i["L1_xattn_Wf"], "bf": i["L1_xattn_bf"],
        "lnsc": i["L1_xattn_ln_scale"],
        "la": turned(i["L1_ffn_A"]), "lb": c(i["L1_ffn_Bw"].transpose(0, 2, 1)).reshape(E1 * R1, D),
        "lg": turned(i["L1_ffn_Wg"]),
        "wq": turned(i["L2_xattn_wq"]), "wk": turned(i["L2_xattn_wk"]), "wv": turned(i["L2_xattn_wv"]),
        "wo": turned(i["L2_xattn_wo"]),
        "q2g": turned(i["L2_ffn_w_gate"]), "q2u": turned(i["L2_ffn_w_up"]), "q2d": turned(i["L2_ffn_w_down"]),
        "w3q": turned(i["L3_xattn_W_qkv"][0:D]), "w3o": turned(i["L3_xattn_W_o"]),
        "mix": _np.stack([i["L3_xattn_beta_q"], i["L3_xattn_beta_k"], i["L3_xattn_gate"], i["L3_xattn_log_tau"]]),
        "q3a": turned(i["L3_ffn_w1"]), "q3b": turned(i["L3_ffn_w2"]),
    }
    nc = _bacc.Bacc("TRN2", target_bir_lowering=False, num_devices=1)
    ins = {n: nc.dram_tensor(f"in_{n}", v.shape, _mybir.dt.from_np(v.dtype), kind="ExternalInput").ap()
           for n, v in arrays.items()}
    out = nc.dram_tensor("out_x", (N, D), F32, kind="ExternalOutput").ap()
    flamingo(nc, ins, out)
    r = _run(nc, [{f"in_{n}": c(v) for n, v in arrays.items()}], core_ids=[0])
    return r.results[0]["out_x"].reshape(B, S, D)
```

```python
from contextlib import ExitStack

import concourse.bass as bass
from concourse import mybir

ALU = mybir.AluOpType
ACT = mybir.ActivationFunctionType
AX = mybir.AxisListType
F32 = mybir.dt.float32
BF16 = mybir.dt.bfloat16
I32 = mybir.dt.int32
U32 = mybir.dt.uint32

P = 128
B, S, D = 4, 256, 256
N = B * S
KD = D // P
TB = S // P
NT = N // P
E0, VOCAB = 4, 12500
PER = VOCAB // E0
E, K, F, CAP = 64, 4, 64, 32
SLOTS = E * CAP
ST = SLOTS // P
EP = P // CAP
SF = 512
NF = SF // P
NH, DH = 16, 16
E1, R1 = 8, 64
NI = 1024
KI = NI // P
NQ = 5
NW = 2 * NQ
CLIP = 54
MAGIC = 12582912.0
FAR = 1048576.0
NEG = -1e30
LOWEST = -3.0e38


FFN2 = [((name, j), engines) for j in range(TB) for name, engines in
        (("in2a", "TVS"), ("in2b", "TVS"), ("round2", "VS"), ("turn2", "TS"), ("out2", "TV" if j < TB - 1 else "TVG"))]
FFN3 = [((name, j), engines) for j in range(TB) for name, engines in
        (("in3", "TVS"), ("round3", "VS"), ("turn3", "TS"), ("out3", "TV"))]
STEPS = ([("heads", "VG"), ("turn1", "TVS"), ("route1", "TVS"), ("low1", "TV"), ("lowturn1", "TS"), ("lowout1", "TVG"),
          ("norm4", "TVS"), ("keys2", "TS"), ("values2", "TS"), ("scores2", "TVS"), ("probs2", "TS"), ("mix2", "TS"),
          ("project2", "TVG"), ("norm5", "VSG"), ("turn5", "TS")] + FFN2 +
         [("norm6", "TVS"), ("queries3", "TS"), ("scores3", "TVS"), ("clip3", "VS"), ("probs3", "TS"), ("mix3", "TS"),
          ("project3", "TVG"), ("norm7", "VSG"), ("turn7", "TS")] + FFN3)
TURNS_OF = {
    "T": ("021012130230130201230201320103123012313010232303112201023031031212013203231010302121313002"
             "3023231110033311202012103130210213232323232"),
    "V": ("012303123001132203312003101220301321021032013012312031023121302303213103032101201313021201"
             "0130123232323232"),
    "S": ("012130230012302012010312312301030231302101220132130321032013013212310203023101310102323231"
             "310003230111201213013021032123232323232"),
    "G": "3012300112233012300113322",
}


def plan(engine):
    left = [[step for step, engines in STEPS if engine in engines and (step not in ("heads", "turn1") or b == B - 1)]
            for b in range(B)]
    return [(left[int(b)].pop(0), int(b)) for b in TURNS_OF[engine]]


PLAN = {engine: plan(engine) for engine in "TVSG"}


def nth(engine, steps, step, b):
    return [e for e in PLAN[engine] if e[0] in steps].index((step, b)) + 1


def flamingo(nc, a, out):
    ctx = ExitStack()
    with ctx:
        def sb(name, shape, dt=F32):
            return ctx.enter_context(nc.sbuf_tensor(name, shape, dt))

        def sem(name):
            return ctx.enter_context(nc.semaphore(name))

        bank = [ctx.enter_context(nc.psum_tensor(f"bank{i}", [P, 512], F32)) for i in range(8)]

        xg_dram = nc.dram_tensor("xg_rows", [SLOTS, D], F32, kind="Internal").ap()
        y_dram = nc.dram_tensor("y_rows", [SLOTS, D], F32, kind="Internal").ap()

        kp_dram = nc.dram_tensor("key_parts", [3, D, N], BF16, kind="Internal").ap()
        qp_dram = nc.dram_tensor("query_parts", [3, D, N], BF16, kind="Internal").ap()

        def bank_a(b):
            return bank[2 * b]

        def bank_b(b):
            return bank[2 * b + 1]

        def pair(ap, n=TB):
            return ap.rearrange("p (j n) -> p j n", j=n)

        X = sb("X", [P, NT, D])
        HN = sb("HN", [P, NT, D])
        HT = sb("HT", [P, KD, N])
        CN = sb("CN", [P, NT, D])
        CT = sb("CT", [P, KD, N])
        identf = sb("identf", [P, P])
        identb = sb("identb", [P, P], BF16)
        onesf = sb("onesf", [P, P])
        onesb = sb("onesb", [P, P], BF16)
        before = sb("before", [P, P], BF16)
        future = sb("future", [P, 2 * P], BF16)
        neghalf = sb("neghalf", [P, 32])
        magic = sb("magic", [P, 2])
        gates8 = sb("gates8", [P, 8])
        tg = sb("tg", [P, 8])
        bnst = sb("bnst", [P, TB, 6])
        mv = sb("mv", [P, B, TB, 2])
        ve = sb("ve", [P, B, TB])
        rstd = sb("rstd", [P, B, TB])

        ar = sb("ar", [P, 4096])
        HM = sb("HM", [P, 4112])
        big = sb("big", [P, 12288])
        WK = sb("WK", [P, 4096])
        WK2 = sb("WK2", [P, 2048])
        SH = sb("SH", [P, 3072])
        ph = sb("ph", [P, 5120])

        def big_of(b, lo, hi):
            return big[:, 3072 * b + lo:3072 * b + hi]

        tokb = ar[:, 0:N].bitcast(I32)
        ge = ar[:, N:2 * N].bitcast(BF16).rearrange("p (i n) -> p i n", i=2)
        maskb = ar[:, 2 * N:4 * N].bitcast(BF16).rearrange("p (e n) -> p e n", e=E0)
        hm = [HM[:, 2048 * q:2048 * (q + 1)].rearrange("p (e k n) -> p e k n", e=E0, k=KD) for q in range(2)]
        gm = [WK[:, 2048 * q:2048 * (q + 1)].rearrange("p (e k n) -> p e k n", e=E0, k=KD) for q in range(2)]
        gz = [WK2[:, 1024 * q:1024 * q + 512] for q in range(2)]

        def logits(b):
            return bank[6][:, 0:TB * E] if b == 0 else bank[7][:, TB * E * (b - 1):TB * E * b]

        SG = pair(SH[:, 0:1024])
        SU = pair(SH[:, 1024:2048])
        SD = pair(SH[:, 2048:3072], NF)
        HS = pair(HM[:, 0:4096], NF)

        RW = sb("RW", [P, KD, E])
        rbias = sb("rbias", [P, E])
        iota64 = sb("iota64", [P, E])
        eoff = sb("eoff", [P, E])
        zer = sb("zer", [P, D])
        lg = sb("lg", [P, TB, E])
        lgb = sb("lgb", [P, TB, E])
        top = sb("top", [P, TB, 8])
        topi = sb("topi", [P, TB, 8], U32)
        pick = sb("pick", [P, TB, K])
        nmax = sb("nmax", [P, TB])
        ex = sb("ex", [P, NT, E])
        oh = ph[:, 0:1024].bitcast(BF16).rearrange("p (t k e) -> p t k e", t=NT, k=K)
        ohx = pair(ph[:, 1024:1536], TB * K)
        chosen = sb("chosen", [P, NT, E], BF16)
        earlier = sb("earlier", [P, NT + 1, E], BF16)
        wk4 = sb("wk4", [P, TB, K])
        wsum = sb("wsum", [P, TB])
        W4 = sb("W4", [P, NT, K])
        val = sb("val", [P, TB, E])
        far = lgb
        slotf = sb("slotf", [P, NT, K])
        slot = sb("slot", [P, NT, K], U32)
        SSL = pair(ph[:, 1536:2560], 2)
        xgt = pair(ph[:, 2560:3584], 4)
        xgT = ph[:, 3584:4096].rearrange("p (q k n) -> p q k n", q=2, k=KD)
        sil = sb("sil", [P, 2, P])
        he = sb("he", [P, 2, 2, 2 * CAP])
        ye = pair(ph[:, 4096:5120], 4)
        G4 = WK[:, 0:2048].rearrange("p (q k d) -> p q k d", q=2, k=K)
        CH, RING = 2, 4
        NCH = ST // CH
        CW = CH * EP * F
        egw = [pair(big[:, 3072 * q:3072 * q + 1024]) for q in range(RING)]
        euw = [pair(big[:, 3072 * q + 1024:3072 * q + 2048]) for q in range(RING)]
        edw = [pair(big[:, 3072 * q + 2048:3072 * (q + 1)], CH * EP // 2) for q in range(RING)]

        WIF = sb("WIF", [P, 2, 3 * KD, 32])
        bif = sb("bif", [P, 2])
        lns = sb("lns", [P, NH * DH])
        selc = sb("selc", [P, NH], BF16)
        sel = sb("sel", [P, NH, P], BF16)
        rows = pair(WK[:, 2048:4096], 8)
        fgt, nf, e1, lf, Fc, ga, cm, nx = (rows[:, r, :] for r in range(8))
        part = sb("part", [P, 3, S], BF16)
        CMP = sb("CMP", [P, B, S], BF16)
        ATN = sb("ATN", [P, 2 * TB, P])
        V1 = HM[:, 0:NT * NH * 17].rearrange("p (t h c) -> p t h c", t=NT, c=17)
        VALUES = NT * NH * 17
        vpad = HM[:, VALUES:VALUES + 16]
        dcs = pair(HM[:, VALUES + 16:VALUES + 16 + 5 * 384], 5)
        HV = sb("HV", [P, 4 * S])
        PAIRS = [(0, 0), (0, 1), (1, 0), (1, 1), (0, 2), (2, 0), (1, 2), (2, 1)]
        kparts = ar[:, 0:3072].bitcast(BF16).rearrange("p (a k n) -> p a k n", a=3, k=KD)
        krest = pair(WK[:, 0:2048])
        qparts = [ar[:, 2048 + 768 * q:2048 + 768 * (q + 1)].bitcast(BF16).rearrange("p (a k n) -> p a k n", a=3, k=KD)
                  for q in range(2)]
        KST = [m.bitcast(BF16).rearrange("p (h n) -> p h n", h=NH) for m in (WK2[:], big[:, 10240:12288])]
        QST = [m.bitcast(BF16).rearrange("p (h n) -> p h n", h=NH) for m in (SH[:, 0:2048], WK[:, 0:2048])]
        HR = pair(ar[:, 0:TB * NH * 17], TB * NH)
        hhf = ar[:, 544:544 + 512]
        hh = pair(hhf, TB * NH)
        sq = pair(ar[:, 1056:1056 + 512], TB * NH)
        ab = sb("ab", [P, TB * NH])
        mu = sb("mu", [P, TB * NH])
        vr = sb("vr", [P, TB * NH])
        rs = sb("rs", [P, TB * NH])
        FORGET = {1: 1, 2: 12}
        GATHER = (0, 2, 5)
        TURN = (3, 7)
        SUMS, SCALES, ROUNDED, CLIPPED, CAST = NH + 1, NH + NW + 3, NH + NW + 5, NH + NW + 7, NH + 2 * NW + 8
        HEADS_NORM = (5, 6, 7, 8, 13, 14)
        SPLIT = (6, 17, 19)
        PART = [(0, 32), (32, 64), (64, 128)]

        LA = pair(SH[:, 0:1024])
        LB = pair(SH[:, 1024:2048], 4)
        LG = sb("LG", [P, KD, E1])
        lg1 = sb("lg1", [P, B, TB, E1])
        ex1 = sb("ex1", [P, B, TB, E1])
        top1 = sb("top1", [P, TB, 8])
        topi1 = sb("topi1", [P, TB, 8], U32)
        pick1 = sb("pick1", [P, TB])
        nmax1 = sb("nmax1", [P, B, TB])
        sum1 = sb("sum1", [P, B, TB])
        MK = sb("MK", [P, B, TB, E1])
        HM1 = [pair(WK[:, 1024 * b:1024 * (b + 1)]) for b in range(B)]
        HMT = [pair(big_of(b, 0, 1024), 4) for b in range(B)]

        W2 = ar[:, 2048:4096].rearrange("p (w k d) -> p w k d", w=4, k=KD)
        W3 = SH[:, 2048:3072].rearrange("p (w k d) -> p w k d", w=2, k=KD)
        QT = [pair(big_of(b, 0, 512)) for b in range(B)]
        KT = [pair(big_of(b, 512, 1024)) for b in range(B)]
        VN = [pair(big_of(b, 1024, 1536)) for b in range(B)]
        PR = [pair(big_of(b, 1536, 2560)) for b in range(B)]
        OT = [pair(big_of(b, 2560, 3072)) for b in range(B)]
        PT = [pair(WK[:, 1024 * b:1024 * (b + 1)], 4) for b in range(B)]
        nmax2 = sb("nmax2", [P, B, TB])
        sum2 = sb("sum2", [P, B, TB])
        mix = sb("mix", [P, 4])
        alpha = sb("alpha", [P, 1])
        coef = sb("coef", [P, 1])
        cf2 = sb("cf2", [P, 1])
        SC = KT
        WR = VN
        EX3 = [pair(big_of(b, 1536, 2048)) for b in range(B)]
        P3 = [pair(big_of(b, 2048, 2560)) for b in range(B)]
        top3 = sb("top3", [P, B, TB, 8])

        RAW = [big[:, 2048 * i:2048 * (i + 1)] for i in range(NQ)]
        QWS = [ph[:, 1024 * i:1024 * (i + 1)].bitcast(BF16) for i in range(NQ)]
        QW = pair(ph[:].bitcast(BF16), NQ)
        asum = sb("asum", [P, NW])
        wsc = sb("wsc", [P, NQ])
        wrec = sb("wrec", [P, NQ])
        amax = sb("amax", [P, TB])
        sx = sb("sx", [P, NT])
        rq = sb("rq", [P, NT])
        fg = sb("fg", [P, NT, 2])
        XQ = HM[:, 512:1536].bitcast(BF16).rearrange("p (b j d) -> p b j d", b=B, j=TB)
        XQT = HM[:, 1536:2560].bitcast(BF16).rearrange("p (b k n) -> p b k n", b=B, k=KD)
        am1 = sb("am1", [P, B])
        sh1 = sb("sh1", [P, B])
        rh1 = sb("rh1", [P, B])
        fy1 = sb("fy1", [P, B])
        H = [big_of(b, 0, 1024) for b in range(B)]
        GS = [big_of(b, 1024, 2048) for b in range(B)]
        HQ = [big_of(b, 2048, 2560).bitcast(BF16) for b in range(B)]
        HQT = [pair(big_of(b, 2560, 3072).bitcast(BF16), KI) for b in range(B)]

        def half(weights, w):
            return weights[w // 2][:, 1024 * (w % 2):1024 * (w % 2 + 1)]

        names = ("s_vec s_const s_tanh s_lnvar s_lnrstd s_norm s_turned s_ht s_out s_xout "
                 "s_hm s_z s_silu s_gm s_y0 "
                 "s_lg s_nmax s_ex s_m s_count s_slot s_zero s_hsg s_ssl s_hs s_ysh s_xsh s_scat s_xgturned s_xgT "
                 "s_egu s_esil s_he s_ey s_ye s_g0 s_gx "
                 "s_kp s_kst s_qp s_qst s_sel s_v1 s_ones s_gate s_nf s_e1 s_ln s_m1 s_nx s_part s_cmp s_trd s_atn s_dq s_dexp s_cs s_pv "
                 "s_hcp s_hvt s_hr16 s_v16 s_r16 s_wif0 "
                 "s_l1 s_nm1 s_ex1 s_ha s_hm1 s_hmt s_hmc s_y1 "
                 "s_qk s_qk2 s_v s_v2 s_sc2 s_nm2 s_ex2 s_pt2 s_ptc2 s_qs s_xf s_sq s_o2 s_oc2 s_y2 "
                 "s_asum s_wtot s_wsc s_wr s_wc s_qw s_mixe "
                 "s_qn s_qt s_qc s_gu s_gs s_hr s_rh s_hm s_hq s_hqt s_hqc s_yq s_xq "
                 "s_q3 s_qc3 s_sc3 s_sl3 s_coef s_m3 s_ex3 s_p3 s_pt3 s_ptc3 s_o3 s_oc3 s_y3").split()
        s = {n: sem(n) for n in dict.fromkeys(names)}
        s_hmg = sem("s_hmg")
        s_xg = [sem(f"s_xg{i}") for i in range(4)]
        s_ys = [sem(f"s_ys{i}") for i in range(4)]
        s_gat = [sem(f"s_gat{i}") for i in range(2)]
        s_st = [sem(f"s_st{i}") for i in range(2)]
        s_ew = [sem(f"s_ew{i}") for i in range(RING)]

        GROUPS = {"x0": ["x0"], "x1": ["x1"], "x2": ["x2"], "x3": ["x3"], "g": ["g"], "tokb": ["tokb"],
                  "ctxT": ["ctxT"], "ctx": ["ctx"],
                  "router": ["router", "rbias"], "shared": ["sg", "su", "sd"],
                  "small": ["wi", "wf", "lnsc", "mix", "lg"] + [f"{g}{b}" for g in ("bi", "bf") for b in range(B)],
                  "lowrank": ["la", "lb"], "w2": ["wq", "wk", "wv", "wo"], "w3": ["w3q", "w3o"],
                  "q2g": ["q2g"], "q2u": ["q2u"], "q2d": ["q2d"], "q3a": ["q3a"], "q3b": ["q3b"]}
        group_sem = {g: sem("ld_" + g) for g in GROUPS}
        loads = {n: group_sem[g] for g, ns in GROUPS.items() for n in ns}

        def landed(eng, g):
            eng.wait_ge(group_sem[g], 16 * len(GROUPS[g]))

        def rows_of(name, k=P):
            return a[name].rearrange("(k p) c -> p k c", p=k)

        def to_all(name, n):
            return a[name].rearrange("(o n) -> o n", o=1).broadcast_to([P, n])

        xd = a["x"].rearrange("(b j p) d -> b p j d", b=B, j=TB)
        DMAS = [("tokb", tokb, to_all("tok", N)),
                ("x0", X[:, 0:TB, :], xd[0]), ("g", gates8[:], to_all("g", 8)),
                ("x1", X[:, TB:2 * TB, :], xd[1]), ("ctxT", CT[:], rows_of("ctxT")),
                ("x2", X[:, 2 * TB:3 * TB, :], xd[2]), ("x3", X[:, 3 * TB:4 * TB, :], xd[3]),
                ("router", RW[:], rows_of("router")), ("rbias", rbias[:], to_all("router_bias", E)),
                ("sg", SG, rows_of("sg")), ("su", SU, rows_of("su")), ("sd", SD, rows_of("sd")),
                ("ctx", CN[:], rows_of("ctx"))]
        for g, (w, bi) in enumerate((("wi", "bi"), ("wf", "bf"))):
            DMAS.append((w, WIF[:, g, :, 0:NH], rows_of(w)))
            for b in range(B):
                DMAS.append((f"{bi}{b}", bif[32 * b:32 * b + NH, g:g + 1], a[bi].rearrange("(h o) -> h o", o=1)))
        DMAS += [("lnsc", lns[:], to_all("lnsc", D)), ("lg", LG[:], rows_of("lg")), ("mix", mix[:], to_all("mix", 4))]

        STATS = ["heads", "lowout1", "project2", ("out2", TB - 1), "project3"]
        NORMS = ["turn1", "norm4", "norm5", "norm6", "norm7"]
        QUANTS = ["norm5", "norm7"]
        QTURNS = ["turn5", "turn7"]
        TURNS = ["turn1", "norm4", "norm6"]
        BEFORE = 3 * B + B - 1
        IN2 = [(st, j) for j in range(TB) for st in ("in2a", "in2b")]
        IN3 = [("in3", j) for j in range(TB)]
        FULL = [("in2b", j) for j in range(TB)] + IN3
        INS = IN2 + [("in3", j) for j in range(TB)]
        ROUNDS = [(st, j) for j in range(TB) for st in ("round2", "round3")]
        HTURNS = [(st, j) for j in range(TB) for st in ("turn2", "turn3")]
        OUT2 = [("out2", j) for j in range(TB)]
        OUTS = OUT2 + [("out3", j) for j in range(TB)]

        block = ctx.enter_context(nc.Block())

        @block.sync
        def _(sp):
            def expert_weights(c):
                q = c % RING
                if c >= RING:
                    sp.wait_ge(s["s_ey"], CH * (c - RING + 1))
                sp.dma_start(egw[q], a["eg"][:, CW * c:CW * (c + 1)].rearrange("(k p) c -> p k c", p=P))\
                    .then_inc(s_ew[q], 16)
                sp.dma_start(euw[q], a["eu"][:, CW * c:CW * (c + 1)].rearrange("(k p) c -> p k c", p=P))\
                    .then_inc(s_ew[q], 16)
                sp.dma_start(edw[q], a["ed"][CW * c:CW * (c + 1), :].rearrange("(i p) d -> p i d", p=P))\
                    .then_inc(s_ew[q], 16)

            def stack(b, dst, parts, which):
                for c, p in enumerate(PAIRS):
                    src = parts[p[which], :, S * b:S * (b + 1)].rearrange("(h d) n -> d h n", d=DH)
                    sp.dma_start(dst[DH * c:DH * (c + 1)], src).then_inc(s_st[b % 2], 16)

            def store_queries(b):
                sp.wait_ge(s["s_qp"], 4 * (b + 1))
                for p in range(3):
                    sp.dma_start(qp_dram[p, :, S * b:S * (b + 1)].rearrange("(k p) n -> p k n", p=P),
                                 qparts[b % 2][:, p]).then_inc(s["s_qst"], 16)
                sp.wait_ge(s["s_qst"], 48 * (b + 1))

            for n, dst, src in DMAS:
                if n == "wi":
                    sp.wait_ge(s["s_wif0"], 1)
                sp.dma_start(dst, src).then_inc(loads[n], 16)
            sp.wait_ge(s["s_const"], 1)
            sp.dma_start(xg_dram.rearrange("(t p) d -> p t d", p=P),
                         zer[:].unsqueeze(1).broadcast_to([P, ST, D])).then_inc(s["s_zero"], 16)
            for c in range(RING):
                expert_weights(c)
            sp.wait_ge(s["s_scat"], 16 * NT * K)
            def load_rows(t):
                sp.dma_start(xgt[:, t % 4, :], xg_dram[P * t:P * (t + 1), :]).then_inc(s_xg[t % 4], 16)

            for t in range(4):
                load_rows(t)
            for t in range(ST + 2):
                if t + 4 < ST:
                    sp.wait_ge(s["s_xgturned"], t + 1)
                    load_rows(t + 4)
                if t == ST // 2:
                    sp.wait_ge(s["s_kp"], 4)
                    for p in range(3):
                        sp.dma_start(kp_dram[p].rearrange("(k p) n -> p k n", p=P), kparts[:, p])\
                            .then_inc(s["s_kst"], 16)
                if t == ST - 4:
                    sp.wait_ge(s["s_kst"], 48)
                    stack(0, KST[0], kp_dram, 1)
                if t >= 2:
                    r = t - 2
                    sp.wait_ge(s["s_ye"], r + 1)
                    sp.dma_start(y_dram[P * r:P * (r + 1), :], ye[:, r % 4, :]).then_inc(s_ys[r % 4], 16)
                    if r % CH == CH - 1 and r // CH + RING < NCH:
                        expert_weights(r // CH + RING)
            sp.wait_ge(s["s_ysh"], B)
            sp.wait_ge(s["s_ey"], ST)
            stack(1, KST[1], kp_dram, 1)
            store_queries(0)
            stack(0, QST[0], qp_dram, 0)
            sp.wait_ge(s["s_gx"], NT)
            store_queries(1)
            stack(1, QST[1], qp_dram, 0)
            for i, n in enumerate(("q2g", "q2u", "q2d", "q3a", "q3b")):
                sp.dma_start(pair(RAW[i], a[n].shape[0] // P), rows_of(n)).then_inc(loads[n], 16)
            for n, dst in (("w3q", W3[:, 0]), ("w3o", W3[:, 1])):
                sp.dma_start(dst, rows_of(n)).then_inc(loads[n], 16)
            for b in range(2, B):
                sp.wait_ge(s["s_dq"], NH * (b - 1))
                stack(b, KST[b % 2], kp_dram, 1)
                store_queries(b)
                stack(b, QST[b % 2], qp_dram, 0)
            for n, dst in (("wq", W2[:, 0]), ("wk", W2[:, 1]), ("wv", W2[:, 2]), ("wo", W2[:, 3])):
                sp.dma_start(dst, rows_of(n)).then_inc(loads[n], 16)
            sp.wait_ge(s["s_dq"], NH * (B - 1))
            for n, dst in (("la", LA), ("lb", LB)):
                sp.dma_start(dst, rows_of(n)).then_inc(loads[n], 16)
            od = out.rearrange("(t p) d -> t p d", p=P)
            ends = [(step[1], b) for step, b in PLAN["V"] if step[0] == "out3"]
            for v, (j, b) in enumerate(ends):
                sp.wait_ge(s["s_xout"], v + 1)
                sp.dma_start(od[TB * b + j], X[:, TB * b + j, :]).then_inc(s["s_out"], 16)
            sp.wait_ge(s["s_out"], 16 * NT)

        @block.gpsimd
        def _(pool):
            def ln_rstd(b, count):
                pool.wait_ge(s["s_lnvar"], count)
                pool.tensor_tensor(rstd[:, b, :], ve[:, b, :], neghalf[:, 0:TB], ALU.pow)\
                    .then_inc(s["s_lnrstd"], 1)

            def ln_rstds(l):
                for b in range(B):
                    ln_rstd(b, B * l + b + 1)

            pool.memset(zer[:], 0.0)
            pool.memset(WIF[:], 0.0)
            pool.memset(bif[:], 0.0).then_inc(s["s_wif0"], 1)
            pool.memset(identf[:], 0.0)
            pool.memset(onesf[:], 1.0)
            pool.memset(onesb[:], 1.0)
            pool.memset(future[:], 0.0)
            pool.memset(he[:], 0.0)
            pool.memset(earlier[:, 0, :], 0.0)
            pool.memset(magic[:, 0:1], MAGIC)
            pool.memset(magic[:, 1:2], -MAGIC)
            pool.iota(iota64[:], [[1, E]], base=0, channel_multiplier=0, allow_small_or_imprecise_dtypes=True)
            pool.iota(eoff[:], [[CAP, E]], base=0, channel_multiplier=0, allow_small_or_imprecise_dtypes=True)
            pool.memset(neghalf[:], -0.5).then_inc(s["s_wif0"], 1)
            pool.wait_ge(s["s_wif0"], 2)
            pool.affine_select(out=before[:], in_=onesb[:], compare_op=ALU.is_gt, fill=0.0, base=0,
                               pattern=[[1, P]], channel_multiplier=-1)
            for c in range(2):
                pool.affine_select(out=future[:, P * c:P * (c + 1)], in_=future[:, P * c:P * (c + 1)],
                                   compare_op=ALU.is_ge, fill=NEG, base=0, pattern=[[1, P]], channel_multiplier=-1)
            pool.affine_select(out=identf[:], in_=identf[:], compare_op=ALU.not_equal, fill=1.0, base=0,
                               pattern=[[-1, P]], channel_multiplier=1).then_inc(s["s_wif0"], 1)
            pool.wait_ge(s["s_wif0"], 3)
            pool.tensor_copy(identb[:], identf[:]).then_inc(s["s_const"], 1)
            ln_rstds(0)
            ln_rstds(1)
            pool.wait_ge(s["s_zero"], 16)
            for t in range(NT):
                if t % TB == 0:
                    pool.wait_ge(s["s_slot"], t // TB + 1)
                for k in range(K):
                    pool.indirect_dma_start(out=xg_dram, out_offset=bass.IndirectOffsetOnAxis(slot[:, t, k:k + 1], 0),
                                            in_=HN[:, t, :], in_offset=None, bounds_check=SLOTS - 1,
                                            oob_is_err=False).then_inc(s["s_scat"], 16)
            pool.tensor_copy(kparts[:, 0], CT[:]).then_inc(s["s_kp"], 1)
            pool.wait_ge(s["s_kp"], 1)
            pool.tensor_tensor(krest, CT[:], kparts[:, 0], ALU.subtract).then_inc(s["s_kp"], 1)
            pool.wait_ge(s["s_kp"], 2)
            pool.tensor_copy(kparts[:, 1], krest).then_inc(s["s_kp"], 1)
            pool.wait_ge(s["s_kp"], 3)
            pool.tensor_tensor(kparts[:, 2], krest, kparts[:, 1], ALU.subtract).then_inc(s["s_kp"], 1)
            pool.wait_ge(s["s_kp"], 4)
            pool.memset(G4, 0.0).then_inc(s["s_g0"], 1)
            pool.wait_ge(s["s_g0"], 1)
            for q in range(4):
                pool.wait_ge(s_ys[q], 16 * ST // 4)
            for t in range(NT):
                q = t % 2
                if t == 2:
                    pool.wait_ge(s["s_ysh"], B)
                    pool.memset(vpad, 0.0)
                    pool.memset(V1[:, :, :, DH:17], 1.0).then_inc(s["s_ones"], 1)
                if t >= 2:
                    pool.wait_ge(s["s_gx"], t - 1)
                for k in range(K):
                    pool.indirect_dma_start(out=G4[:, q, k, :], out_offset=None, in_=y_dram,
                                            in_offset=bass.IndirectOffsetOnAxis(slot[:, t, k:k + 1], 0),
                                            bounds_check=SLOTS - 1, oob_is_err=False).then_inc(s_gat[q], 16)
                if t >= 2 and t % 2 == 0:
                    ln_rstd(t // 2 - 1, 2 * B + t // 2)
            ln_rstd(B - 1, 3 * B)

            for b in range(B):
                pool.wait_ge(s["s_v16"], b + 1)
                pool.tensor_tensor(rs[:], vr[:], neghalf[:], ALU.pow).then_inc(s["s_r16"], 1)
                if b < B - 1:
                    ln_rstd(b, 3 * B + b + 1)
            for step, b in PLAN["G"]:
                if step in STATS:
                    ln_rstd(b, BEFORE + nth("V", STATS, step, b))
                if step in QUANTS:
                    pool.wait_ge(s["s_xf"], nth("S", QUANTS, step, b))
                    pool.tensor_scalar(XQ[:, b], HN[:, TB * b:TB * (b + 1), :], -MAGIC, None, ALU.add)\
                        .then_inc(s["s_qn"], 1)

        @block.vector
        def _(dve):
            chain = [0]

            def mark(ins):
                chain[0] += 1
                ins.then_inc(s["s_vec"], 1)
                return chain[0]

            def link(ins):
                dve.wait_ge(s["s_vec"], mark(ins))

            def xb(b):
                return X[:, TB * b:TB * (b + 1), :]

            def ln_stats(b):
                for j in range(TB):
                    last = dve.bn_stats(bnst[:, j, :], X[:, TB * b + j, :])
                link(last)
                for j in range(TB):
                    last = dve.bn_aggr(mv[:, b, j, :], bnst[:, j, :])
                link(last)
                dve.tensor_scalar(ve[:, b, :], mv[:, b, :, 1], 1e-5, None, ALU.add).then_inc(s["s_lnvar"], 1)

            def ln_norm(b, count):
                dve.wait_ge(s["s_lnrstd"], count)
                for j in range(TB):
                    last = dve.tensor_scalar(HN[:, TB * b + j, :], X[:, TB * b + j, :], mv[:, b, j, 0:1],
                                             rstd[:, b, j:j + 1], ALU.subtract, ALU.mult)
                last.then_inc(s["s_norm"], 1)

            landed(dve, "tokb")
            g1, g2 = ge[:, 0, :], ge[:, 1, :]
            dve.tensor_scalar(g1, tokb, float(PER), None, ALU.is_ge)
            dve.tensor_scalar(g2, tokb, float(2 * PER), None, ALU.is_ge)
            link(dve.tensor_scalar(maskb[:, 3, :], tokb, float(3 * PER), None, ALU.is_ge))
            dve.tensor_scalar(maskb[:, 0, :], g1, -1.0, 1.0, ALU.mult, ALU.add)
            dve.tensor_tensor(maskb[:, 1, :], g1, g2, ALU.subtract)
            link(dve.tensor_tensor(maskb[:, 2, :], g2, maskb[:, 3, :], ALU.subtract))
            for b in range(B):
                landed(dve, f"x{b}")
                ln_stats(b)
                if b >= 1:
                    ln_norm(b - 1, 0 * B + b - 1 + 1)
            ln_norm(B - 1, 0 * B + B - 1 + 1)

            def masked(out_, in_, b):
                m = maskb[:, :, S * b:S * (b + 1)].unsqueeze(2).broadcast_to([P, E0, KD, S])
                i = in_.unsqueeze(1).broadcast_to([P, E0, KD, S])
                return dve.tensor_tensor(out_, i, m, ALU.mult)

            def masked_in(b):
                dve.wait_ge(s["s_ht"], b + 1)
                if b >= 2:
                    dve.wait_ge(s["s_z"], b - 1)
                masked(hm[b % 2], HT[:, :, S * b:S * (b + 1)], b).then_inc(s["s_hm"], 1)

            def masked_hidden(b):
                q = b % 2
                dve.wait_ge(s["s_silu"], b + 1)
                link(dve.tensor_tensor(gz[q], gz[q], bank_a(b)[:], ALU.mult))
                if b >= 2:
                    dve.wait_ge(s["s_y0"], b - 1)
                masked(gm[q], pair(gz[q]), b).then_inc(s["s_gm"], 1)

            def add_gated(b, src, g):
                link(dve.scalar_tensor_tensor(out=xb(b), in0=pair(src), scalar=tg[:, g:g + 1], in1=xb(b),
                                              op0=ALU.mult, op1=ALU.add))

            masked_in(0)
            masked_in(1)
            dve.wait_ge(s["s_tanh"], 1)
            for b in range(B + 1):
                if b < B:
                    masked_hidden(b)
                if b + 2 < B:
                    masked_in(b + 2)
                if b >= 1:
                    dve.wait_ge(s["s_y0"], b)
                    add_gated(b - 1, bank_b(b - 1)[:], 0)
                    ln_stats(b - 1)
                if b >= 2:
                    ln_norm(b - 2, 1 * B + b - 2 + 1)
            ln_norm(B - 1, 1 * B + B - 1 + 1)
            landed(dve, "router")

            def route(b):
                t0, t1 = TB * b, TB * (b + 1)
                dve.wait_ge(s["s_lg"], min(b, 1) + 1)
                if b >= 1:
                    dve.wait_ge(s["s_ex"], b)
                link(dve.tensor_copy(lg[:], pair(logits(b))))
                dve.tensor_tensor(lgb[:], lg[:], rbias[:].unsqueeze(1).broadcast_to([P, TB, E]), ALU.add)
                link(dve.tensor_reduce(nmax[:], lg[:], AX.X, ALU.max, negate=True))
                for j in range(TB):
                    last = dve.max(top[:, j, :], lgb[:, j, :])
                last.then_inc(s["s_nmax"], 1)
                dve.wait_ge(s["s_nmax"], b + 1)
                for j in range(TB):
                    last = dve.max_index(topi[:, j, :], top[:, j, :], lgb[:, j, :])
                link(last)
                link(dve.tensor_copy(pick[:], topi[:, :, 0:K]))
                for j in range(TB):
                    last = dve.tensor_tensor(oh[:, t0 + j], iota64[:].unsqueeze(1).broadcast_to([P, K, E]),
                                             pick[:, j, :].unsqueeze(2).broadcast_to([P, K, E]), ALU.is_equal)
                link(last)
                with nc.allow_low_precision(reason="sums of at most 4 zeros and ones"):
                    link(dve.tensor_reduce(chosen[:, t0:t1, :], oh[:, t0:t1].rearrange("p j k e -> p j e k"),
                                           AX.X, ALU.add))
                link(dve.tensor_tensor(earlier[:, t0 + 1, :], earlier[:, t0, :], chosen[:, t0, :], ALU.add))
                dve.tensor_tensor(earlier[:, t0 + 2, :], earlier[:, t0 + 1, :], chosen[:, t0 + 1, :], ALU.add)\
                    .then_inc(s["s_m"], 1)
                dve.wait_ge(s["s_m"], b + 1)

            def pick_weights(b):
                t0, t1 = TB * b, TB * (b + 1)
                dve.wait_ge(s["s_ex"], b + 1)
                for j in range(TB):
                    last = dve.tensor_tensor(ohx[:, K * j:K * (j + 1), :], oh[:, t0 + j],
                                             ex[:, t0 + j, :].unsqueeze(1).broadcast_to([P, K, E]), ALU.mult)
                link(last)
                link(dve.tensor_reduce(wk4[:].rearrange("p j k -> p (j k)"), ohx, AX.X, ALU.add))
                link(dve.tensor_reduce(wsum[:], wk4[:], AX.X, ALU.add))
                link(dve.reciprocal(wsum[:], wsum[:]))
                for j in range(TB):
                    last = dve.tensor_scalar(W4[:, t0 + j, :], wk4[:, j, :], wsum[:, j:j + 1], tg[:, 4:5],
                                             ALU.mult, ALU.mult)
                link(last)
                link(dve.scalar_tensor_tensor(out=W4[:, t0:t1, :], in0=slotf[:, t0:t1, :], scalar=float(SLOTS),
                                              in1=W4[:, t0:t1, :], op0=ALU.is_lt, op1=ALU.mult))

            def places(b):
                t0, t1 = TB * b, TB * (b + 1)
                dve.wait_ge(s["s_count"], b + 1)
                cnt = pair(bank[6][:, 0:TB * E])
                dve.tensor_scalar(far[:], cnt, float(CAP), FAR, ALU.is_ge, ALU.mult)
                link(dve.tensor_tensor(val[:], cnt, eoff[:].unsqueeze(1).broadcast_to([P, TB, E]), ALU.add))
                link(dve.tensor_tensor(val[:], val[:], far[:], ALU.add))
                for j in range(TB):
                    last = dve.tensor_tensor(ohx[:, K * j:K * (j + 1), :], oh[:, t0 + j],
                                             val[:, j, :].unsqueeze(1).broadcast_to([P, K, E]), ALU.mult)
                link(last)
                link(dve.tensor_reduce(slotf[:, t0:t1, :].rearrange("p j k -> p (j k)"), ohx, AX.X, ALU.add))
                dve.tensor_copy(slot[:, t0:t1, :], slotf[:, t0:t1, :]).then_inc(s["s_slot"], 1)

            def shared_hidden(i):
                c, f, q = i // NF, i % NF, i % 3
                dve.wait_ge(s["s_ssl"], i + 1)
                dve.tensor_tensor(HS[:, f, 512 * c:512 * (c + 1)], SSL[:, i % 2, :], bank[3 + q][:],
                                  ALU.mult).then_inc(s["s_hs"], 1)

            for b in range(B):
                route(b)
                places(b)
                shared_hidden(b)
            for b in range(B):
                pick_weights(b)
                shared_hidden(B + b)
            dve.wait_ge(s["s_const"], 1)
            link(dve.tensor_tensor(selc[:], identb[:, 0:NH], identb[:, 32:32 + NH], ALU.add))
            link(dve.tensor_tensor(selc[:], selc[:], identb[:, 64:64 + NH], ALU.add))
            dve.tensor_copy(sel[:], selc[:].unsqueeze(2).broadcast_to([P, NH, P])).then_inc(s["s_sel"], 1)
            def add_shared(b):
                dve.wait_ge(s["s_ysh"], b + 1)
                dve.scalar_tensor_tensor(out=xb(b), in0=pair(bank[6 + b % 2][:]), scalar=tg[:, 4:5], in1=xb(b),
                                         op0=ALU.mult, op1=ALU.add).then_inc(s["s_xsh"], 1)

            for t in range(ST):
                q = t % 2
                dve.wait_ge(s["s_esil"], t + 1)
                if t >= 2:
                    dve.wait_ge(s["s_ey"], t - 1)
                for h in range(2):
                    r = slice(F * h, F * (h + 1))
                    cols = slice(CAP * h, CAP * (h + 1))
                    last = dve.tensor_tensor(he[r, q, :, cols], pair(sil[:, q, :])[r, :, cols],
                                             pair(bank[2 + q][:, P:2 * P])[r, :, cols], ALU.mult)
                last.then_inc(s["s_he"], 1)
                if t % (2 * TB) == 0 and t > 0:
                    add_shared(t // (2 * TB) - 1)

            add_shared(B - 1)

            def gathered(t):
                dve.wait_ge(s_gat[t % 2], 16 * K * (t // 2 + 1))
                for k in range(K):
                    last = dve.scalar_tensor_tensor(out=X[:, t, :], in0=G4[:, t % 2, k, :], scalar=W4[:, t, k:k + 1],
                                                    in1=X[:, t, :], op0=ALU.mult, op1=ALU.add)
                    if k < K - 1:
                        link(last)
                last.then_inc(s["s_gx"], 1)
                dve.wait_ge(s["s_gx"], t + 1)

            def forget_rows(r):
                p0, p1 = PART[r]
                dve.wait_ge(s["s_gate"], (1, 2, 4)[r])
                link(dve.tensor_scalar(fgt[p0:p1], bank[1][p0:p1, S:2 * S], bif[p0:p1, 1:2], None, ALU.add))
                dve.scalar_tensor_tensor(out=nf[p0:p1], in0=fgt[p0:p1], scalar=-1.0, in1=fgt[p0:p1],
                                         op0=ALU.mult, op1=ALU.min).then_inc(s["s_nf"], 1)

            def sum_rows(r):
                p0, p1 = PART[r]
                dve.wait_ge(s["s_ln"], r + 1)
                link(dve.scalar_tensor_tensor(out=lf[p0:p1], in0=fgt[p0:p1], scalar=0.0, in1=e1[p0:p1],
                                              op0=ALU.min, op1=ALU.subtract))
                link(dve.tensor_tensor_scan(Fc[p0:p1], lf[p0:p1], zer[p0:p1], 0.0, ALU.add, ALU.add))

            def max_rows(r):
                p0, p1 = PART[r]
                link(dve.scalar_tensor_tensor(out=ga[p0:p1], in0=bank[1][p0:p1, 0:S], scalar=bif[p0:p1, 0:1],
                                              in1=Fc[p0:p1], op0=ALU.add, op1=ALU.subtract))
                link(dve.tensor_tensor_scan(cm[p0:p1], ga[p0:p1], ga[p0:p1], LOWEST, ALU.max, ALU.max))
                dve.tensor_tensor(Fc[p0:p1], Fc[p0:p1], cm[p0:p1], ALU.add).then_inc(s["s_m1"], 1)

            def part_rows(r):
                p0, p1 = PART[r]
                link(dve.tensor_scalar(part[p0:p1, 0, :], cm[p0:p1], -1.0, None, ALU.mult))
                link(dve.scalar_tensor_tensor(out=lf[p0:p1], in0=cm[p0:p1], scalar=-1.0, in1=part[p0:p1, 0, :],
                                              op0=ALU.mult, op1=ALU.subtract))
                link(dve.tensor_copy(part[p0:p1, 1, :], lf[p0:p1]))
                link(dve.tensor_tensor(lf[p0:p1], lf[p0:p1], part[p0:p1, 1, :], ALU.subtract))
                dve.tensor_copy(part[p0:p1, 2, :], lf[p0:p1]).then_inc(s["s_part"], 1)

            def part_queries(b):
                q, h, rest = qparts[b % 2], HT[:, :, S * b:S * (b + 1)], HN[:, TB * b:TB * (b + 1), :]
                dve.wait_ge(s["s_ht"], 2 * B + b + 1)
                if b == 0:
                    dve.wait_ge(s["s_kst"], 48)
                if b >= 2:
                    dve.wait_ge(s["s_qst"], 48 * (b - 1))
                for n, (out_, in0, in1) in enumerate(((q[:, 0], h, None), (rest, h, q[:, 0]), (q[:, 1], rest, None),
                                                      (q[:, 2], rest, q[:, 1]))):
                    if n >= 1:
                        dve.wait_ge(s["s_qp"], 4 * b + n)
                    if in1 is None:
                        dve.tensor_copy(out_, in0).then_inc(s["s_qp"], 1)
                    else:
                        dve.tensor_tensor(out_, in0, in1, ALU.subtract).then_inc(s["s_qp"], 1)

            landed(dve, "small")
            link(dve.tensor_scalar(lns[:], lns[:], tg[:, 1:2], None, ALU.mult))
            gathered(0)
            gathered(1)
            ln_stats(0)
            gathered(2)
            ln_norm(0, 2 * B + 0 + 1)
            gathered(3)
            ln_stats(1)
            forget_rows(0)
            part_queries(0)
            ln_norm(1, 2 * B + 1 + 1)
            sum_rows(0)
            max_rows(0)
            part_rows(0)
            gathered(4)

            def heads_norm(b, step):
                wide = ab[:].unsqueeze(2).broadcast_to([P, TB * NH, DH])
                if step == 0:
                    dve.wait_ge(s["s_hr16"], b + 1)
                    sums = HR[:, :, DH]
                    link(dve.scalar_tensor_tensor(out=ab[:], in0=sums, scalar=-1.0, in1=sums, op0=ALU.mult,
                                                  op1=ALU.max))
                    link(dve.tensor_tensor(pair(ab[:]), pair(ab[:]), ATN[:, TB:2 * TB, 32 * b:32 * b + NH], ALU.max))
                    link(dve.tensor_scalar(ab[:], ab[:], 1e-6, None, ALU.add))
                    link(dve.reciprocal(ab[:], ab[:]))
                elif step == 1:
                    link(dve.tensor_tensor(hh, HR[:, :, 0:DH], wide, ALU.mult))
                    link(dve.tensor_reduce(mu[:], hh, AX.X, ALU.add))
                    link(dve.tensor_scalar(mu[:], mu[:], 1.0 / DH, None, ALU.mult))
                elif step == 2:
                    link(dve.tensor_tensor(hh, hh, mu[:].unsqueeze(2).broadcast_to([P, TB * NH, DH]), ALU.subtract))
                    link(dve.tensor_tensor(sq, hh, hh, ALU.mult))
                elif step == 3:
                    link(dve.tensor_reduce(vr[:], sq, AX.X, ALU.add))
                    dve.tensor_scalar(vr[:], vr[:], 1.0 / DH, 1e-6, ALU.mult, ALU.add).then_inc(s["s_v16"], 1)
                elif step == 4:
                    dve.wait_ge(s["s_r16"], b + 1)
                    link(dve.tensor_tensor(hh, hh, rs[:].unsqueeze(2).broadcast_to([P, TB * NH, DH]), ALU.mult))
                    link(dve.tensor_tensor(pair(hhf), pair(hhf), lns[:].unsqueeze(1).broadcast_to([P, TB, D]), ALU.mult))
                elif step == 5:
                    link(dve.tensor_tensor(xb(b), xb(b), pair(hhf), ALU.add))
                    ln_stats(b)
                elif step == 6:
                    ln_norm(b, 3 * B + b + 1)

            for i in range(B * NH):
                b, h = i // NH, i % NH
                dve.wait_ge(s["s_dexp"], i + 1)
                if i >= 3:
                    dve.wait_ge(s["s_pv"], i - 2)
                dve.scalar_tensor_tensor(out=dcs[:, 2 + i % 3, :], in0=bank[4 + i % 2][:, 0:384], scalar=DH ** -0.5,
                                         in1=dcs[:, i % 2, :], op0=ALU.mult, op1=ALU.mult).then_inc(s["s_cs"], 1)
                for r in (1, 2):
                    if i == FORGET[r]:
                        forget_rows(r)
                    if i == FORGET[r] + 2:
                        sum_rows(r)
                    if i == FORGET[r] + 3:
                        max_rows(r)
                    if i == FORGET[r] + 4:
                        part_rows(r)
                if i in GATHER:
                    gathered(5 + GATHER.index(i))
                    if i != GATHER[1]:
                        ln_stats(2 + GATHER.index(i) // 2)
                if i in TURN:
                    ln_norm(2 + TURN.index(i), 2 * B + 2 + TURN.index(i) + 1)
                if i in SPLIT:
                    part_queries(1 + SPLIT.index(i))
                if b >= 1 and h in HEADS_NORM:
                    heads_norm(b - 1, HEADS_NORM.index(h))
                if b >= 2 and h == 0:
                    heads_norm(b - 2, 6)
                if i == SCALES:
                    dve.wait_ge(s["s_wtot"], 1)
                    link(dve.tensor_reduce(wsc[:], pair(bank[0][:, 0:NW], NQ), AX.X, ALU.add))
                    link(dve.tensor_scalar(wsc[:], wsc[:], 1.0 / (NI * D), 1e-5, ALU.mult, ALU.add))
                    dve.reciprocal(wrec[:], wsc[:]).then_inc(s["s_wsc"], 1)
                if CLIPPED <= i < CLIPPED + NW:
                    w = i - CLIPPED
                    dve.wait_ge(s["s_wr"], w + 1)
                    dve.tensor_scalar(half(RAW, w), half(RAW, w), MAGIC + 1.0, MAGIC - 1.0, ALU.min, ALU.max)\
                        .then_inc(s["s_wc"], 1)
            heads_norm(B - 2, 6)
            for step in range(4):
                heads_norm(B - 1, step)

            def add_scaled(b, src):
                for j in range(TB):
                    t = TB * b + j
                    last = dve.scalar_tensor_tensor(out=X[:, t, :], in0=src[:, D * j:D * (j + 1)],
                                                    scalar=sum2[:, b, j:j + 1], in1=X[:, t, :], op0=ALU.mult,
                                                    op1=ALU.add)
                link(last)

            def quantise_tokens(b, f):
                t0, t1 = TB * b, TB * (b + 1)
                link(dve.tensor_reduce(amax[:], HN[:, t0:t1, :], AX.X, ALU.max, apply_absolute_value=True))
                if f == 0:
                    link(dve.tensor_scalar(sx[:, t0:t1], amax[:], 1.0 / 127.0, 1e-5, ALU.mult, ALU.add))
                else:
                    link(dve.tensor_scalar(sx[:, t0:t1], amax[:], 1e-5, 1.0 / 127.0, ALU.max, ALU.mult))
                for w in range(2 - f):
                    dve.tensor_scalar(fg[:, t0:t1, w], sx[:, t0:t1], wsc[:, 3 * f + w:3 * f + w + 1], None, ALU.mult)
                dve.reciprocal(rq[:, t0:t1], sx[:, t0:t1]).then_inc(s["s_qs"], 1)

            def hidden_scale(b, f):
                w = slice(b, b + 1)
                if f == 0:
                    link(dve.tensor_reduce(am1[:, w], H[b], AX.X, ALU.max, apply_absolute_value=True))
                    link(dve.tensor_scalar(sh1[:, w], am1[:, w], 1.0 / 127.0, 1e-5, ALU.mult, ALU.add))
                else:
                    link(dve.tensor_reduce(am1[:, w], GS[b], AX.X, ALU.max))
                    link(dve.tensor_tensor(am1[:, w], am1[:, w], am1[:, w], ALU.mult))
                    link(dve.tensor_scalar(sh1[:, w], am1[:, w], 1e-5, 1.0 / 127.0, ALU.max, ALU.mult))
                dve.reciprocal(rh1[:, w], sh1[:, w]).then_inc(s["s_rh"], 1)
                link(dve.tensor_scalar(fy1[:, w], sh1[:, w], wsc[:, 2 + 2 * f:3 + 2 * f], tg[:, 6 + f:7 + f],
                                       ALU.mult, ALU.mult))

            dve.wait_ge(s["s_mixe"], 1)
            link(dve.tensor_scalar(coef[:], alpha[:], mix[:, 0:1], None, ALU.mult))
            link(dve.tensor_scalar(cf2[:], alpha[:], -1.0, 1.0, ALU.mult, ALU.add))
            link(dve.scalar_tensor_tensor(out=coef[:], in0=cf2[:], scalar=mix[:, 1:2], in1=coef[:],
                                          op0=ALU.mult, op1=ALU.add))
            dve.tensor_scalar(coef[:], coef[:], D ** -0.5, mix[:, 3:4], ALU.mult, ALU.mult).then_inc(s["s_coef"], 1)

            for step, b in PLAN["V"]:
                if step == "heads":
                    for last in range(4, 6):
                        heads_norm(b, last)
                if step in NORMS:
                    ln_norm(b, BEFORE + nth("G", STATS, STATS[NORMS.index(step)], b))
                if step == "route1":
                    dve.wait_ge(s["s_l1"], nth("T", ["route1"], step, b))
                    link(dve.tensor_copy(lg1[:, b], pair(bank_a(b)[:, 0:TB * E1])))
                    dve.tensor_reduce(nmax1[:, b], lg1[:, b], AX.X, ALU.max, negate=True)
                    for j in range(TB):
                        last = dve.max(top1[:, j, :], lg1[:, b, j, :])
                    last.then_inc(s["s_nm1"], 1)
                    dve.wait_ge(s["s_nm1"], nth("V", ["route1"], step, b))
                    for j in range(TB):
                        last = dve.max_index(topi1[:, j, :], top1[:, j, :], lg1[:, b, j, :])
                    link(last)
                    link(dve.tensor_copy(pick1[:], topi1[:, :, 0]))
                    link(dve.tensor_tensor(MK[:, b], iota64[:, 0:E1].unsqueeze(1).broadcast_to([P, TB, E1]),
                                           pick1[:].unsqueeze(2).broadcast_to([P, TB, E1]), ALU.is_equal))
                if step == "low1":
                    dve.wait_ge(s["s_ex1"], nth("S", ["route1"], "route1", b))
                    link(dve.reciprocal(sum1[:, b], sum1[:, b]))
                    link(dve.tensor_scalar(sum1[:, b], sum1[:, b], 64.0 / 16.0, tg[:, 5:6], ALU.mult, ALU.mult))
                    link(dve.tensor_tensor(MK[:, b], MK[:, b], sum1[:, b].unsqueeze(2).broadcast_to([P, TB, E1]),
                                           ALU.mult))
                    dve.wait_ge(s["s_ha"], nth("T", ["low1"], step, b))
                    for j in range(TB):
                        last = dve.tensor_tensor(pair(HM1[b][:, j, :], E1), pair(bank[2 * b + j][:], E1),
                                                 MK[:, b, j, :].unsqueeze(2).broadcast_to([P, E1, R1]), ALU.mult)
                    last.then_inc(s["s_hm1"], 1)
                if step == "lowout1":
                    dve.wait_ge(s["s_y1"], nth("T", ["lowout1"], step, b))
                    link(dve.tensor_tensor(xb(b), xb(b), pair(bank_a(b)[:]), ALU.add))
                    ln_stats(b)
                if step == "scores2":
                    dve.wait_ge(s["s_sc2"], nth("T", ["scores2"], step, b))
                    for j in range(TB):
                        last = dve.tensor_reduce(nmax2[:, b, j:j + 1], bank[2 * b + j][:], AX.X, ALU.max, negate=True)
                    link(last)
                    dve.tensor_scalar(nmax2[:, b], nmax2[:, b], D ** -0.5, None, ALU.mult).then_inc(s["s_nm2"], 1)
                if step == "project2":
                    link(dve.reciprocal(sum2[:, b], sum2[:, b]))
                    link(dve.tensor_scalar(sum2[:, b], sum2[:, b], tg[:, 2:3], None, ALU.mult))
                    dve.wait_ge(s["s_y2"], nth("T", ["project2"], step, b))
                    add_scaled(b, bank_b(b))
                    ln_stats(b)
                if step in ("norm5", "norm7"):
                    dve.wait_ge(s["s_norm"], BEFORE + nth("V", NORMS, step, b))
                    quantise_tokens(b, ("norm5", "norm7").index(step))
                if step[0] in ("in2a", "in2b"):
                    n = ("in2a", "in2b").index(step[0])
                    dve.wait_ge(s["s_gs"], nth("S", INS, step, b))
                    dve.scalar_tensor_tensor(out=H[b][:, 512 * n:512 * (n + 1)], in0=bank_b(b)[:],
                                             scalar=fg[:, TB * b + step[1], 1:2],
                                             in1=GS[b][:, 512 * n:512 * (n + 1)], op0=ALU.mult, op1=ALU.mult)\
                        .then_inc(s_hmg, 1)
                    if n == 1:
                        dve.wait_ge(s_hmg, nth("V", IN2, step, b))
                        hidden_scale(b, 0)
                if step[0] == "in3":
                    dve.wait_ge(s["s_gs"], nth("S", INS, step, b))
                    hidden_scale(b, 1)
                if step in ROUNDS:
                    dve.wait_ge(s["s_hr"], nth("S", ROUNDS, step, b))
                    dve.tensor_scalar(HQ[b], H[b], -MAGIC, None, ALU.add).then_inc(s["s_hq"], 1)
                if step in OUTS:
                    t = TB * b + step[1]
                    dve.wait_ge(s["s_yq"], nth("T", OUTS, step, b))
                    last = dve.scalar_tensor_tensor(out=X[:, t, :], in0=bank_b(b)[:, 0:D], scalar=fy1[:, b:b + 1],
                                                    in1=X[:, t, :], op0=ALU.mult, op1=ALU.add)
                    if step[0] == "out3":
                        last.then_inc(s["s_xout"], 1)
                    else:
                        last.then_inc(s["s_xq"], 1)
                        dve.wait_ge(s["s_xq"], nth("V", OUT2, step, b))
                        if step[1] == TB - 1:
                            ln_stats(b)
                if step == "scores3":
                    dve.wait_ge(s["s_sl3"], nth("S", ["scores3"], step, b))
                    for j in range(TB):
                        last = dve.max(top3[:, b, j, :], SC[b][:, j, :])
                    link(last)
                    link(dve.tensor_scalar(nmax2[:, b], top3[:, b, :, 0], -1.0, None, ALU.mult))
                    for j in range(TB):
                        dve.tensor_scalar(top3[:, b, j, :], top3[:, b, j, :], nmax2[:, b, j:j + 1], None, ALU.add)
                    for j in range(TB):
                        last = dve.tensor_scalar(SC[b][:, j, :], SC[b][:, j, :], nmax2[:, b, j:j + 1], None, ALU.add)
                    last.then_inc(s["s_m3"], 1)
                if step == "clip3":
                    dve.wait_ge(s["s_m3"], nth("V", ["scores3"], "scores3", b))
                    done = [0] * TB
                    for r in range((CLIP + 7) // 8 - 1):
                        src = SC[b] if r == 0 else WR[b]
                        for j in range(TB):
                            if r >= 1:
                                dve.wait_ge(s["s_vec"], done[j])
                            done[j] = mark(dve.match_replace(WR[b][:, j, :], top3[:, b, j, :], src[:, j, :], LOWEST))
                        for j in range(TB):
                            dve.wait_ge(s["s_vec"], done[j])
                            done[j] = mark(dve.max(top3[:, b, j, :], WR[b][:, j, :]))
                    dve.wait_ge(s["s_ex3"], nth("S", ["clip3"], step, b))
                    at = (CLIP - 1) % 8
                    for j in range(TB):
                        dve.wait_ge(s["s_vec"], done[j])
                        last = dve.scalar_tensor_tensor(out=P3[b][:, j, :], in0=SC[b][:, j, :],
                                                        scalar=top3[:, b, j, at:at + 1], in1=EX3[b][:, j, :],
                                                        op0=ALU.is_ge, op1=ALU.mult)
                    last.then_inc(s["s_p3"], 1)
                    dve.wait_ge(s["s_p3"], nth("V", ["clip3"], step, b))
                    link(dve.tensor_reduce(sum2[:, b], P3[b], AX.X, ALU.add))
                    link(dve.reciprocal(sum2[:, b], sum2[:, b]))
                    link(dve.tensor_scalar(sum2[:, b], sum2[:, b], tg[:, 3:4], None, ALU.mult))
                if step == "project3":
                    dve.wait_ge(s["s_y3"], nth("T", ["project3"], step, b))
                    add_scaled(b, bank_b(b))
                    ln_stats(b)

        @block.scalar
        def _(act):
            def turned_copy(u, src, b=None):
                if b is None:
                    b = u % B
                act.wait_ge(s["s_turned"], u + 1)
                act.activation(HT[:, :, S * b:S * (b + 1)], pair(src[:]), ACT.Copy).then_inc(s["s_ht"], 1)

            landed(act, "g")
            act.activation(tg[:], gates8[:], ACT.Tanh).then_inc(s["s_tanh"], 1)
            for b in range(B):
                turned_copy(b, bank_a(b))
            for b in range(B):
                q = b % 2
                act.wait_ge(s["s_z"], b + 1)
                if b >= 2:
                    act.wait_ge(s["s_gm"], b - 1)
                act.activation(gz[q], bank_a(b)[:], ACT.Silu).then_inc(s["s_silu"], 1)
            for b in range(B):
                turned_copy(B + b, bank[b])

            def route_exp(b):
                act.wait_ge(s["s_nmax"], b + 1)
                for j in range(TB):
                    last = act.activation(ex[:, TB * b + j, :], lg[:, j, :], ACT.Exp, bias=nmax[:, j:j + 1])
                last.then_inc(s["s_ex"], 1)

            def shared_silu(i):
                act.wait_ge(s["s_hsg"], i + 1)
                if i >= 2:
                    act.wait_ge(s["s_hs"], i - 1)
                act.activation(SSL[:, i % 2, :], bank[i % 3][:], ACT.Silu).then_inc(s["s_ssl"], 1)

            for b in range(B):
                route_exp(b)
                shared_silu(b)
            for i in range(B, 2 * NF):
                shared_silu(i)
            for t in range(ST + 2):
                if t < ST:
                    q = t % 2
                    act.wait_ge(s["s_xgturned"], t + 1)
                    if t >= 2:
                        act.wait_ge(s["s_egu"], t - 1)
                    act.activation(xgT[:, q], pair(bank[q][:, 0:D]), ACT.Copy).then_inc(s["s_xgT"], 1)
                if 1 <= t <= ST:
                    q = (t - 1) % 2
                    act.wait_ge(s["s_egu"], t)
                    if t >= 3:
                        act.wait_ge(s["s_he"], t - 2)
                    act.activation(sil[:, q, :], bank[2 + q][:, 0:P], ACT.Silu).then_inc(s["s_esil"], 1)
                if t >= 2:
                    r = t - 2
                    act.wait_ge(s["s_ey"], r + 1)
                    if r >= 4:
                        act.wait_ge(s_ys[r % 4], 16 * (r // 4))
                    act.activation(ye[:, r % 4, :], bank[4 + r % 2][:, 0:D], ACT.Copy).then_inc(s["s_ye"], 1)

            act.wait_ge(s["s_ysh"], B)
            landed(act, "ctx")
            for t in range(NT):
                last = act.activation(V1[:, t, :, 0:DH], CN[:, t, :].rearrange("p (h c) -> p h c", c=DH), ACT.Copy)
            last.then_inc(s["s_v1"], 1)

            def log_rows(r):
                p0, p1 = PART[r]
                act.wait_ge(s["s_nf"], r + 1)
                act.activation(e1[p0:p1], nf[p0:p1], ACT.Exp).then_inc(s["s_e1"], 1)
                act.wait_ge(s["s_e1"], r + 1)
                act.activation(e1[p0:p1], e1[p0:p1], ACT.Ln, bias=1.0).then_inc(s["s_ln"], 1)

            def spread_rows(r):
                p0, p1 = PART[r]
                act.wait_ge(s["s_m1"], r + 1)
                act.activation(nx[p0:p1], Fc[p0:p1], ACT.Exp, scale=-1.0).then_inc(s["s_nx"], 1)
                act.wait_ge(s["s_part"], r + 1)
                for p in range(3):
                    for b in range(p0 // 32, p1 // 32):
                        last = act.activation(CMP[32 * p:32 * (p + 1), b, :], part[32 * b:32 * (b + 1), p, :],
                                              ACT.Copy)
                last.then_inc(s["s_cmp"], 1)

            def turned_rows(r):
                p0, p1 = PART[r]
                act.wait_ge(s["s_trd"], r + 1)
                act.activation(ATN[:, :, p0:p1], pair(bank[0][:], 4)[:, :, 0:p1 - p0], ACT.Copy)\
                    .then_inc(s["s_atn"], 1)

            turned_copy(2 * B, bank[0])
            log_rows(0)
            turned_copy(2 * B + 1, bank[0])
            spread_rows(0)
            turned_rows(0)
            act.wait_ge(s["s_atn"], 1)

            def heads_copy(b):
                act.wait_ge(s["s_pv"], NH * (b + 1))
                act.activation(HV[:, 0:512], bank[6][:], ACT.Copy)
                act.activation(HV[:, 512:1024], bank[7][:], ACT.Copy).then_inc(s["s_hcp"], 1)

            def heads_turned(b):
                act.wait_ge(s["s_hvt"], b + 1)
                for t in range(TB):
                    last = act.activation(HR[:, NH * t:NH * (t + 1), :], pair(bank[t][:], NH)[:, :, 0:17], ACT.Copy)
                last.then_inc(s["s_hr16"], 1)

            for i in range(B * NH):
                b, h = i // NH, i % NH
                act.wait_ge(s["s_dq"], i + 1)
                if h == 0 and b >= 1:
                    act.wait_ge(s["s_atn"], (2, 3, 3)[b - 1])
                if i >= 2:
                    act.wait_ge(s["s_cs"], i - 1)
                act.activation(dcs[:, i % 2, 0:S], bank[2 + i % 2][:, 0:S], ACT.Exp,
                               bias=ATN[:, 0, 32 * b + h:32 * b + h + 1])
                act.activation(dcs[:, i % 2, S:384], bank[2 + i % 2][:, S:384], ACT.Exp,
                               bias=ATN[:, 1, 32 * b + h:32 * b + h + 1]).then_inc(s["s_dexp"], 1)
                if i >= NH and h == 1:
                    heads_copy(b - 1)
                if i >= NH and h == 4:
                    heads_turned(b - 1)
                for r in (1, 2):
                    if i == FORGET[r] + 1:
                        log_rows(r)
                    if i == FORGET[r] + 5:
                        spread_rows(r)
                    if i == FORGET[r] + 7:
                        turned_rows(r)
                for n in range(2):
                    if i == TURN[n] + 2:
                        turned_copy(2 * B + 2 + n, bank[0])
                if b >= 2 and h == 2:
                    turned_copy(3 * B + b - 2, bank[1])
                if SUMS <= i < SUMS + NW:
                    w = i - SUMS
                    landed(act, ("q2g", "q2u", "q2d", "q3a", "q3b")[w // 2])
                    act.activation(half(QWS, w), half(RAW, w), ACT.Abs, accum_out=asum[:, w:w + 1])\
                        .then_inc(s["s_asum"], 1)
                if ROUNDED <= i < ROUNDED + NW:
                    w = i - ROUNDED
                    act.wait_ge(s["s_wsc"], 1)
                    act.activation(half(RAW, w), half(RAW, w), ACT.Identity, bias=magic[:, 0:1],
                                   scale=wrec[:, w // 2:w // 2 + 1]).then_inc(s["s_wr"], 1)
                if CAST <= i < CAST + NW:
                    w = i - CAST
                    act.wait_ge(s["s_wc"], w + 1)
                    act.activation(half(QWS, w), half(RAW, w), ACT.Identity, bias=magic[:, 1:2]).then_inc(s["s_qw"], 1)
            turned_copy(3 * B + B - 2, bank[1])
            heads_copy(B - 1)
            heads_turned(B - 1)
            act.activation(alpha[:], mix[:, 2:3], ACT.Sigmoid)
            act.activation(mix[:, 3:4], mix[:, 3:4], ACT.Exp).then_inc(s["s_mixe"], 1)
            act.wait_ge(s["s_coef"], 1)
            for step, b in PLAN["S"]:
                if step in TURNS:
                    turned_copy(BEFORE + nth("T", TURNS, step, b) - 1, bank_b(b) if step == "turn1" else bank_a(b), b)
                if step == "route1":
                    act.wait_ge(s["s_nm1"], nth("V", ["route1"], step, b))
                    for j in range(TB):
                        last = act.activation(ex1[:, b, j, :], lg1[:, b, j, :], ACT.Exp, bias=nmax1[:, b, j:j + 1],
                                              accum_out=sum1[:, b, j:j + 1])
                    last.then_inc(s["s_ex1"], 1)
                if step == "lowturn1":
                    act.wait_ge(s["s_qw"], NW)
                    act.wait_ge(s["s_hmt"], nth("T", ["lowturn1"], step, b))
                    for h in range(2):
                        last = act.activation(HMT[b][:, 2 * h:2 * h + 2, :], pair(bank[2 * b + h][:]), ACT.Copy)
                    last.then_inc(s["s_hmc"], 1)
                if step == "keys2":
                    act.wait_ge(s["s_qk"], nth("T", ["keys2"], step, b))
                    act.activation(QT[b], pair(bank_a(b)[:]), ACT.Copy)
                    act.activation(KT[b], pair(bank_b(b)[:]), ACT.Copy).then_inc(s["s_qk2"], 1)
                if step == "values2":
                    act.wait_ge(s["s_v"], nth("T", ["values2"], step, b))
                    act.activation(VN[b], pair(bank_a(b)[:]), ACT.Copy).then_inc(s["s_v2"], 1)
                if step == "scores2":
                    act.wait_ge(s["s_nm2"], nth("V", ["scores2"], step, b))
                    for j in range(TB):
                        last = act.activation(PR[b][:, j, :], bank[2 * b + j][:], ACT.Exp, bias=nmax2[:, b, j:j + 1],
                                              scale=D ** -0.5, accum_out=sum2[:, b, j:j + 1])
                    last.then_inc(s["s_ex2"], 1)
                if step == "probs2":
                    act.wait_ge(s["s_pt2"], nth("T", ["probs2"], step, b))
                    act.activation(PT[b][:, 0:TB, :], pair(bank_a(b)[:]), ACT.Copy)
                    act.activation(PT[b][:, TB:2 * TB, :], pair(bank_b(b)[:]), ACT.Copy).then_inc(s["s_ptc2"], 1)
                if step == "mix2":
                    act.wait_ge(s["s_o2"], nth("T", ["mix2"], step, b))
                    act.activation(OT[b], pair(bank_a(b)[:]), ACT.Copy).then_inc(s["s_oc2"], 1)
                if step in QUANTS:
                    act.wait_ge(s["s_qs"], nth("V", QUANTS, step, b))
                    for t in range(TB * b, TB * (b + 1)):
                        last = act.activation(HN[:, t, :], HN[:, t, :], ACT.Identity, bias=magic[:, 0:1],
                                              scale=rq[:, t:t + 1])
                    last.then_inc(s["s_xf"], 1)
                if step in QTURNS:
                    act.wait_ge(s["s_qt"], nth("T", QTURNS, step, b))
                    act.activation(XQT[:, b], pair(bank_a(b)[:, 0:S].bitcast(BF16)), ACT.Copy).then_inc(s["s_qc"], 1)
                if step[0] in ("in2a", "in2b"):
                    n = ("in2a", "in2b").index(step[0])
                    act.wait_ge(s["s_gu"], nth("T", INS, step, b))
                    act.activation(GS[b][:, 512 * n:512 * (n + 1)], bank_a(b)[:], ACT.Silu,
                                   scale=fg[:, TB * b + step[1], 0:1]).then_inc(s["s_gs"], 1)
                if step[0] == "in3":
                    act.wait_ge(s["s_gu"], nth("T", INS, step, b))
                    for n in range(2):
                        last = act.activation(GS[b][:, 512 * n:512 * (n + 1)], bank[2 * b + n][:], ACT.Relu,
                                              scale=fg[:, TB * b + step[1], 0:1])
                    last.then_inc(s["s_gs"], 1)
                    act.wait_ge(s["s_gs"], nth("S", INS, step, b))
                    act.activation(H[b], GS[b], ACT.Square).then_inc(s["s_sq"], 1)
                if step in ROUNDS:
                    if step[0] == "round3":
                        act.wait_ge(s["s_sq"], nth("S", IN3, ("in3", step[1]), b))
                    act.wait_ge(s["s_rh"], nth("V", FULL, ("in2b" if step[0] == "round2" else "in3", step[1]), b))
                    act.activation(H[b], H[b], ACT.Identity, bias=magic[:, 0:1], scale=rh1[:, b:b + 1])\
                        .then_inc(s["s_hr"], 1)
                if step in HTURNS:
                    act.wait_ge(s["s_hqt"], nth("T", HTURNS, step, b))
                    act.activation(HQT[b], pair(bank_a(b)[:].bitcast(BF16), KI), ACT.Copy).then_inc(s["s_hqc"], 1)
                if step == "queries3":
                    act.wait_ge(s["s_q3"], nth("T", ["queries3"], step, b))
                    act.activation(QT[b], pair(bank_b(b)[:]), ACT.Copy).then_inc(s["s_qc3"], 1)
                if step == "scores3":
                    act.wait_ge(s["s_sc3"], nth("T", ["scores3"], step, b))
                    act.activation(SC[b], pair(bank_a(b)[:]), ACT.Copy, scale=coef[:]).then_inc(s["s_sl3"], 1)
                if step == "clip3":
                    act.wait_ge(s["s_m3"], nth("V", ["scores3"], "scores3", b))
                    act.activation(EX3[b], SC[b], ACT.Exp).then_inc(s["s_ex3"], 1)
                if step == "probs3":
                    act.wait_ge(s["s_pt3"], nth("T", ["probs3"], step, b))
                    act.activation(PT[b][:, 0:TB, :], pair(bank_b(b)[:]), ACT.Copy).then_inc(s["s_ptc3"], 1)
                if step == "mix3":
                    act.wait_ge(s["s_o3"], nth("T", ["mix3"], step, b))
                    act.activation(OT[b], pair(bank_a(b)[:]), ACT.Copy).then_inc(s["s_oc3"], 1)

        @block.tensor
        def _(pe):
            def turn(u, dst, b=None, ln=None):
                if b is None:
                    b, ln = u % B, u + 1
                pe.wait_ge(s["s_norm"], ln)
                for k in range(KD):
                    for j in range(TB):
                        last = pe.transpose(dst[:, S * k + P * j:S * k + P * (j + 1)],
                                            HN[:, TB * b + j, P * k:P * (k + 1)], identf[:])
                last.then_inc(s["s_turned"], 1)

            def tokens(b, j, k):
                return HT[:, k, S * b + P * j:S * b + P * (j + 1)]

            pe.wait_ge(s["s_const"], 1)
            for b in range(B):
                turn(b, bank_a(b))
            landed(pe, "ctxT")

            def product_in0(b):
                pe.wait_ge(s["s_hm"], b + 1)
                for m in range(KD):
                    for e in range(E0):
                        for k in range(KD):
                            last = pe.matmul(bank_a(b)[:, S * m:S * (m + 1)],
                                             CT[:, k, S * e + P * m:S * e + P * (m + 1)], hm[b % 2][:, e, k, :],
                                             start=(e + k == 0), stop=(e == E0 - 1 and k == KD - 1))
                last.then_inc(s["s_z"], 1)

            def product_out0(b):
                pe.wait_ge(s["s_gm"], b + 1)
                for j in range(TB):
                    for e in range(E0):
                        for k in range(KD):
                            last = pe.matmul(bank_b(b)[:, D * j:D * (j + 1)],
                                             gm[b % 2][:, e, k, P * j:P * (j + 1)], CT[:, k, S * e:S * (e + 1)],
                                             start=(e + k == 0), stop=(e == E0 - 1 and k == KD - 1))
                last.then_inc(s["s_y0"], 1)

            product_in0(0)
            for b in range(1, B):
                product_in0(b)
                product_out0(b - 1)
            product_out0(B - 1)

            for b in range(B):
                turn(B + b, bank[b])
            landed(pe, "router")
            for b in range(B):
                pe.wait_ge(s["s_ht"], B + b + 1)
                for j in range(TB):
                    for k in range(KD):
                        last = pe.matmul(logits(b)[:, E * j:E * (j + 1)], tokens(b, j, k), RW[:, k, :],
                                         start=(k == 0), stop=(k == KD - 1))
                if b in (0, B - 1):
                    last.then_inc(s["s_lg"], 1)
            landed(pe, "shared")

            def shared_in(i):
                c, f, q = i // NF, i % NF, i % 3
                if i >= 3:
                    pe.wait_ge(s["s_hs"], i - 2)
                for w, bk in ((SG, 0), (SU, 3)):
                    for k in range(KD):
                        last = pe.matmul(bank[bk + q][:], w[:, k, P * f:P * (f + 1)],
                                         HT[:, k, 512 * c:512 * (c + 1)], start=(k == 0), stop=(k == KD - 1))
                last.then_inc(s["s_hsg"], 1)

            def counts(b):
                pe.wait_ge(s["s_m"], b + 1)
                if b >= 1:
                    pe.wait_ge(s["s_slot"], b)
                for j in range(TB):
                    c = bank[6][:, E * j:E * (j + 1)]
                    pe.matmul(c, before[:], chosen[:, TB * b + j, :], start=True, stop=False)
                    last = pe.matmul(c, onesb[:], earlier[:, TB * b + j, :], start=False, stop=True)
                last.then_inc(s["s_count"], 1)

            counts(0)
            shared_in(0)
            for b in range(1, B):
                shared_in(b)
                counts(b)
            for i in range(B, 2 * NF):
                shared_in(i)
            def experts_turn(t):
                q = t % 2
                pe.wait_ge(s_xg[t % 4], 16 * (t // 4 + 1))
                if t >= 2:
                    pe.wait_ge(s["s_xgT"], t - 1)
                for k in range(KD):
                    last = pe.transpose(bank[q][:, P * k:P * (k + 1)], xgt[:, t % 4, P * k:P * (k + 1)], identf[:])
                last.then_inc(s["s_xgturned"], 1)

            def experts_in(t):
                q, c, o = t % 2, t // CH, t % CH
                pe.wait_ge(s["s_xgT"], t + 1)
                if t >= 2:
                    pe.wait_ge(s["s_he"], t - 1)
                if o == 0:
                    pe.wait_ge(s_ew[c % RING], 48 * (c // RING + 1))
                for w, at in ((egw[c % RING], 0), (euw[c % RING], P)):
                    for i in range(2):
                        for k in range(KD):
                            last = pe.matmul(bank[2 + q][:, at + 64 * i:at + 64 * (i + 1)],
                                             w[:, k, 256 * o + P * i:256 * o + P * (i + 1)],
                                             xgT[:, q, k, 64 * i:64 * (i + 1)], start=(k == 0), stop=(k == KD - 1))
                last.then_inc(s["s_egu"], 1)

            def experts_out(t):
                q, c, o = t % 2, t // CH, t % CH
                pe.wait_ge(s["s_he"], t + 1)
                if t >= 2:
                    pe.wait_ge(s["s_ye"], t - 1)
                for i in range(2):
                    last = pe.matmul(bank[4 + q][64 * i:64 * (i + 1), 0:D], he[:, q, i, :],
                                     edw[c % RING][:, 2 * o + i, :], start=True, stop=True)
                last.then_inc(s["s_ey"], 1)

            def shared_out(t):
                b, j = t // 2 // TB, t // 2 % TB
                if b >= 2 and t % (2 * TB) == 0:
                    pe.wait_ge(s["s_xsh"], b - 1)
                for f in range(NF // 2 * (t % 2), NF // 2 * (t % 2 + 1)):
                    last = pe.matmul(bank[6 + b % 2][:, D * j:D * (j + 1)],
                                     HS[:, f, S * b + P * j:S * b + P * (j + 1)], SD[:, f, :],
                                     start=(f == 0), stop=(f == NF - 1))
                if (t + 1) % (2 * TB) == 0:
                    last.then_inc(s["s_ysh"], 1)

            pe.wait_ge(s["s_hs"], 2 * NF)
            for t in range(ST + 2):
                if t < ST:
                    experts_turn(t)
                    shared_out(t)
                if 1 <= t <= ST:
                    experts_in(t - 1)
                if t >= 2:
                    experts_out(t - 2)

            def gate_products(b, tiles):
                for g in range(2):
                    for kt in tiles:
                        src = HT if kt < KD else CT
                        last = pe.matmul(bank[1][32 * b:32 * (b + 1), S * g:S * (g + 1)], WIF[:, g, kt, :],
                                         src[:, kt % KD, S * b:S * (b + 1)], start=False, stop=True,
                                         skip_group_check=True)
                return last

            def gates_context(b):
                pe.matmul(bank[1][32 * b:32 * (b + 1), :], earlier[:, 0, 0:32], sel[:, 0:4, :], start=True, stop=True)
                gate_products(b, range(KD, 3 * KD))

            def gates(b):
                pe.wait_ge(s["s_ht"], 2 * B + b + 1)
                gate_products(b, range(KD)).then_inc(s["s_gate"], 1)

            def rows_turn(r):
                p0, p1 = PART[r]
                pe.wait_ge(s["s_nx"], r + 1)
                if r >= 1:
                    pe.wait_ge(s["s_atn"], r)
                for i, row in enumerate((ga, nx)):
                    for j in range(TB):
                        o = P * (TB * i + j)
                        last = pe.transpose(bank[0][:, o:o + p1 - p0], row[p0:p1, P * j:P * (j + 1)],
                                            identf[p0:p1, p0:p1])
                last.then_inc(s["s_trd"], 1)

            landed(pe, "small")
            pe.wait_ge(s["s_sel"], 1)
            pe.wait_ge(s["s_xgT"], ST)
            for b in range(B):
                gates_context(b)
            turn(2 * B, bank[0])
            gates(0)
            turn(2 * B + 1, bank[0])
            gates(1)
            rows_turn(0)
            pe.wait_ge(s["s_v1"], 1)
            pe.wait_ge(s["s_ones"], 1)

            def scores(i):
                b, h = i // NH, i % NH
                if h == 0:
                    pe.wait_ge(s_st[b % 2], 16 * 2 * len(PAIRS) * (b // 2 + 1))
                    pe.wait_ge(s["s_cmp"], (1, 2, 3, 3)[b])
                if i >= 2:
                    pe.wait_ge(s["s_dexp"], i - 1)
                    pe.wait_ge(s["s_cs"], i - 1)
                dbk, sbk = bank[2 + i % 2], bank[4 + i % 2]
                pe.matmul(dbk[:, 0:S], sel[0:96, h, :], CMP[0:96, b, :], start=True, stop=True)
                pe.matmul(dbk[:, S:384], sel[0:96, h, :], CMP[0:96, b, P:S], start=False, stop=True,
                          skip_group_check=True)
                pe.matmul(pair(dbk[:, 0:384], 3)[:, 0:3:2, :], identb[:], pair(future[:], 2), start=False, stop=True,
                          skip_group_check=True)
                k, q = KST[b % 2][:, h, :], QST[b % 2][:, h, :]
                pe.matmul(sbk[:, 0:S], k[:, 0:P], q, start=True, stop=True)
                pe.matmul(sbk[:, S:384], k[:, P:S], q[:, P:S], start=True, stop=True).then_inc(s["s_dq"], 1)

            def values(i):
                b, h = i // NH, i % NH
                pe.wait_ge(s["s_cs"], i + 1)
                if h == 0 and b >= 1:
                    pe.wait_ge(s["s_hcp"], b)
                cs = dcs[:, 2 + i % 3, :]
                q, r = h // 4, h % 4
                out_ = bank[6 + q // 2][32 * r:32 * (r + 1), S * (q % 2):S * (q % 2 + 1)]
                v = [HM[:, 17 * (NH * t + h):17 * (NH * t + h) + 32] for t in range(TB * b, TB * (b + 1))]
                pe.matmul(out_, v[0], cs[:, 0:S], start=True, stop=True)
                pe.matmul(out_[:, P:S], v[1], cs[:, S:384], start=False, stop=True, skip_group_check=True)\
                    .then_inc(s["s_pv"], 1)

            def heads_turn(b):
                pe.wait_ge(s["s_hcp"], b + 1)
                pe.wait_ge(s["s_m1"], 3)
                pe.wait_ge(s["s_atn"], 3)
                if b >= 1:
                    pe.wait_ge(s["s_wsc"], 1)
                    pe.wait_ge(s["s_ht"], 3 * B + b)
                for t in range(TB):
                    for q in range(4):
                        last = pe.transpose(bank[t][:, P * q:P * (q + 1)], HV[:, S * q + P * t:S * q + P * (t + 1)],
                                            identf[:])
                last.then_inc(s["s_hvt"], 1)

            for i in range(B * NH):
                b, h = i // NH, i % NH
                scores(i)
                if i >= 2:
                    values(i - 2)
                for n in range(2):
                    if i == TURN[n] + 2:
                        pe.wait_ge(s["s_atn"], n + 1)
                        turn(2 * B + 2 + n, bank[0])
                    if i == TURN[n] + 3:
                        gates(2 + n)
                for r in (1, 2):
                    if i == FORGET[r] + 6:
                        rows_turn(r)
                if i == SCALES - 1:
                    pe.wait_ge(s["s_hr16"], 1)
                    pe.wait_ge(s["s_asum"], NW)
                    pe.matmul(bank[0][:, 0:NW], onesf[:], asum[:], start=True, stop=True).then_inc(s["s_wtot"], 1)
                if b >= 2 and h == 2:
                    pe.wait_ge(s["s_hr16"], b - 1)
                    turn(3 * B + b - 2, bank[1])
                if b >= 1 and h == 3:
                    heads_turn(b - 1)
            values(B * NH - 2)
            values(B * NH - 1)
            pe.wait_ge(s["s_hr16"], B - 1)
            turn(3 * B + B - 2, bank[1])
            heads_turn(B - 1)
            landed(pe, "lowrank")
            pe.wait_ge(s["s_hr16"], B)
            pe.wait_ge(s["s_ht"], BEFORE)
            for step, b in PLAN["T"]:
                if step in TURNS:
                    turn(None, bank_b(b) if step == "turn1" else bank_a(b), b, BEFORE + nth("V", NORMS, step, b))
                if step == "route1":
                    if b == B - 1:
                        pe.wait_ge(s["s_ht"], BEFORE + nth("S", TURNS, "turn1", b))
                    for j in range(TB):
                        for k in range(KD):
                            last = pe.matmul(bank_a(b)[:, E1 * j:E1 * (j + 1)], tokens(b, j, k), LG[:, k, :],
                                             start=(k == 0), stop=(k == KD - 1))
                    last.then_inc(s["s_l1"], 1)
                if step == "low1":
                    pe.wait_ge(s["s_nm1"], nth("V", ["route1"], "route1", b))
                    for j in range(TB):
                        for k in range(KD):
                            last = pe.matmul(bank[2 * b + j][:], tokens(b, j, k), LA[:, k, :],
                                             start=(k == 0), stop=(k == KD - 1))
                    last.then_inc(s["s_ha"], 1)
                if step == "lowturn1":
                    pe.wait_ge(s["s_hm1"], nth("V", ["low1"], "low1", b))
                    for j in range(TB):
                        for f in range(4):
                            last = pe.transpose(bank[2 * b + f // 2][:, S * (f % 2) + P * j:S * (f % 2) + P * (j + 1)],
                                                HM1[b][:, j, P * f:P * (f + 1)], identf[:])
                    last.then_inc(s["s_hmt"], 1)
                if step == "lowout1":
                    pe.wait_ge(s["s_hmc"], nth("S", ["lowturn1"], "lowturn1", b))
                    for j in range(TB):
                        for f in range(4):
                            last = pe.matmul(bank_a(b)[:, D * j:D * (j + 1)], HMT[b][:, f, P * j:P * (j + 1)],
                                             LB[:, f, :], start=(f == 0), stop=(f == 3))
                    last.then_inc(s["s_y1"], 1)
                if step == "keys2":
                    landed(pe, "w2")
                    pe.wait_ge(s["s_ht"], BEFORE + nth("S", TURNS, "norm4", b))
                    for w in range(2):
                        for m in range(KD):
                            for k in range(KD):
                                last = pe.matmul(bank[2 * b + w][:, S * m:S * (m + 1)], W2[:, w, k, P * m:P * (m + 1)],
                                                 HT[:, k, S * b:S * (b + 1)], start=(k == 0), stop=(k == KD - 1))
                    last.then_inc(s["s_qk"], 1)
                if step == "values2":
                    pe.wait_ge(s["s_qk2"], nth("S", ["keys2"], "keys2", b))
                    for j in range(TB):
                        for k in range(KD):
                            last = pe.matmul(bank_a(b)[:, D * j:D * (j + 1)], tokens(b, j, k), W2[:, 2, k, :],
                                             start=(k == 0), stop=(k == KD - 1))
                    last.then_inc(s["s_v"], 1)
                if step == "scores2":
                    pe.wait_ge(s["s_v2"], nth("S", ["values2"], "values2", b))
                    for j in range(TB):
                        for half in range(2):
                            for k in range(KD):
                                keys = CT[:, k, S * b:S * (b + 1)] if half == 0 else KT[b][:, k, :]
                                last = pe.matmul(bank[2 * b + j][:, S * half:S * (half + 1)],
                                                 QT[b][:, k, P * j:P * (j + 1)], keys,
                                                 start=(k == 0), stop=(k == KD - 1))
                    last.then_inc(s["s_sc2"], 1)
                if step == "probs2":
                    pe.wait_ge(s["s_ex2"], nth("S", ["scores2"], "scores2", b))
                    for j in range(TB):
                        for c in range(4):
                            last = pe.transpose(bank[2 * b + c // 2][:, S * (c % 2) + P * j:S * (c % 2) + P * (j + 1)],
                                                PR[b][:, j, P * c:P * (c + 1)], identf[:])
                    last.then_inc(s["s_pt2"], 1)
                if step == "mix2":
                    pe.wait_ge(s["s_ptc2"], nth("S", ["probs2"], "probs2", b))
                    for m in range(KD):
                        for c in range(4):
                            v = CN[:, TB * b + c, P * m:P * (m + 1)] if c < TB else VN[b][:, c - TB, P * m:P * (m + 1)]
                            last = pe.matmul(bank_a(b)[:, S * m:S * (m + 1)], v, PT[b][:, c, :],
                                             start=(c == 0), stop=(c == 3))
                    last.then_inc(s["s_o2"], 1)
                if step == "project2":
                    pe.wait_ge(s["s_oc2"], nth("S", ["mix2"], "mix2", b))
                    for j in range(TB):
                        for m in range(KD):
                            last = pe.matmul(bank_b(b)[:, D * j:D * (j + 1)], OT[b][:, m, P * j:P * (j + 1)],
                                             W2[:, 3, m, :], start=(m == 0), stop=(m == KD - 1))
                    last.then_inc(s["s_y2"], 1)
                if step in QTURNS:
                    pe.wait_ge(s["s_qn"], nth("G", QUANTS, QUANTS[QTURNS.index(step)], b))
                    for k in range(KD):
                        for j in range(TB):
                            o = S * k + P * j
                            last = pe.transpose(bank_a(b)[:, 0:S].bitcast(BF16)[:, o:o + P],
                                                XQ[:, b, j, P * k:P * (k + 1)], identb[:])
                    last.then_inc(s["s_qt"], 1)
                if step in INS:
                    if step == ("in2a", 0) or step == ("in3", 0):
                        pe.wait_ge(s["s_qc"], nth("S", QTURNS, "turn5" if step[0] == "in2a" else "turn7", b))
                    elif step[0] == "in2b":
                        pe.wait_ge(s_hmg, nth("V", IN2, ("in2a", step[1]), b))
                    elif step[0] == "in2a":
                        pe.wait_ge(s["s_xq"], nth("V", OUT2, ("out2", step[1] - 1), b))
                    else:
                        pe.wait_ge(s["s_xout"], nth("V", [("out3", j) for j in range(TB)], ("out3", step[1] - 1), b))
                    pairs = {"in2a": ((0, 0), (1, 0)), "in2b": ((0, 1), (1, 1)), "in3": ((3, 0), (3, 1))}[step[0]]
                    for dst, (w, n) in zip((bank_a(b), bank_b(b)), pairs):
                        for k in range(KD):
                            last = pe.matmul(dst[:], XQT[:, b, k, P * step[1]:P * (step[1] + 1)],
                                             QW[:, w, NI * k + 512 * n:NI * k + 512 * (n + 1)],
                                             start=(k == 0), stop=(k == KD - 1))
                    last.then_inc(s["s_gu"], 1)
                if step in HTURNS:
                    pe.wait_ge(s["s_hq"], nth("V", ROUNDS, ("round" + step[0][-1], step[1]), b))
                    for f in range(KI):
                        last = pe.transpose(bank_a(b)[:].bitcast(BF16)[:, P * f:P * (f + 1)],
                                            HQ[b][:, P * f:P * (f + 1)], identb[:])
                    last.then_inc(s["s_hqt"], 1)
                if step in OUTS:
                    w = 2 if step[0] == "out2" else 4
                    pe.wait_ge(s["s_hqc"], nth("S", HTURNS, ("turn" + step[0][-1], step[1]), b))
                    for f in range(KI):
                        last = pe.matmul(bank_b(b)[:, 0:D], HQT[b][:, f, :], QW[:, w, D * f:D * (f + 1)],
                                         start=(f == 0), stop=(f == KI - 1))
                    last.then_inc(s["s_yq"], 1)
                if step == "queries3":
                    landed(pe, "w3")
                    pe.wait_ge(s["s_ht"], BEFORE + nth("S", TURNS, "norm6", b))
                    for m in range(KD):
                        for k in range(KD):
                            last = pe.matmul(bank_b(b)[:, S * m:S * (m + 1)], W3[:, 0, k, P * m:P * (m + 1)],
                                             HT[:, k, S * b:S * (b + 1)], start=(k == 0), stop=(k == KD - 1))
                    last.then_inc(s["s_q3"], 1)
                if step == "scores3":
                    pe.wait_ge(s["s_qc3"], nth("S", ["queries3"], "queries3", b))
                    for j in range(TB):
                        for k in range(KD):
                            last = pe.matmul(bank_a(b)[:, S * j:S * (j + 1)], QT[b][:, k, P * j:P * (j + 1)],
                                             CT[:, k, S * b:S * (b + 1)], start=(k == 0), stop=(k == KD - 1))
                    last.then_inc(s["s_sc3"], 1)
                if step == "probs3":
                    pe.wait_ge(s["s_p3"], nth("V", ["clip3"], "clip3", b))
                    for j in range(TB):
                        for c in range(TB):
                            last = pe.transpose(bank_b(b)[:, S * c + P * j:S * c + P * (j + 1)],
                                                P3[b][:, j, P * c:P * (c + 1)], identf[:])
                    last.then_inc(s["s_pt3"], 1)
                if step == "mix3":
                    pe.wait_ge(s["s_ptc3"], nth("S", ["probs3"], "probs3", b))
                    for m in range(KD):
                        for c in range(TB):
                            last = pe.matmul(bank_a(b)[:, S * m:S * (m + 1)], CN[:, TB * b + c, P * m:P * (m + 1)],
                                             PT[b][:, c, :], start=(c == 0), stop=(c == TB - 1))
                    last.then_inc(s["s_o3"], 1)
                if step == "project3":
                    pe.wait_ge(s["s_oc3"], nth("S", ["mix3"], "mix3", b))
                    for j in range(TB):
                        for m in range(KD):
                            last = pe.matmul(bank_b(b)[:, D * j:D * (j + 1)], OT[b][:, m, P * j:P * (j + 1)],
                                             W3[:, 1, m, :], start=(m == 0), stop=(m == KD - 1))
                    last.then_inc(s["s_y3"], 1)


def kernel(**inputs):
    import numpy as _np
    import concourse.bacc as _bacc
    from concourse import mybir as _mybir
    from concourse.bass_utils import run_bass_kernel_spmd as _run

    i = {n: _np.asarray(v) for n, v in inputs.items()}
    c = _np.ascontiguousarray

    def turned(w):
        return c(_np.moveaxis(w, -1, 0).reshape(w.shape[-1], -1))

    arrays = {
        "x": i["x"].reshape(N, D), "g": _np.concatenate([i["g_xattn"], i["g_ffn"]]),
        "tok": i["itok_BxS_13_99985"].reshape(N), "ctx": i["ctx_2048"].reshape(N, D), "ctxT": turned(i["ctx_2048"]),
        "router": turned(i["L0_ffn_router_w"]), "router_bias": i["L0_ffn_router_bias"],
        "eg": turned(i["L0_ffn_gate_w"]), "eu": turned(i["L0_ffn_up_w"]),
        "ed": c(i["L0_ffn_down_w"].transpose(0, 2, 1)).reshape(E * F, D),
        "sg": turned(i["L0_ffn_sh_gate_w"]), "su": turned(i["L0_ffn_sh_up_w"]),
        "sd": c(i["L0_ffn_sh_down_w"].transpose(0, 2, 1)).reshape(SF, D),
        "wi": i["L1_xattn_Wi"], "bi": i["L1_xattn_bi"], "wf": i["L1_xattn_Wf"], "bf": i["L1_xattn_bf"],
        "lnsc": i["L1_xattn_ln_scale"],
        "la": turned(i["L1_ffn_A"]), "lb": c(i["L1_ffn_Bw"].transpose(0, 2, 1)).reshape(E1 * R1, D),
        "lg": turned(i["L1_ffn_Wg"]),
        "wq": turned(i["L2_xattn_wq"]), "wk": turned(i["L2_xattn_wk"]), "wv": turned(i["L2_xattn_wv"]),
        "wo": turned(i["L2_xattn_wo"]),
        "q2g": turned(i["L2_ffn_w_gate"]), "q2u": turned(i["L2_ffn_w_up"]), "q2d": turned(i["L2_ffn_w_down"]),
        "w3q": turned(i["L3_xattn_W_qkv"][0:D]), "w3o": turned(i["L3_xattn_W_o"]),
        "mix": _np.stack([i["L3_xattn_beta_q"], i["L3_xattn_beta_k"], i["L3_xattn_gate"], i["L3_xattn_log_tau"]]),
        "q3a": turned(i["L3_ffn_w1"]), "q3b": turned(i["L3_ffn_w2"]),
    }
    nc = _bacc.Bacc("TRN2", target_bir_lowering=False, num_devices=1)
    ins = {n: nc.dram_tensor(f"in_{n}", v.shape, _mybir.dt.from_np(v.dtype), kind="ExternalInput").ap()
           for n, v in arrays.items()}
    out = nc.dram_tensor("out_x", (N, D), F32, kind="ExternalOutput").ap()
    flamingo(nc, ins, out)
    r = _run(nc, [{f"in_{n}": c(v) for n, v in arrays.items()}], core_ids=[0])
    return r.results[0]["out_x"].reshape(B, S, D)
```
